# Optimizing a Trainium2 kernel written in Bass

```python
import numpy as np
import jax
import jax.numpy as jnp

def _softmax(x, axis=-1):
    return jax.nn.softmax(x, axis=axis)

def _gelu(x):
    return jax.nn.gelu(x, approximate=True)

def _silu(x):
    return jax.nn.silu(x)

def _sigmoid(x):
    return jax.nn.sigmoid(x)

def _layernorm(x, axis=-1, eps=1e-05):
    m = jnp.mean(x, axis=axis, keepdims=True)
    v = jnp.var(x, axis=axis, keepdims=True)
    return (x - m) / jnp.sqrt(v + eps)

def _scatter_add(tgt, idx, src, axis=0):
    return tgt.at[idx].add(src)

def _segment_sum(src, seg, n):
    return jax.ops.segment_sum(src, seg, n)
kernel_name = 'mk_gps_d2_gnn_r8_c6ac77'

def setup_inputs(seed: int=0):
    np.random.seed(seed)
    _w = jnp.asarray

    def _rec_inputs():
        import jax
        import jax.numpy as jnp
        _gk = jax.random.key(seed)
        x = -0.0004776 + 1.001 * jax.random.normal(jax.random.fold_in(_gk, 1), (1250, 1024), jnp.float32)
        src = jax.random.randint(jax.random.fold_in(_gk, 2), (20000,), 0, 1250, jnp.int32)
        dst = jax.random.randint(jax.random.fold_in(_gk, 3), (20000,), 0, 1250, jnp.int32)
        _o = jnp.argsort(dst, stable=True)
        src = src[_o]
        dst = dst[_o]
        edge_weight = -0.000130211 + 0.031236 * jax.random.normal(jax.random.fold_in(_gk, 12), (20000,), jnp.float32)
        return (x, src, dst, edge_weight)
    x, src, dst, edge_weight = _rec_inputs()

    def _L0_gnn_setup():
        import jax, jax.numpy as jnp
        import numpy as np
        N_DIM = 1024
        NHID = 512
        NUM_K = 4
        DIA_LEN = [50] * 60
        N_NODES = sum(DIA_LEN)

        def _build_edge_index(dia_len):
            pieces = []
            off = 0
            for L in dia_len:
                idx = np.arange(off, off + L)
                src = np.repeat(idx, L)
                dst = np.tile(idx, L)
                m = src != dst
                pieces.append(np.stack([src[m], dst[m]], axis=0))
                off += L
            return np.concatenate(pieces, axis=1).astype(np.int32)

        def _graph_gcn(x, row, col, gw, gb, n_nodes):
            deg = jax.ops.segment_sum(jnp.ones(row.shape[0], x.dtype), col, num_segments=n_nodes)
            dis = jnp.maximum(deg, 1.0) ** (-0.5)
            norm = dis[row] * dis[col]
            x_i = x[col]
            x_j = x[row]
            alpha = jnp.tanh(x_i @ gw[:x.shape[1]] + x_j @ gw[x.shape[1]:] + gb)
            msg = norm[:, None] * alpha * x_j
            return jax.ops.segment_sum(msg, col, num_segments=n_nodes)
        key = jax.random.key(seed)
        ks = jax.random.split(key, 6)
        emotions_feat = jax.random.normal(ks[0], (N_NODES, N_DIM), dtype=jnp.float32)
        qmask = jax.random.uniform(ks[1], (max(DIA_LEN), len(DIA_LEN), 2), dtype=jnp.float32)
        edge_index = jnp.asarray(_build_edge_index(DIA_LEN))
        s1 = 1.0 / np.sqrt(N_DIM)
        W1 = jax.random.uniform(ks[2], (N_DIM, NHID), minval=-s1, maxval=s1, dtype=jnp.float32)
        b1 = jax.random.uniform(ks[3], (NHID,), minval=-s1, maxval=s1, dtype=jnp.float32)
        s2 = 1.0 / np.sqrt(2 * NHID)
        gate_w = jax.random.uniform(ks[4], (NUM_K, 2 * NHID, 1), minval=-s2, maxval=s2, dtype=jnp.float32)
        gate_b = jax.random.uniform(ks[5], (NUM_K, 1), minval=-s2, maxval=s2, dtype=jnp.float32)
        return {'emotions_feat': emotions_feat, 'qmask': qmask, 'edge_index': edge_index, 'epoch': 0, 'W1': W1, 'b1': b1, 'gate_w': gate_w, 'gate_b': gate_b}
    _L0_gnn_all = _L0_gnn_setup()
    _L0_gnn_in = {k: v for k, v in _L0_gnn_all.items() if k in ('qmask', 'W1', 'b1', 'gate_w', 'gate_b')}
    del _L0_gnn_all

    def _L0_mix_setup():
        import jax, jax.numpy as jnp
        import numpy as np
        EMBED_DIM = 1024
        NUM_HEADS = 16
        HEAD_DIM = EMBED_DIM // NUM_HEADS

        def _feature_map(x):
            return jax.nn.elu(x) + 1.0

        def _split_heads(x, bsz, seq_len):
            return x.reshape(bsz, seq_len, NUM_HEADS, HEAD_DIM).transpose(0, 2, 1, 3)
        key = jax.random.key(seed)
        ks = jax.random.split(key, 9)
        s = 0.02
        E = EMBED_DIM
        return {'hidden_states': jax.random.normal(ks[0], (4, 512, E), dtype=jnp.float32), 'Wq': jax.random.normal(ks[1], (E, E), dtype=jnp.float32) * s, 'bq': jnp.zeros((E,), dtype=jnp.float32), 'Wk': jax.random.normal(ks[2], (E, E), dtype=jnp.float32) * s, 'bk': jnp.zeros((E,), dtype=jnp.float32), 'Wv': jax.random.normal(ks[3], (E, E), dtype=jnp.float32) * s, 'bv': jnp.zeros((E,), dtype=jnp.float32), 'Wo': jax.random.normal(ks[4], (E, E), dtype=jnp.float32) * s, 'bo': jnp.zeros((E,), dtype=jnp.float32)}
    _L0_mix_all = _L0_mix_setup()
    _L0_mix_in = {k: v for k, v in _L0_mix_all.items() if k in ('Wq', 'bq', 'Wk', 'bk', 'Wv', 'bv', 'Wo', 'bo')}
    del _L0_mix_all

    def _L0_ffn_setup():
        import jax, jax.numpy as jnp
        import numpy as np
        W_SCALE = 0.02
        TOP_K = 2
        key = jax.random.key(seed)
        ks = jax.random.split(key, 5)
        B, S, H, I, E = (2, 1024, 1024, 512, 8)
        return {'x': jax.random.normal(ks[0], (B, S, H), dtype=jnp.float32), 'gate': jax.random.normal(ks[1], (H, E), dtype=jnp.float32) * W_SCALE, 'experts_w1': jax.random.normal(ks[2], (E, H, I), dtype=jnp.float32) * W_SCALE, 'experts_w2': jax.random.normal(ks[3], (E, I, H), dtype=jnp.float32) * W_SCALE, 'experts_w3': jax.random.normal(ks[4], (E, H, I), dtype=jnp.float32) * W_SCALE}
    _L0_ffn_all = _L0_ffn_setup()
    _L0_ffn_in = {k: v for k, v in _L0_ffn_all.items() if k in ('gate', 'experts_w1', 'experts_w2', 'experts_w3')}
    del _L0_ffn_all

    def _L1_gnn_setup():
        import jax, jax.numpy as jnp
        import numpy as np
        INDIM = 1024
        OUTDIM = 1024
        NNZ = 8192
        N = 6250
        key = jax.random.key(seed)
        k1, k2, k3, k4, k5 = jax.random.split(key, 5)
        x = jax.random.normal(k1, (N, INDIM), dtype=jnp.float32)
        stdv = np.sqrt(6.0 / (INDIM + OUTDIM))
        nnz_weight = jax.random.uniform(k2, (NNZ,), dtype=jnp.float32, minval=-stdv, maxval=stdv)
        bias = jax.random.normal(k3, (OUTDIM,), dtype=jnp.float32) * 0.02
        row = jax.random.randint(k4, (NNZ,), 0, OUTDIM, dtype=jnp.int64)
        col = jax.random.randint(k5, (NNZ,), 0, INDIM, dtype=jnp.int64)
        edge_index = jnp.stack([row, col])
        return {'x': x, 'nnz_weight': nnz_weight, 'bias': bias, 'edge_index': edge_index}
    _L1_gnn_all = _L1_gnn_setup()
    _L1_gnn_in = {k: v for k, v in _L1_gnn_all.items() if k in ('bias',)}
    del _L1_gnn_all

    def _L1_mix_setup():
        import jax, jax.numpy as jnp
        import numpy as np
        B, S, D, H = (4, 512, 1024, 16)
        HD = D // H
        key = jax.random.key(seed)
        ks = jax.random.split(key, 9)
        sc = 1.0 / np.sqrt(D)
        return {'x': jax.random.normal(ks[0], (B, S, D), dtype=jnp.float32), 'q_w': jax.random.normal(ks[1], (D, D), dtype=jnp.float32) * sc, 'q_b': jax.random.normal(ks[2], (D,), dtype=jnp.float32) * 0.01, 'k_w': jax.random.normal(ks[3], (D, D), dtype=jnp.float32) * sc, 'k_b': jax.random.normal(ks[4], (D,), dtype=jnp.float32) * 0.01, 'v_w': jax.random.normal(ks[5], (D, D), dtype=jnp.float32) * sc, 'v_b': jax.random.normal(ks[6], (D,), dtype=jnp.float32) * 0.01, 'o_w': jax.random.normal(ks[7], (D, D), dtype=jnp.float32) * sc, 'o_b': jax.random.normal(ks[8], (D,), dtype=jnp.float32) * 0.01}
    _L1_mix_all = _L1_mix_setup()
    _L1_mix_in = {k: v for k, v in _L1_mix_all.items() if k in ('q_w', 'q_b', 'k_w', 'k_b', 'v_w', 'v_b', 'o_w', 'o_b')}
    del _L1_mix_all

    def _L1_ffn_setup():
        import jax, jax.numpy as jnp
        import numpy as np
        DIM = 1024
        HIDDEN = 384
        SCALE = 1.0 / 127.0

        def _dequant(w_int, dtype):
            return w_int.astype(dtype) * jnp.asarray(SCALE, dtype)
        key = jax.random.key(seed)
        k_x, k_g, k_u, k_d = jax.random.split(key, 4)
        x = jax.random.normal(k_x, (4, 256, DIM), dtype=jnp.float32)
        w_gate = jax.random.randint(k_g, (HIDDEN, DIM), -127, 128, dtype=jnp.int32)
        w_up = jax.random.randint(k_u, (HIDDEN, DIM), -127, 128, dtype=jnp.int32)
        w_down = jax.random.randint(k_d, (DIM, HIDDEN), -127, 128, dtype=jnp.int32)
        return {'x': x, 'w_gate': w_gate, 'w_up': w_up, 'w_down': w_down}
    _L1_ffn_all = _L1_ffn_setup()
    _L1_ffn_in = {k: v for k, v in _L1_ffn_all.items() if k in ('w_gate', 'w_up', 'w_down')}
    del _L1_ffn_all
    return {'x': x, 'src': src, 'dst': dst, 'edge_weight': edge_weight, 'L0_gnn_qmask': _L0_gnn_in['qmask'], 'L0_gnn_W1': _L0_gnn_in['W1'], 'L0_gnn_b1': _L0_gnn_in['b1'], 'L0_gnn_gate_w': _L0_gnn_in['gate_w'], 'L0_gnn_gate_b': _L0_gnn_in['gate_b'], 'L0_mix_Wq': _L0_mix_in['Wq'], 'L0_mix_bq': _L0_mix_in['bq'], 'L0_mix_Wk': _L0_mix_in['Wk'], 'L0_mix_bk': _L0_mix_in['bk'], 'L0_mix_Wv': _L0_mix_in['Wv'], 'L0_mix_bv': _L0_mix_in['bv'], 'L0_mix_Wo': _L0_mix_in['Wo'], 'L0_mix_bo': _L0_mix_in['bo'], 'L0_ffn_gate': _L0_ffn_in['gate'], 'L0_ffn_experts_w1': _L0_ffn_in['experts_w1'], 'L0_ffn_experts_w2': _L0_ffn_in['experts_w2'], 'L0_ffn_experts_w3': _L0_ffn_in['experts_w3'], 'L1_gnn_bias': _L1_gnn_in['bias'], 'L1_mix_q_w': _L1_mix_in['q_w'], 'L1_mix_q_b': _L1_mix_in['q_b'], 'L1_mix_k_w': _L1_mix_in['k_w'], 'L1_mix_k_b': _L1_mix_in['k_b'], 'L1_mix_v_w': _L1_mix_in['v_w'], 'L1_mix_v_b': _L1_mix_in['v_b'], 'L1_mix_o_w': _L1_mix_in['o_w'], 'L1_mix_o_b': _L1_mix_in['o_b'], 'L1_ffn_w_gate': _L1_ffn_in['w_gate'], 'L1_ffn_w_up': _L1_ffn_in['w_up'], 'L1_ffn_w_down': _L1_ffn_in['w_down']}

def reference(x, src, dst, edge_weight, L0_gnn_qmask, L0_gnn_W1, L0_gnn_b1, L0_gnn_gate_w, L0_gnn_gate_b, L0_mix_Wq, L0_mix_bq, L0_mix_Wk, L0_mix_bk, L0_mix_Wv, L0_mix_bv, L0_mix_Wo, L0_mix_bo, L0_ffn_gate, L0_ffn_experts_w1, L0_ffn_experts_w2, L0_ffn_experts_w3, L1_gnn_bias, L1_mix_q_w, L1_mix_q_b, L1_mix_k_w, L1_mix_k_b, L1_mix_v_w, L1_mix_v_b, L1_mix_o_w, L1_mix_o_b, L1_ffn_w_gate, L1_ffn_w_up, L1_ffn_w_down):
    import jax
    import jax.numpy as jnp

    def _L0_gnn_ref(emotions_feat, qmask, edge_index, epoch, W1, b1, gate_w, gate_b):
        import jax, jax.numpy as jnp
        import numpy as np
        N_DIM = 1024
        NHID = 512
        NUM_K = 4
        DIA_LEN = [50] * 60
        N_NODES = sum(DIA_LEN)

        def _build_edge_index(dia_len):
            pieces = []
            off = 0
            for L in dia_len:
                idx = np.arange(off, off + L)
                src = np.repeat(idx, L)
                dst = np.tile(idx, L)
                m = src != dst
                pieces.append(np.stack([src[m], dst[m]], axis=0))
                off += L
            return np.concatenate(pieces, axis=1).astype(np.int32)

        def _graph_gcn(x, row, col, gw, gb, n_nodes):
            deg = jax.ops.segment_sum(jnp.ones(row.shape[0], x.dtype), col, num_segments=n_nodes)
            dis = jnp.maximum(deg, 1.0) ** (-0.5)
            norm = dis[row] * dis[col]
            x_i = x[col]
            x_j = x[row]
            alpha = jnp.tanh(x_i @ gw[:x.shape[1]] + x_j @ gw[x.shape[1]:] + gb)
            msg = norm[:, None] * alpha * x_j
            return jax.ops.segment_sum(msg, col, num_segments=n_nodes)
        row, col = (edge_index[0], edge_index[1])
        n_nodes = emotions_feat.shape[0]
        x1 = emotions_feat @ W1 + b1
        gnn_out = x1
        for kk in range(NUM_K):
            gnn_out = gnn_out + _graph_gcn(gnn_out, row, col, gate_w[kk], gate_b[kk], n_nodes)
        return jnp.concatenate([x1, gnn_out], axis=1)

    def _L0_mix_ref(hidden_states, Wq, bq, Wk, bk, Wv, bv, Wo, bo):
        import jax, jax.numpy as jnp
        import numpy as np
        EMBED_DIM = 1024
        NUM_HEADS = 16
        HEAD_DIM = EMBED_DIM // NUM_HEADS

        def _feature_map(x):
            return jax.nn.elu(x) + 1.0

        def _split_heads(x, bsz, seq_len):
            return x.reshape(bsz, seq_len, NUM_HEADS, HEAD_DIM).transpose(0, 2, 1, 3)
        bsz, tgt_len, _ = hidden_states.shape
        q = _feature_map(hidden_states @ Wq.T + bq)
        k = _feature_map(hidden_states @ Wk.T + bk)
        v = hidden_states @ Wv.T + bv
        q = _split_heads(q, bsz, tgt_len)
        k = _split_heads(k, bsz, tgt_len)
        v = _split_heads(v, bsz, tgt_len)
        KV = jnp.einsum('bhsd,bhsm->bhmd', k, v)
        Z = 1.0 / (jnp.einsum('bhsd,bhd->bhs', q, k.sum(axis=2)) + 1e-06)
        attn = jnp.einsum('bhsd,bhmd,bhs->bshm', q, KV, Z)
        attn = attn.reshape(bsz, tgt_len, EMBED_DIM)
        return attn @ Wo.T + bo

    def _L0_ffn_ref(x, gate, experts_w1, experts_w2, experts_w3):
        import jax, jax.numpy as jnp
        import numpy as np
        W_SCALE = 0.02
        TOP_K = 2
        E = experts_w1.shape[0]
        router_logits = jnp.einsum('bsh,he->bse', x, gate)
        routing_weights, selected = jax.lax.top_k(router_logits, TOP_K)
        routing_weights = jax.nn.softmax(routing_weights, axis=-1)
        onehot = jax.nn.one_hot(selected, E, dtype=x.dtype)
        tok_w = jnp.einsum('bsk,bske->bse', routing_weights, onehot)
        g = jnp.einsum('bsh,ehi->ebsi', x, experts_w1)
        u = jnp.einsum('bsh,ehi->ebsi', x, experts_w3)
        hid = jax.nn.silu(g) * u
        eo = jnp.einsum('ebsi,eih->ebsh', hid, experts_w2)
        out = jnp.einsum('ebsh,bse->bsh', eo, tok_w)
        return out

    def _L1_gnn_ref(x, nnz_weight, bias, edge_index):
        import jax, jax.numpy as jnp
        import numpy as np
        INDIM = 1024
        OUTDIM = 1024
        NNZ = 8192
        N = 6250
        row, col = (edge_index[0], edge_index[1])
        W = jnp.zeros((OUTDIM, INDIM), dtype=nnz_weight.dtype).at[row, col].add(nnz_weight)
        return x @ W.T + bias

    def _L1_mix_ref(x, q_w, q_b, k_w, k_b, v_w, v_b, o_w, o_b):
        import jax, jax.numpy as jnp
        import numpy as np
        B, S, D, H = (4, 512, 1024, 16)
        HD = D // H
        b, s, _ = x.shape
        q = (x @ q_w.T + q_b).reshape(b, s, H, HD)
        k = (x @ k_w.T + k_b).reshape(b, s, H, HD)
        v = (x @ v_w.T + v_b).reshape(b, s, H, HD)
        q = jax.nn.relu(q)
        k = jax.nn.relu(k)
        kv = jnp.einsum('bshd,bshe->bhde', k, v)
        out = jnp.einsum('bqhd,bhde->bqhe', q, kv)
        out = out.reshape(b, s, D)
        return out @ o_w.T + o_b

    def _L1_ffn_ref(x, w_gate, w_up, w_down):
        import jax, jax.numpy as jnp
        import numpy as np
        DIM = 1024
        HIDDEN = 384
        SCALE = 1.0 / 127.0

        def _dequant(w_int, dtype):
            return w_int.astype(dtype) * jnp.asarray(SCALE, dtype)
        wg = _dequant(w_gate, x.dtype)
        wu = _dequant(w_up, x.dtype)
        wd = _dequant(w_down, x.dtype)
        gate = jnp.einsum('bsd,hd->bsh', x, wg)
        up = jnp.einsum('bsd,hd->bsh', x, wu)
        h = jax.nn.silu(gate) * up
        return jnp.einsum('bsh,dh->bsd', h, wd)
    edge_index = jnp.stack([src, dst])
    xn = _layernorm(x, axis=-1)
    x = x + _L0_gnn_ref(xn, L0_gnn_qmask, edge_index, 0, L0_gnn_W1, L0_gnn_b1, L0_gnn_gate_w, L0_gnn_gate_b) + _L0_mix_ref(xn[None], L0_mix_Wq, L0_mix_bq, L0_mix_Wk, L0_mix_bk, L0_mix_Wv, L0_mix_bv, L0_mix_Wo, L0_mix_bo)[0]
    x = x + _L0_ffn_ref(_layernorm(x, axis=-1)[None], L0_ffn_gate, L0_ffn_experts_w1, L0_ffn_experts_w2, L0_ffn_experts_w3)[0]
    xn = _layernorm(x, axis=-1)
    x = x + _L1_gnn_ref(xn, edge_weight, L1_gnn_bias, edge_index) + _L1_mix_ref(xn[None], L1_mix_q_w, L1_mix_q_b, L1_mix_k_w, L1_mix_k_b, L1_mix_v_w, L1_mix_v_b, L1_mix_o_w, L1_mix_o_b)[0]
    x = x + _L1_ffn_ref(_layernorm(x, axis=-1)[None], L1_ffn_w_gate, L1_ffn_w_up, L1_ffn_w_down)[0]
    return x

_drawn_inputs = setup_inputs


def setup_inputs(seed=0):
    import zlib

    import numpy as np

    out = dict(_drawn_inputs(seed))
    spreads = {'L0_mix_bq': (0.0, 2.0),
     'L0_mix_bk': (0.0, 2.0),
     'L0_mix_bv': (0.0, 0.1),
     'L0_mix_bo': (0.0, 0.1)}
    factors = {'edge_weight': 200.0,
     'L0_gnn_gate_b': 31.787,
     'L0_mix_Wq': 200.0,
     'L0_mix_Wk': 14.747,
     'L1_gnn_bias': 200.0,
     'L1_mix_q_b': 8.0,
     'L1_mix_k_b': 8.0,
     'L1_mix_o_b': 200.0}
    for name, (base, spread) in spreads.items():
        noise = np.random.default_rng([zlib.crc32(name.encode()), seed]).standard_normal(out[name].shape)
        drawn = base * np.exp(spread * noise) if base else spread * noise
        out[name] = jnp.asarray(drawn.astype(out[name].dtype))
    for name, factor in factors.items():
        out[name] = (out[name] * factor).astype(out[name].dtype)
    return out
```

```python
from contextlib import contextmanager, ExitStack

import numpy as np
import concourse.bass as bass
from concourse import mybir

F32, F32R, I32, U32, U16, BF16 = (mybir.dt.float32, mybir.dt.float32r, mybir.dt.int32, mybir.dt.uint32,
                                  mybir.dt.uint16, mybir.dt.bfloat16)
ALU = mybir.AluOpType
ACT = mybir.ActivationFunctionType
AX = mybir.AxisListType

P = 128
N = 1250
E = 20000
D = 1024
NH = 512
KC = D // P
GC = NH // P
NT = 3
TW = 418
TM = NT * TW
TC = 10
LAST = N - (TC - 1) * P
EPS = 1e-5
EP, EK = 125, 160
NBUCK = TC * TC
NCH = 256
assert E // P + NBUCK <= NCH and EP * EK == E


def rows_of(c):
    return P if c < TC - 1 else LAST


class Loops:

    def __init__(self):
        self.active, self.counts, self.steps = {}, {}, []

    @contextmanager
    def run(self, engine, name, count):
        self.counts[name] = count
        before = [s.count for s in self.steps]
        with engine.Fori(0, count) as i:
            self.active[name] = i
            yield i
        del self.active[name]
        for s, b in zip(self.steps, before):
            s.close(name, b, count)


class Steps:

    def __init__(self, nc, ctx, loops, name, known, each=1):
        self.sem = nc.alloc_semaphore(name)
        self.loops, self.each, self.name = loops, each, name
        self.known = known.get(name, ({}, {}))
        self.count, self.at, self.slope = 0, {}, {}
        if not loops.steps:
            loops.spare = nc.alloc_semaphore(name + "_spare")
        loops.steps.append(self)

    def mark(self, instruction, step):
        assert step not in self.at, step
        instruction.then_inc(self.sem, self.each)
        self.count += self.each
        self.at[step] = (self.count, tuple(self.loops.active))
        return instruction

    def alias(self, step, of):
        self.at[step] = self.at[of]

    def start(self, engine, by):
        engine.sem_inc(self.sem, by)
        self.count = by

    def close(self, loop, before, turns):
        if self.count > before:
            self.slope[loop] = self.count - before
            self.count = before + turns * (self.count - before)

    def wait(self, engine, step, back=0):
        at, slope = self.known
        if not at:
            return
        value, around = at[step]
        for n, loop in enumerate(around):
            shift = back.get(loop, 0) if isinstance(back, dict) else back if n == len(around) - 1 else 0
            i = self.loops.active.get(loop)
            if i is None:
                value += slope[loop] * (self.loops.counts[loop] - 1 - shift)
            else:
                value -= slope[loop] * shift
        assert value >= 0, (self.name, step, value)
        if value==0 and any(l in self.loops.active for l in around): print("ZERO",self.name,step)
        for loop in around:
            i = self.loops.active.get(loop)
            if i is not None:
                value = i * slope[loop] + value
        engine.wait_ge(self.sem, value)
        if not isinstance(value, int):
            engine.sem_inc(self.loops.spare, 1)

    def learned(self):
        return self.at, self.slope



def graph_sort(nc, known, dram):
    loops, got = Loops(), {}
    with ExitStack() as ctx:
        sb = lambda n, s, d=F32: ctx.enter_context(nc.sbuf_tensor("gs_" + n, s, d))
        new = lambda n, each=1: got.setdefault(n, Steps(nc, ctx, loops, n, known, each))
        ld, pl, dv, pe, act = new("gs_ld", 16), new("gs_pool"), new("gs_dve"), new("gs_pe"), new("gs_act")
        fill, scat, offs = new("gs_fill", 16), new("gs_scat", 16), new("gs_offs", 16)
        src, dst, wgt = sb("src", [EP, EK], I32), sb("dst", [EP, EK], I32), sb("wgt", [EP, EK])
        hs, hd = sb("hs", [EP, EK], I32), sb("hd", [EP, EK], I32)
        fs, fd, fhs, fhd = sb("fs", [EP, EK]), sb("fd", [EP, EK]), sb("fhs", [EP, EK]), sb("fhd", [EP, EK])
        key = sb("key", [EP, EK])
        iob = sb("iob", [P, NBUCK])
        cid = sb("cid", [P, 2])
        hot = sb("hot", [EP, NBUCK, EK], BF16)
        run = sb("run", [EP, NBUCK, EK])
        slot = sb("slot", [EP, NBUCK, EK])
        cnt = sb("cnt", [EP, NBUCK])
        tri = sb("tri", [EP, P])
        ones = sb("ones", [EP, P])
        tot, toti = sb("tot", [P, NBUCK]), sb("toti", [P, NBUCK], I32)
        nch, incl = sb("nch", [P, NBUCK]), sb("incl", [P, NBUCK])
        base = sb("base", [EP, NBUCK])
        pos, posi = sb("pos", [EP, EK]), sb("posi", [EP, EK], I32)
        lo7, hi7, idx = sb("lo7", [EP, EK], I32), sb("hi7", [EP, EK], I32), sb("idx", [EP, EK], I32)
        pay = sb("pay", [EP, EK, 4])
        empty = sb("empty", [P, NCH * 4])
        cmp = sb("cmp", [P, NBUCK])
        bk = sb("bk", [P, 2])
        bki, sbi = sb("bki", [P, 2], I32), sb("sbi", [P, 2], I32)
        bkb, far = sb("bkb", [P, 2]), sb("far", [P, 2])
        sbf, offc, offw = sb("sbf", [P, 2]), sb("offc", [P, 2]), sb("offw", [P, 2])
        off = sb("off", [P, 2, 2], I32)
        pp = ctx.enter_context(nc.psum_tensor("gs_pp", [P, NBUCK], F32))
        pt = ctx.enter_context(nc.psum_tensor("gs_pt", [P, NBUCK], F32))
        block = ctx.enter_context(nc.Block())

        @block.sync
        def _(e):
            ld.mark(e.dma_start(src[:], dram["src"]), "src")
            ld.mark(e.dma_start(dst[:], dram["dst"]), "dst")
            ld.mark(e.dma_start(wgt[:], dram["edge_weight"]), "wgt")
            pl.wait(e, "empty")
            fill.mark(e.dma_start(dram["slots"], empty[:]), "fill")
            dv.wait(e, "off")
            offs.mark(e.dma_start(dram["offs"], off[:]), "off")
            offs.wait(e, "off")

        @block.gpsimd
        def _(e):
            e.iota(iob[:], [[1, NBUCK]], base=0, channel_multiplier=0, allow_small_or_imprecise_dtypes=True)
            e.iota(cid[:], [[P, 2]], base=0, channel_multiplier=1, allow_small_or_imprecise_dtypes=True)
            e.memset(ones[:], 1.0)
            e.memset(tri[:], 1.0)
            pl.mark(e.memset(empty[:], -1.0), "empty")
            pl.wait(e, "empty")
            pl.mark(e.affine_select(out=tri[:], in_=tri[:], compare_op=ALU.is_gt, fill=0.0, base=0,
                                    pattern=[[1, P]], channel_multiplier=-1), "tri")
            dv.wait(e, "idx")
            fill.wait(e, "fill")
            for k in range(EK):
                i = e.indirect_dma_start(dram["slot_rows"],
                                         bass.IndirectOffsetOnAxis(idx[:, k:k + 1].bitcast(U32), 0),
                                         pay[:, k, :], None)
                scat.mark(i, f"scatter{k}")
            scat.wait(e, f"scatter{EK - 1}")

        @block.tensor
        def _(e):
            dv.wait(e, "cnt")
            pl.wait(e, "tri")
            e.matmul(pp[0:EP, :], tri[:, 0:EP], cnt[:], start=True, stop=True)
            pe.mark(e.matmul(pt[:], ones[:], cnt[:], start=True, stop=True), "sums")

        @block.vector
        def _(e):
            def d(i=None):
                e.drain()
            ld.wait(e, "wgt")
            e.tensor_scalar(hs[:], src[:], 7, None, ALU.arith_shift_right)
            e.tensor_scalar(hd[:], dst[:], 7, None, ALU.arith_shift_right)
            e.tensor_copy(fs[:], src[:])
            e.tensor_copy(fd[:], dst[:])
            d()
            e.tensor_copy(fhs[:], hs[:])
            e.tensor_copy(fhd[:], hd[:])
            d()
            e.scalar_tensor_tensor(key[:], fhs[:], float(TC), fhd[:], ALU.mult, ALU.add)
            e.scalar_tensor_tensor(pay[:, :, 0], fhs[:], -float(P), fs[:], ALU.mult, ALU.add)
            e.scalar_tensor_tensor(pay[:, :, 1], fhd[:], -float(P), fd[:], ALU.mult, ALU.add)
            e.tensor_copy(pay[:, :, 2], wgt[:])
            e.memset(pay[:, :, 3], 0.0)
            pl.wait(e, "tri")
            d()
            e.tensor_tensor(hot[:], key[:].unsqueeze(1).broadcast_to([EP, NBUCK, EK]),
                            iob[0:EP, :].unsqueeze(2).broadcast_to([EP, NBUCK, EK]), ALU.is_equal)
            d()
            flat = lambda t: t[:].rearrange("p b k -> p (b k)")
            e.tensor_tensor_scan(flat(run), flat(hot), flat(hot), 0.0, ALU.add, ALU.max)
            d()
            e.tensor_copy(cnt[:, 0:1], run[:, 0, EK - 1:EK])
            dv.mark(e.tensor_tensor(cnt[:, 1:NBUCK], run[:, 1:NBUCK, EK - 1], run[:, 0:NBUCK - 1, EK - 1],
                                    ALU.subtract), "cnt")
            pe.wait(e, "sums")
            e.tensor_scalar(tot[:], pt[:], float(P - 1), None, ALU.add)
            d()
            e.tensor_copy(toti[:], tot[:])
            d()
            e.tensor_scalar(toti[:], toti[:], 7, None, ALU.arith_shift_right)
            d()
            e.tensor_copy(nch[:], toti[:])
            d()
            e.tensor_tensor_scan(incl[:], nch[:], nch[:], 0.0, ALU.add, ALU.max)
            d()
            e.tensor_tensor(nch[:], incl[:], nch[:], ALU.subtract)
            d()
            e.scalar_tensor_tensor(base[:], nch[0:EP, :], float(P), pp[0:EP, :], ALU.mult, ALU.add)
            d()
            e.tensor_tensor(base[:, 1:NBUCK], base[:, 1:NBUCK], run[:, 0:NBUCK - 1, EK - 1], ALU.subtract)
            d()
            e.tensor_scalar(base[:], base[:], -1.0, None, ALU.add)
            for t in range(2):
                e.tensor_scalar(cmp[:], incl[:], cid[:, t:t + 1], 0.0, ALU.is_le, ALU.add,
                                accum_out=bk[:, t:t + 1])
                d()
            e.tensor_tensor(slot[:], run[:], base[:].unsqueeze(2).broadcast_to([EP, NBUCK, EK]), ALU.add)
            d()
            e.tensor_tensor(slot[:], slot[:], hot[:], ALU.mult)
            e.tensor_copy(bki[:], bk[:])
            d()
            e.tensor_reduce(pos[:], slot[:].rearrange("p b k -> p k b"), AX.X, ALU.add)
            d()
            e.tensor_copy(posi[:], pos[:])
            d()
            e.tensor_scalar(lo7[:], posi[:], P - 1, 8, ALU.bitwise_and, ALU.arith_shift_left)
            e.tensor_scalar(hi7[:], posi[:], 7, None, ALU.arith_shift_right)
            d()
            dv.mark(e.tensor_tensor(idx[:], lo7[:], hi7[:], ALU.add), "idx")
            e.tensor_scalar(bkb[:], bk[:], 103.0, None, ALU.mult)
            e.tensor_scalar(offc[:], bk[:], float(P), None, ALU.mult)
            d()
            e.tensor_copy(sbi[:], bkb[:])
            d()
            e.tensor_scalar(sbi[:], sbi[:], 10, None, ALU.arith_shift_right)
            d()
            e.tensor_copy(sbf[:], sbi[:])
            d()
            e.scalar_tensor_tensor(far[:], sbf[:], -float(TC), bk[:], ALU.mult, ALU.add)
            d()
            e.scalar_tensor_tensor(offw[:], sbf[:], float(KC), far[:], ALU.mult, ALU.add)
            d()
            e.tensor_scalar(far[:], far[:], float(KC), float(KC * KC), ALU.is_ge, ALU.mult)
            d()
            e.tensor_tensor(offw[:], offw[:], far[:], ALU.add)
            d()
            e.tensor_scalar(offw[:], offw[:], float(KC * KC), float(P), ALU.min, ALU.mult)
            d()
            e.tensor_copy(off[:, 0, :], offc[:])
            dv.mark(e.tensor_copy(off[:, 1, :], offw[:]), "off")
    known.update({n: s.learned() for n, s in got.items()})


def graph_build(nc, known, dram):
    loops, got = Loops(), {}
    UN = 8
    BODY = 2 * UN
    with ExitStack() as ctx:
        sb = lambda n, s, d=F32: ctx.enter_context(nc.sbuf_tensor("gb_" + n, s, d))
        new = lambda n, each=1: got.setdefault(n, Steps(nc, ctx, loops, n, known, each))
        ld, pl, dv, pe, act, st = (new("gb_ld", 16), new("gb_pool"), new("gb_dve"), new("gb_pe"),
                                   new("gb_act"), new("gb_st", 16))
        slots = sb("slots", [P, NCH, 4])
        whi, wlo = sb("whi", [P, NCH], F32R), sb("wlo", [P, NCH])
        offc, offw = sb("offc", [1, NCH], I32), sb("offw", [1, NCH], I32)
        iot = sb("iot", [P, P])
        hs = sb("hs", [P, 2, UN, P], F32R)
        hd = sb("hd", [P, 2, UN, P], F32R)
        wh = sb("wh", [P, 2, UN, P], F32R)
        wl = sb("wl", [P, 2, UN, P], F32R)
        cacc = sb("cacc", [P, (NBUCK + 1) * P])
        wacc = sb("wacc", [P, (KC * KC + 1) * P])
        c16 = sb("c16", [P, NBUCK * P], U16)
        pc = [ctx.enter_context(nc.psum_tensor(f"gb_pc{i}", [P, 4, P], F32)) for i in range(4)]
        pw = [ctx.enter_context(nc.psum_tensor(f"gb_pw{i}", [P, 4, P], F32)) for i in range(4)]
        block = ctx.enter_context(nc.Block())

        @block.sync
        def _(e):
            ld.mark(e.dma_start(slots[:], dram["slots"]), "slots")
            o = dram["offs"].rearrange("p (a t) -> a t p", a=2)
            ld.mark(e.dma_start(offc[:], o[0:1], allow_slow_non_contiguous=True), "offc")
            ld.mark(e.dma_start(offw[:], o[1:2], allow_slow_non_contiguous=True), "offw")
            dv.wait(e, "c16")
            st.mark(e.dma_start(dram["counts"], c16[:]), "counts")
            st.mark(e.dma_start(dram["wmat"].rearrange("m p n -> p m n"),
                                wacc[:, 0:KC * KC * P].rearrange("p (m n) -> p m n", m=KC)), "wmat")
            st.wait(e, "wmat")

        @block.gpsimd
        def _(e):
            pl.mark(e.iota(iot[:], [[1, P]], base=0, channel_multiplier=0,
                           allow_small_or_imprecise_dtypes=True), "iota")
            e.memset(cacc[:], 0.0)
            pl.mark(e.memset(wacc[:], 0.0), "zero")

        @block.scalar
        def _(e):
            dv.wait(e, "wlo")
            with loops.run(e, "chunks", NCH // BODY) as i:
                for h in range(2):
                    pe.wait(e, f"w{h}", back=1)
                    dv.wait(e, f"hs{h}")
                    for u in range(UN):
                        c = i * BODY + (h * UN + u)
                        e.activation(wh[:, h, u], hs[:, h, u].bitcast(F32), ACT.Copy,
                                     scale=whi[:, bass.ds(c, 1)].bitcast(F32))
                        a = e.activation(wl[:, h, u], hs[:, h, u].bitcast(F32), ACT.Copy,
                                         scale=wlo[:, bass.ds(c, 1)])
                    act.mark(a, f"wh{h}")

        @block.tensor
        def _(e):
            pe.start(e, 2)
            with loops.run(e, "chunks", NCH // BODY):
                for h in range(2):
                    dv.wait(e, f"add{h}", back=1)
                    dv.wait(e, f"hd{h}")
                    for u in range(UN):
                        e.matmul(pc[2 * h + u // 4][:, u % 4], hs[:, h, u], hd[:, h, u], start=True, stop=True)
                    act.wait(e, f"wh{h}")
                    for u in range(UN):
                        o = pw[2 * h + u // 4][:, u % 4]
                        e.matmul(o, hd[:, h, u], wh[:, h, u], start=True, stop=False)
                        m = e.matmul(o, hd[:, h, u], wl[:, h, u], start=False, stop=True)
                    pe.mark(m, f"w{h}")

        @block.vector
        def _(e):
            dv.start(e, 8)
            ld.wait(e, "offw")
            e.tensor_copy(whi[:], slots[:, :, 2])
            e.drain()
            dv.mark(e.tensor_tensor(wlo[:], slots[:, :, 2], whi[:].bitcast(F32), ALU.subtract), "wlo")
            pl.wait(e, "iota")
            pl.wait(e, "zero")

            def hot(i, h):
                for field, out, step in ((0, hs, "hs"), (1, hd, "hd")):
                    t = slots[:, bass.ds(i * BODY + h * UN, UN), field]
                    dv.mark(e.tensor_tensor(out[:, h], t.unsqueeze(2).broadcast_to([P, UN, P]),
                                            iot[:].unsqueeze(1).broadcast_to([P, UN, P]), ALU.is_equal),
                            f"{step}{h}")

            with loops.run(e, "chunks", NCH // BODY) as i:
                for h in range(2):
                    pe.wait(e, f"w{h}", back=1)
                    hot(i, h)
                for h in range(2):
                    pe.wait(e, f"w{h}")
                    for u in range(UN):
                        c = i * BODY + (h * UN + u)
                        oc = e.value_load(offc[0:1, bass.ds(c, 1)], min_val=0, max_val=NBUCK * P)
                        ow = e.value_load(offw[0:1, bass.ds(c, 1)], min_val=0, max_val=KC * KC * P)
                        a, b = cacc[:, bass.ds(oc, P)], wacc[:, bass.ds(ow, P)]
                        e.tensor_tensor(a, a, pc[2 * h + u // 4][:, u % 4], ALU.add)
                        last = e.tensor_tensor(b, b, pw[2 * h + u // 4][:, u % 4], ALU.add)
                        if u < UN - 1:
                            e.drain()
                    dv.mark(last, f"add{h}")
                    e.drain()
            dv.mark(e.tensor_copy(c16[:], cacc[:, 0:NBUCK * P]), "c16")
    known.update({n: s.learned() for n, s in got.items()})


class Weights:

    def __init__(self, nc, ctx, tag, slots, width, new, dtype=F32, scale=None):
        t = lambda n, d: ctx.enter_context(nc.sbuf_tensor(f"{tag}_{n}", [P, slots, width], d))
        self.raw, self.hi, self.lo, self.scale = t("raw", dtype), t("hi", F32R), t("lo", F32R), scale
        self.loaded = [new(f"{tag}_ld{s}", 16) for s in range(slots)]
        self.his, self.los = new(f"{tag}_hi"), new(f"{tag}_lo")

    def load(self, e, slot, src, step):
        self.loaded[slot].mark(e.dma_start(self.raw[:, slot], src), step)

    def make_hi(self, e, slot, step, back=0):
        self.loaded[slot].wait(e, step, back)
        self.his.mark(e.activation(self.hi[:, slot], self.raw[:, slot], ACT.Copy, scale=self.scale or 1.0), step)

    def make_lo(self, e, slot, step, back=0):
        self.his.wait(e, step, back)
        hi = self.hi[:, slot].bitcast(F32)
        if self.scale is None:
            i = e.tensor_tensor(self.lo[:, slot], self.raw[:, slot], hi, ALU.subtract)
        else:
            i = e.scalar_tensor_tensor(self.lo[:, slot], self.raw[:, slot], self.scale, hi, ALU.mult, ALU.subtract)
        self.los.mark(i, step)

    def blocks(self, slot, first, count):
        cut = lambda w: [w[:, slot, (first + k) * P:(first + k + 1) * P] for k in range(count)]
        return cut(self.hi), cut(self.lo)


def product(e, out, w, x):
    (wh, wl), (xh, xl) = w, x
    terms = list(zip(wl, xh)) + list(zip(wh, xl)) + list(zip(wh, xh))
    for n, (a, b) in enumerate(terms):
        i = e.matmul(out, a, b, start=n == 0, stop=n == len(terms) - 1)
    return i


class Phase:

    def __init__(self, nc, known, tag):
        self.nc, self.known, self.tag = nc, known, tag
        self.ctx, self.loops, self.got = ExitStack(), Loops(), {}

    def __enter__(self):
        return self

    def __exit__(self, *a):
        self.ctx.close()
        if a[0] is None:
            self.nc.clear_and_free_semaphores([self.loops.spare] + [s.sem for s in self.got.values()])
            self.nc.all_engine_barrier()
        self.known.update({n: s.learned() for n, s in self.got.items()})

    def new(self, n, each=1):
        n = f"{self.tag}_{n}"
        s = self.got[n] = Steps(self.nc, self.ctx, self.loops, n, self.known, each)
        return s

    def sb(self, n, shape, d=F32):
        return self.ctx.enter_context(self.nc.sbuf_tensor(f"{self.tag}_{n}", shape, d))

    def banks(self, count):
        return [self.ctx.enter_context(self.nc.psum_tensor(f"{self.tag}_bank{i}", [P, 512], F32))
                for i in range(count)]

    def block(self):
        return self.ctx.enter_context(self.nc.Block())


def tile(t):
    return slice(t * TW, (t + 1) * TW)


def parts(xh, xl, t, count=KC):
    return [xh[:, k, tile(t)] for k in range(count)], [xl[:, k, tile(t)] for k in range(count)]


def layer_norm(nc, known, tag, x, xh, xl, x_dram=None):
    with Phase(nc, known, tag) as p:
        ld, pl, dv, pe, ac = p.new("ld", 16), p.new("pool"), p.new("dve"), p.new("pe"), p.new("act")
        ones = p.sb("ones", [P, P])
        xc = p.sb("xc", [P, NT, KC, TW])
        sq = p.sb("sq", [P, 2, KC, TW])
        ve, rv, y = (p.sb(n, [P, NT, TW]) for n in ("ve", "rv", "y"))
        z = p.sb("z", [P, TW])
        bank = p.banks(6)
        block = p.block()

        @block.sync
        def _(e):
            if x_dram is not None:
                for k in range(KC):
                    ld.mark(e.dma_start(x[:, k, 0:N], x_dram[k]), f"x{k}")

        @block.gpsimd
        def _(e):
            if x_dram is not None:
                e.memset(x[:, :, N:TM], 0.0)
            pl.mark(e.memset(ones[:], 1.0 / D), "ones")

        @block.tensor
        def _(e):
            pl.wait(e, "ones")
            if x_dram is not None:
                ld.wait(e, f"x{KC - 1}")
            for t in range(NT):
                for k in range(KC):
                    m = e.matmul(bank[t][:, 0:TW], ones[:], x[:, k, tile(t)], start=k == 0, stop=k == KC - 1)
                pe.mark(m, f"mean{t}")
            for t in range(NT):
                ac.wait(e, f"sq{t}")
                for k in range(KC):
                    m = e.matmul(bank[3 + t][:, 0:TW], ones[:], sq[:, t % 2, k], start=k == 0, stop=k == KC - 1)
                pe.mark(m, f"var{t}")

        @block.scalar
        def _(e):
            for t in range(NT):
                dv.wait(e, f"centred{t}")
                if t == 2:
                    pe.wait(e, "var0")
                ac.mark(e.activation(sq[:, t % 2], xc[:, t], ACT.Square), f"sq{t}")
            for t in range(NT):
                dv.wait(e, f"rv{t}")
                ac.mark(e.activation(y[:, t], rv[:, t], ACT.Sqrt), f"root{t}")
            for t in range(NT):
                dv.wait(e, f"normed{t}")
                ac.mark(e.activation(xh[:, :, tile(t)], xc[:, t], ACT.Copy), f"hi{t}")

        @block.vector
        def _(e):
            pl.wait(e, "ones")
            if x_dram is not None:
                ld.wait(e, f"x{KC - 1}")
            for t in range(NT):
                pe.wait(e, f"mean{t}")
                dv.mark(e.tensor_tensor(xc[:, t], x[:, :, tile(t)],
                                        bank[t][:, 0:TW].unsqueeze(1).broadcast_to([P, KC, TW]),
                                        ALU.subtract), f"centred{t}")
            for t in range(NT):
                pe.wait(e, f"var{t}")
                e.tensor_scalar(ve[:, t], bank[3 + t][:, 0:TW], EPS, None, ALU.add)
                e.drain()
                dv.mark(e.reciprocal(rv[:, t], ve[:, t]), f"rv{t}")
            for t in range(NT):
                ac.wait(e, f"root{t}")
                e.tensor_tensor(z[:], y[:, t], y[:, t], ALU.mult)
                e.drain()
                e.tensor_tensor(z[:], z[:], ve[:, t], ALU.mult)
                e.drain()
                e.tensor_scalar(z[:], z[:], -0.5, 1.5, ALU.mult, ALU.add)
                e.drain()
                e.tensor_tensor(y[:, t], y[:, t], z[:], ALU.mult)
                e.drain()
                dv.mark(e.tensor_tensor(xc[:, t], xc[:, t], y[:, t].unsqueeze(1).broadcast_to([P, KC, TW]),
                                        ALU.mult), f"normed{t}")
            for t in range(NT):
                ac.wait(e, f"hi{t}")
                e.tensor_tensor(xl[:, :, tile(t)], xc[:, t], xh[:, :, tile(t)].bitcast(F32), ALU.subtract)


def dense(nc, known, tag, xh, xl, w_dram, units, bias_dram, out=None, store=None, base=None, spill=None):
    with Phase(nc, known, tag) as p:
        w = Weights(nc, p.ctx, tag + "_w", 2, D, lambda n, each=1: p.new(n, each))
        ld, st, dv, pe, ac, pl = (p.new("ld", 16), p.new("st", 16), p.new("dve"), p.new("pe"), p.new("act"),
                                  p.new("pool"))
        bs, at = p.new("base", 16), p.new("at")
        sts = [p.new(f"st{b}", 16) for b in range(2)]
        bias = p.sb("bias", [P, units])
        to_dram = store is not None
        res = p.sb("res", [P, 2, NT, TW]) if to_dram else None
        bank = p.banks(6)
        block = p.block()
        turns = units // 2

        @block.sync
        def _(e):
            ld.mark(e.dma_start(bias[:], bias_dram, allow_slow_non_contiguous=True), "bias")
            w.load(e, 0, w_dram[0], "first")
            if base is not None:
                at.wait(e, "split")
                for k in range(KC):
                    bs.mark(e.dma_start(out[:, k, 0:N], base[k]), f"base{k}")
            with p.loops.run(e, "units", turns) as i:
                w.los.wait(e, "w1", back=1)
                w.load(e, 1, w_dram[i * 2 + 1], "w1")
                w.los.wait(e, "w0", back=1)
                w.load(e, 0, w_dram[(i * 2 + 2) % units], "w0")
                if to_dram:
                    for b in range(2):
                        for t in range(NT):
                            ac.wait(e, f"ev{b}{t}")
                        sts[b].mark(e.dma_start(store[i * 2 + b], res[:, b].rearrange("p t n -> p (t n)")), f"st{b}")
            if to_dram:
                sts[0].wait(e, "st0")
                sts[1].wait(e, "st1")
            if spill is not None:
                dv.wait(e, "ev12")
                for k in range(KC):
                    st.mark(e.dma_start(spill[k], out[:, k, 0:N]), f"spill{k}")
                st.wait(e, f"spill{KC - 1}")

        @block.scalar
        def _(e):
            if base is not None:
                for k in range(KC):
                    ac.mark(e.activation(xh[:, k], out[:, k], ACT.Copy), f"ah{k}")
            if to_dram:
                ac.start(e, 6)
            ld.wait(e, "bias")
            w.make_hi(e, 0, "first")
            with p.loops.run(e, "units", turns) as i:
                for b in range(2):
                    if b == 0:
                        pe.wait(e, "t12", back=1)
                        w.make_hi(e, 1, "w1")
                    else:
                        pe.wait(e, "t02")
                        w.make_hi(e, 0, "w0")
                    if to_dram:
                        sts[b].wait(e, f"st{b}", back=1)
                        for t in range(NT):
                            pe.wait(e, f"t{b}{t}")
                            ac.mark(e.activation(res[:, b, t], bank[3 * b + t][:, 0:TW], ACT.Identity,
                                                 bias=bias[:, bass.ds(i * 2 + b, 1)]), f"ev{b}{t}")

        @block.vector
        def _(e):
            if not to_dram:
                dv.start(e, 6)
            if base is not None:
                for k in range(KC):
                    ac.wait(e, f"ah{k}")
                    m = e.tensor_tensor(xl[:, k], out[:, k], xh[:, k].bitcast(F32), ALU.subtract)
                    at.mark(m, f"al{k}" if k < KC - 1 else "split")
            ld.wait(e, "bias")
            w.make_lo(e, 0, "first")
            if base is not None:
                bs.wait(e, f"base{KC - 1}")
            with p.loops.run(e, "units", turns) as i:
                for b in range(2):
                    w.make_lo(e, 1 - b, f"w{1 - b}")
                    if not to_dram:
                        for t in range(NT):
                            pe.wait(e, f"t{b}{t}")
                            o = out[:, i * 2 + b, tile(t)]
                            dv.mark(e.scalar_tensor_tensor(o, bank[3 * b + t][:, 0:TW],
                                                           bias[:, bass.ds(i * 2 + b, 1)], o, ALU.add, ALU.add),
                                    f"ev{b}{t}")

        @block.tensor
        def _(e):
            if base is not None:
                at.wait(e, "split")
            with p.loops.run(e, "units", turns):
                for b in range(2):
                    w.los.wait(e, f"w{b}", back=1 - b)
                    for t in range(NT):
                        (ac if to_dram else dv).wait(e, f"ev{b}{t}", back=1)
                        m = product(e, bank[3 * b + t][:, 0:TW], w.blocks(b, 0, KC), parts(xh, xl, t))
                        pe.mark(m, f"t{b}{t}")


def attention(nc, known, tag, xh, xl, at, w_dram, bq_dram, bkv_dram, softly):
    PAIRS, W2 = KC, 2 * P
    KW = W2 + 2
    Q, K, V = 0, 1, 2
    with Phase(nc, known, tag) as p:
        w = Weights(nc, p.ctx, tag + "_w", 3, D, lambda n, each=1: p.new(n, each))
        ld, pl = p.new("ld", 16), p.new("pool")
        dv_kv, dv_q, dv_m, dv_at = p.new("dkv"), p.new("dq"), p.new("dm"), p.new("dat")
        ac_kv, ac_q, ac_m = p.new("akv"), p.new("aq"), p.new("am")
        pe_kv, pe_q, pe_m, pe_at = p.new("pkv"), p.new("pq"), p.new("pm"), p.new("pat")
        bq = p.sb("bq", [P, KC])
        bkv = p.sb("bkv", [P, W2])
        bld = p.new("bld", 16)
        mask = p.sb("mask", [P, P])
        kvf = p.sb("kvf", [P, 4, W2])
        neg = p.sb("neg", [P, 4, P])
        kvh, kvl = p.sb("kvh", [P, TC, KW], F32R), p.sb("kvl", [P, TC, KW], F32R)
        qf = p.sb("qf", [P, NT, TW])
        qn = p.sb("qn", [P, NT, TW])
        qh, ql = p.sb("qh", [P, TM], F32R), p.sb("ql", [P, TM], F32R)
        ks = p.sb("ks", [P, 1])
        mf = p.sb("mf", [P, W2])
        mh, ml = p.sb("mh", [P, W2], F32R), p.sb("ml", [P, W2], F32R)
        bank = p.banks(8)
        NUM, DEN = (7, 0, 2), (6, 1, 5)
        MW = W2 if softly else P
        block = p.block()

        @block.sync
        def _(e):
            ld.mark(e.dma_start(bq[:], bq_dram, allow_slow_non_contiguous=True), "bq")
            bld.mark(e.dma_start(bkv[:], bkv_dram[0:1].broadcast_to([P, W2])), "first")
            for n, s in enumerate((K, V, Q)):
                w.load(e, s, w_dram[n], f"first{s}")
            with p.loops.run(e, "pairs", PAIRS) as j:
                for n, s in enumerate((K, V, Q)):
                    w.los.wait(e, f"w{s}", back=1)
                    w.load(e, s, w_dram[(j * 3 + (3 + n)) % (3 * PAIRS)], f"w{s}")
                    if s == V:
                        dv_kv.wait(e, f"kv{TC - 1}")
                        bld.mark(e.dma_start(bkv[:], bkv_dram[bass.ds((j + 1) % PAIRS, 1)].broadcast_to([P, W2])),
                                 "next")
            bld.wait(e, "next")

        @block.gpsimd
        def _(e):
            for a in range(2):
                for b in range(2):
                    i = e.memset(mask[64 * a:64 * a + 64, 64 * b:64 * b + 64], 1.0 if a == b else 0.0)
                pl.mark(i, f"mask{a}")
                pl.wait(e, f"mask{a}")
            e.memset(kvh[:, :, W2:KW].bitcast(F32), 1.0)
            pl.mark(e.memset(kvl[:, :, W2:KW].bitcast(F32), 0.0), "consts")

        @block.tensor
        def _(e):
            pl.wait(e, "consts")
            with p.loops.run(e, "pairs", PAIRS):
                w.los.wait(e, f"w{V}", back=1)
                dv_at.wait(e, "at2", back=1)
                for c in range(TC):
                    r = rows_of(c)
                    if c < 3:
                        dv_kv.wait(e, f"kv{TC - 3 + c}", back=1)
                    else:
                        dv_kv.wait(e, f"kv{c - 3}")
                    tok = slice(c * P, c * P + r)
                    n = 0
                    for a, b in ((xh, w.lo), (xl, w.hi), (xh, w.hi)):
                        for k in range(KC):
                            m = e.matmul(bank[3 + c % 3][0:r, 0:W2], a[:, k, tok],
                                         b[:, K:V + 1, k * P:(k + 1) * P], start=n == 0, stop=n == 3 * KC - 1)
                            n += 1
                    pe_kv.mark(m, f"kv{c}")
                w.los.wait(e, f"w{Q}", back=1)
                for t in range(NT):
                    pe_q.mark(product(e, bank[t][:, 0:TW], w.blocks(Q, 0, KC), parts(xh, xl, t)), f"q{t}")
                dv_kv.wait(e, f"lo{TC - 1}")
                n = 0
                for a, b in ((kvl, kvh), (kvh, kvl), (kvh, kvh)):
                    for c in range(TC):
                        r = rows_of(c)
                        m = e.matmul(bank[6][:, 0:P + 2], a[0:r, c, 0:P], b[0:r, c, P:KW],
                                     start=n == 0, stop=n == 3 * TC - 1)
                        n += 1
                pe_m.mark(m, "m")
                dv_q.wait(e, "lo2")
                dv_m.wait(e, "lo")
                for t in range(NT):
                    for cut, b in ((slice(0, P), NUM[t]), (slice(P, W2), DEN[t]))[:2 if softly else 1]:
                        e.matmul(bank[b][:, 0:TW], ml[:, cut], qh[:, tile(t)], start=True, stop=False)
                        e.matmul(bank[b][:, 0:TW], mh[:, cut], ql[:, tile(t)], start=False, stop=False)
                        m = e.matmul(bank[b][:, 0:TW], mh[:, cut], qh[:, tile(t)], start=False, stop=True)
                    pe_at.mark(m, f"at{t}")

        @block.scalar
        def _(e):
            ac_q.start(e, 16)
            for s in (K, V, Q):
                w.make_hi(e, s, f"first{s}")
            ld.wait(e, "bq")
            with p.loops.run(e, "pairs", PAIRS) as j:
                for s in range(TC + 1):
                    if s < TC and softly:
                        dv_kv.wait(e, f"kv{s}")
                        r = rows_of(s)
                        ac_kv.mark(e.activation(neg[0:r, s % 4], neg[0:r, s % 4], ACT.Exp), f"exp{s}")
                    if s >= 1:
                        c = s - 1
                        r = rows_of(c)
                        dv_kv.wait(e, f"map{c}")
                        if c == 0:
                            pe_m.wait(e, "m", back=1)
                        ac_kv.mark(e.activation(kvh[0:r, c, 0:W2], kvf[0:r, c % 4], ACT.Copy), f"hi{c}")
                pe_kv.wait(e, f"kv{TC - 1}")
                w.make_hi(e, K, f"w{K}")
                w.make_hi(e, V, f"w{V}")
                for t in range(NT):
                    pe_q.wait(e, f"q{t}")
                    ac_q.mark(e.activation(qf[:, t], bank[t][:, 0:TW], ACT.Identity if softly else ACT.Relu,
                                           bias=bq[:, bass.ds(j, 1)]), f"q{t}")
                if softly:
                    for t in range(NT):
                        dv_q.wait(e, f"neg{t}")
                        ac_q.mark(e.activation(qn[:, t], qn[:, t], ACT.Exp), f"exp{t}")
                else:
                    e.drain()
                pe_at.wait(e, "at2", back=1)
                for t in range(NT):
                    if softly:
                        dv_q.wait(e, f"map{t}")
                    ac_q.mark(e.activation(qh[:, tile(t)], qf[:, t], ACT.Copy), f"hi{t}")
                w.make_hi(e, Q, f"w{Q}")
                dv_m.wait(e, "m")
                ac_m.mark(e.activation(mh[:, 0:MW], mf[:, 0:MW], ACT.Copy), "hi")

        @block.vector
        def _(e):
            dv_kv.start(e, 64)
            pl.wait(e, "consts")
            for s in (K, V, Q):
                w.make_lo(e, s, f"first{s}")
            with p.loops.run(e, "pairs", PAIRS) as j:
                bld.wait(e, "next", back=1)
                for s in range(TC + 2):
                    if s < TC:
                        r = rows_of(s)
                        pe_kv.wait(e, f"kv{s}")
                        f = kvf[0:r, s % 4]
                        i = e.tensor_tensor(f, bank[3 + s % 3][0:r, 0:W2], bkv[0:r], ALU.add)
                        e.drain()
                        if softly:
                            i = e.tensor_scalar(neg[0:r, s % 4], f[:, 0:P], 0.0, None, ALU.min)
                            dv_kv.mark(i, f"kv{s}")
                        else:
                            dv_kv.mark(e.tensor_scalar(f[:, 0:P], f[:, 0:P], 0.0, None, ALU.max), f"kv{s}")
                    if 1 <= s <= TC:
                        c = s - 1
                        r = rows_of(c)
                        f = kvf[0:r, c % 4]
                        if softly:
                            ac_kv.wait(e, f"exp{c}")
                            dv_kv.mark(e.scalar_tensor_tensor(f[:, 0:P], f[:, 0:P], 0.0, neg[0:r, c % 4],
                                                              ALU.max, ALU.add), f"map{c}")
                        else:
                            dv_kv.alias(f"map{c}", f"kv{c}")
                    if s >= 2:
                        c = s - 2
                        r = rows_of(c)
                        ac_kv.wait(e, f"hi{c}")
                        dv_kv.mark(e.tensor_tensor(kvl[0:r, c, 0:W2], kvf[0:r, c % 4],
                                                   kvh[0:r, c, 0:W2].bitcast(F32), ALU.subtract), f"lo{c}")
                w.make_lo(e, K, f"w{K}")
                w.make_lo(e, V, f"w{V}")
                if softly:
                    for t in range(NT):
                        ac_q.wait(e, f"q{t}")
                        dv_q.mark(e.tensor_scalar(qn[:, t], qf[:, t], 0.0, None, ALU.min), f"neg{t}")
                    for t in range(NT):
                        ac_q.wait(e, f"exp{t}")
                        dv_q.mark(e.scalar_tensor_tensor(qf[:, t], qf[:, t], 0.0, qn[:, t], ALU.max, ALU.add),
                                  f"map{t}")
                for t in range(NT):
                    ac_q.wait(e, f"hi{t}")
                    dv_q.mark(e.tensor_tensor(ql[:, tile(t)], qf[:, t], qh[:, tile(t)].bitcast(F32),
                                              ALU.subtract), f"lo{t}")
                w.make_lo(e, Q, f"w{Q}")
                pe_m.wait(e, "m")
                if softly:
                    e.tensor_copy(ks[:], bank[6][:, P:P + 1])
                    e.drain()
                    e.tensor_scalar(mf[:, P:W2], mask[:], ks[:, 0:1], None, ALU.mult)
                dv_m.mark(e.tensor_tensor(mf[:, 0:P], bank[6][:, 0:P], mask[:], ALU.mult), "m")
                ac_m.wait(e, "hi")
                dv_m.mark(e.tensor_tensor(ml[:, 0:MW], mf[:, 0:MW], mh[:, 0:MW].bitcast(F32), ALU.subtract), "lo")
                for t in range(NT):
                    pe_at.wait(e, f"at{t}")
                    o = at[:, bass.ds(j, 1), tile(t)].rearrange("p a b -> p (a b)")
                    if softly:
                        e.tensor_scalar(qn[:, t], bank[DEN[t]][:, 0:TW], 1e-6, None, ALU.add)
                        e.drain()
                        e.reciprocal(qn[:, t], qn[:, t])
                        e.drain()
                        i = e.tensor_tensor(o, bank[NUM[t]][:, 0:TW], qn[:, t], ALU.mult)
                    else:
                        i = e.tensor_copy(o, bank[NUM[t]][:, 0:TW])
                    dv_at.mark(i, f"at{t}")


def graph_layer(nc, known, tag, x, dram):
    HOPS, HALF = 4, TC // 2
    HWID = (HALF * P, N - HALF * P)
    with Phase(nc, known, tag) as p:
        ld, st, pl = p.new("ld", 16), p.new("st", 16), p.new("pool")
        x1s = [p.new(f"x1_{b}", 16) for b in range(2)]
        pe_t, dv_t = p.new("pt"), p.new("dt")
        pe_s, dv_s, ac_s = p.new("ps"), p.new("ds"), p.new("as")
        pe_g, dv_g, dv_o, ac_g = p.new("pg"), p.new("dg"), p.new("do"), p.new("ag")
        dv_a, ac_a, pe_a = p.new("da"), p.new("aa"), p.new("pa")
        x1 = p.sb("x1", [P, 2, TM])
        cnt = p.sb("cnt", [P, TC, TC * P], U16)
        cf = p.sb("cf", [P, N])
        g = p.sb("g", [P, TC, NH])
        gf = p.sb("gf", [P, 4, NH])
        gh, gl = p.sb("gh", [P, TC, NH], F32R), p.sb("gl", [P, TC, NH], F32R)
        gw = p.sb("gw", [P, 2, NH])
        gld = p.new("gld", 16)
        gb = p.sb("gb", [P, HOPS])
        ident, ones = p.sb("ident", [P, P]), p.sb("ones", [P, P])
        deg, rdeg, dis, z = (p.sb(n, [P, TC]) for n in ("deg", "rdeg", "dis", "z"))
        ga, gs = p.sb("ga", [P, TC]), p.sb("gs", [P, TC])
        diag = p.sb("diag", [P, TC, P])
        ab = p.sb("ab", [P, TM])
        th = p.sb("th", [P, 2, HALF * P])
        af = p.sb("af", [P, 4, HALF * P])
        ah, al = p.sb("ah", [P, 2, HALF * P], F32R), p.sb("al", [P, 2, HALF * P], F32R)
        bank = p.banks(8)
        block = p.block()
        BANKS = ((0, 1, 2, 3, 4), (5, 6, 7, 0, 1))

        @block.sync
        def _(e):
            for m in range(GC):
                if m >= 2:
                    dv_t.wait(e, f"x1_{m - 2}")
                x1s[m % 2].mark(e.dma_start(x1[:, m % 2], dram["x1"][m]), f"x1_{m}")
                if m == 1:
                    ld.mark(e.dma_start(cnt[:].rearrange("p a b -> p (a b)"), dram["counts"]), "cnt")
                    ld.mark(e.dma_start(gb[:], dram["gate_b"].broadcast_to([P, HOPS])), "gb")
            gwf = gw[:].rearrange("p b c -> p (b c)")
            gld.mark(e.dma_start(gwf, dram["gate_w"][0:1].broadcast_to([P, 2 * NH])), "first")
            with p.loops.run(e, "hops", HOPS) as k:
                dv_g.wait(e, "gs")
                gld.mark(e.dma_start(gwf, dram["gate_w"][bass.ds((k + 1) % HOPS, 1)].broadcast_to([P, 2 * NH])),
                         "next")
            gld.wait(e, "next")

        @block.gpsimd
        def _(e):
            e.memset(ones[:], 1.0)
            e.memset(ga[:], 0.0)
            e.memset(gs[:], 0.0)
            e.memset(g[:, TC - 1], 0.0)
            pl.mark(e.memset(ident[:], 1.0), "one")
            pl.wait(e, "one")
            pl.mark(e.affine_select(out=ident[:], in_=ident[:], compare_op=ALU.is_equal, fill=0.0, base=0,
                                    pattern=[[1, P]], channel_multiplier=-1), "ident")

        def turned(m, c):
            n = m * TC + c
            return n % 4, slice(0, P)

        @block.tensor
        def _(e):
            pe_a.start(e, 2)
            pl.wait(e, "ident")
            for m in range(GC):
                x1s[m % 2].wait(e, f"x1_{m}")
                for c in range(TC):
                    r, n = rows_of(c), m * TC + c
                    if n >= 4:
                        dv_t.wait(e, f"g{n - 4}")
                    pe_t.mark(e.transpose(bank[n % 4][0:r, 0:P], x1[:, m % 2, c * P:c * P + r], ident[:]), f"t{n}")
            for c in range(TC):
                r = rows_of(c)
                dv_s.wait(e, f"cf{c}")
                for d in range(TC):
                    q = rows_of(d)
                    m = e.matmul(bank[4][0:q, d:d + 1], cf[0:r, d * P:d * P + q], ones[0:r, 0:1],
                                 start=c == 0 and d == 0, stop=c == TC - 1, skip_group_check=True)
                pe_s.mark(m, f"deg{c}")
            with p.loops.run(e, "hops", HOPS):
                dv_g.wait(e, "diag")
                for t in range(NT):
                    m = e.matmul(bank[5 + t][:, 0:TW], ones[:], diag[:].rearrange("p a b -> p (a b)")[:, tile(t)],
                                 start=True, stop=True)
                pe_g.mark(m, "ab")
                for h in range(2):
                    for c in range(TC):
                        r = rows_of(c)
                        dv_a.wait(e, f"al{h}{c}")
                        if c == 0:
                            if h == 0:
                                dv_o.wait(e, "out1", back=1)
                            else:
                                ac_g.wait(e, "ab")
                                dv_o.wait(e, "out0")
                        for d in range(HALF):
                            q = rows_of(h * HALF + d)
                            cut = slice(d * P, d * P + q)
                            o = bank[BANKS[h][d]][0:q, :]
                            e.matmul(o, al[0:r, c % 2, cut], gh[0:r, c], start=c == 0, stop=False)
                            e.matmul(o, ah[0:r, c % 2, cut], gl[0:r, c], start=False, stop=False)
                            m = e.matmul(o, ah[0:r, c % 2, cut], gh[0:r, c], start=False, stop=c == TC - 1)
                        pe_a.mark(m, f"a{h}{c}")
            dv_o.wait(e, "out1")
            for m in range(GC):
                for c in range(TC):
                    r, n = rows_of(c), m * TC + c
                    if n >= 8:
                        dv_t.wait(e, f"x{n - 8}")
                    pe_t.mark(e.transpose(bank[n % 8][:, 0:r], g[0:r, c, m * P:(m + 1) * P],
                                          ident[0:r, 0:r]), f"b{n}")

        @block.scalar
        def _(e):
            dv_s.wait(e, "rdeg")
            ac_s.mark(e.activation(dis[:], rdeg[:], ACT.Sqrt), "root")
            with p.loops.run(e, "hops", HOPS):
                for c in range(TC):
                    r = rows_of(c)
                    dv_g.wait(e, f"gf{c}")
                    if c == 0:
                        pe_a.wait(e, f"a1{TC - 1}", back=1)
                    ac_g.mark(e.activation(gh[0:r, c], gf[0:r, c % 4], ACT.Copy), f"gh{c}")
                pe_g.wait(e, "ab")
                for t in range(NT):
                    i = e.activation(ab[:, tile(t)], bank[5 + t][:, 0:TW], ACT.Copy)
                ac_g.mark(i, "ab")
                e.drain()
                dv_g.wait(e, "gs")
                for h in range(2):
                    for s in range(TC + 1):
                        if s < TC:
                            r, b = rows_of(s), s % 2
                            if s >= 2:
                                dv_a.wait(e, f"af{h}{s - 2}")
                            cols = slice(h * HALF * P, h * HALF * P + HWID[h])
                            ac_a.mark(e.activation(th[0:r, b, 0:HWID[h]], ab[0:r, cols], ACT.Tanh,
                                                   bias=gs[0:r, s:s + 1]), f"th{h}{s}")
                        if s >= 1:
                            c = s - 1
                            r, b = rows_of(c), c % 2
                            dv_a.wait(e, f"af{h}{c}")
                            if c >= 2:
                                pe_a.wait(e, f"a{h}{c - 2}")
                            elif h == 1:
                                pe_a.wait(e, f"a0{TC - 2 + c}")
                            else:
                                pe_a.wait(e, f"a1{TC - 2 + c}", back=1)
                            ac_a.mark(e.activation(ah[0:r, b, 0:HWID[h]], af[0:r, c % 4, 0:HWID[h]], ACT.Copy),
                                      f"ah{h}{c}")

        @block.vector
        def _(e):
            dv_o.start(e, 2)
            pl.wait(e, "ident")
            for m in range(GC):
                for c in range(TC):
                    r, n = rows_of(c), m * TC + c
                    pe_t.wait(e, f"t{n}")
                    dv_t.mark(e.tensor_copy(g[0:r, c, m * P:(m + 1) * P], bank[n % 4][0:r, 0:P]), f"g{n}")
                dv_t.mark(e.tensor_tensor(x[:, m], x[:, m], x1[:, m % 2], ALU.add), f"x1_{m}")
            ld.wait(e, "gb")
            for c in range(TC):
                r = rows_of(c)
                if c:
                    pe_s.wait(e, f"deg{c - 1}")
                dv_s.mark(e.tensor_copy(cf[0:r], cnt[0:r, c, 0:N]), f"cf{c}")
            pe_s.wait(e, f"deg{TC - 1}")
            e.memset(deg[:], 1.0)
            e.drain()
            e.tensor_scalar(deg[:, 0:TC - 1], bank[4][:, 0:TC - 1], 1.0, None, ALU.max)
            e.tensor_scalar(deg[0:LAST, TC - 1:TC], bank[4][0:LAST, TC - 1:TC], 1.0, None, ALU.max)
            e.drain()
            dv_s.mark(e.reciprocal(rdeg[:], deg[:]), "rdeg")
            ac_s.wait(e, "root")
            e.tensor_tensor(z[:], dis[:], dis[:], ALU.mult)
            e.drain()
            e.tensor_tensor(z[:], z[:], deg[:], ALU.mult)
            e.drain()
            e.tensor_scalar(z[:], z[:], -0.5, 1.5, ALU.mult, ALU.add)
            e.drain()
            e.tensor_tensor(dis[:], dis[:], z[:], ALU.mult)
            e.drain()
            with p.loops.run(e, "hops", HOPS) as k:
                gld.wait(e, "next", back=1)
                for c in range(TC):
                    r = rows_of(c)
                    e.tensor_tensor_reduce(gl[0:r, c], g[0:r, c], gw[0:r, 0],
                                           1.0, 0.0, ALU.mult, ALU.add, ga[0:r, c:c + 1])
                e.drain()
                dv_g.mark(e.tensor_tensor(diag[:], ident[:].unsqueeze(1).broadcast_to([P, TC, P]),
                                          ga[:].unsqueeze(2).broadcast_to([P, TC, P]), ALU.mult), "diag")
                for c in range(TC):
                    r = rows_of(c)
                    e.tensor_tensor_reduce(gl[0:r, c], g[0:r, c], gw[0:r, 1],
                                           1.0, 0.0, ALU.mult, ALU.add, gs[0:r, c:c + 1])
                e.drain()
                dv_g.mark(e.tensor_scalar(gs[:], gs[:], gb[:, bass.ds(k, 1)], None, ALU.add), "gs")
                for c in range(TC + 1):
                    if c < TC:
                        r = rows_of(c)
                        dv_g.mark(e.tensor_scalar(gf[0:r, c % 4], g[0:r, c], dis[0:r, c:c + 1], None, ALU.mult),
                                  f"gf{c}")
                    if c >= 1:
                        r = rows_of(c - 1)
                        ac_g.wait(e, f"gh{c - 1}")
                        e.tensor_tensor(gl[0:r, c - 1], gf[0:r, (c - 1) % 4], gh[0:r, c - 1].bitcast(F32),
                                        ALU.subtract)
                for h in range(2):
                    for s in range(TC + 1):
                        if s < TC:
                            r, b = rows_of(s), s % 2
                            ac_a.wait(e, f"th{h}{s}")
                            cols = slice(h * HALF * P, h * HALF * P + HWID[h])
                            dv_a.mark(e.tensor_tensor(af[0:r, s % 4, 0:HWID[h]], th[0:r, b, 0:HWID[h]],
                                                      cnt[0:r, s, cols], ALU.mult), f"af{h}{s}")
                        if s >= 1:
                            c = s - 1
                            r, b = rows_of(c), c % 2
                            ac_a.wait(e, f"ah{h}{c}")
                            dv_a.mark(e.tensor_tensor(al[0:r, b, 0:HWID[h]], af[0:r, c % 4, 0:HWID[h]],
                                                      ah[0:r, b, 0:HWID[h]].bitcast(F32), ALU.subtract),
                                      f"al{h}{c}")
                    pe_a.wait(e, f"a{h}{TC - 1}")
                    for d in range(HALF):
                        c = h * HALF + d
                        q = rows_of(c)
                        i = e.scalar_tensor_tensor(g[0:q, c], bank[BANKS[h][d]][0:q, :], dis[0:q, c:c + 1],
                                                   g[0:q, c], ALU.mult, ALU.add)
                    dv_o.mark(i, f"out{h}")
                e.drain()
            for m in range(GC):
                for c in range(TC):
                    r, n = rows_of(c), m * TC + c
                    pe_t.wait(e, f"b{n}")
                    o = x[:, GC + m, c * P:c * P + r]
                    dv_t.mark(e.tensor_tensor(o, o, bank[n % 8][:, 0:r], ALU.add), f"x{n}")


def router(nc, known, tag, xh, xl, gate_dram, tw):
    EX = 8
    with Phase(nc, known, tag) as p:
        ld, pl, dv, pe, ac = p.new("ld", 16), p.new("pool"), p.new("dve"), p.new("pe"), p.new("act")
        gr = p.sb("gr", [P, KC, EX])
        gh, gl = p.sb("gh", [P, KC, EX], F32R), p.sb("gl", [P, KC, EX], F32R)
        lg, top = p.sb("lg", [P, TC, EX]), p.sb("top", [P, TC, EX])
        at = p.sb("at", [P, TC, EX], U32)
        af = p.sb("af", [P, TC, EX])
        io = p.sb("io", [P, EX])
        df, ex, w1, w2 = (p.sb(n, [P, TC]) for n in ("df", "ex", "w1", "w2"))
        hot = p.sb("hot", [P, TC, EX])
        bank = p.banks(1)
        block = p.block()

        @block.sync
        def _(e):
            ld.mark(e.dma_start(gr[:].rearrange("p a b -> p (a b)"), gate_dram), "gate")

        @block.gpsimd
        def _(e):
            e.memset(lg[:], 0.0)
            pl.mark(e.iota(io[:], [[1, EX]], base=0, channel_multiplier=0, allow_small_or_imprecise_dtypes=True),
                    "iota")

        @block.scalar
        def _(e):
            dv.wait(e, "df")
            ac.mark(e.activation(ex[:], df[:], ACT.Exp), "exp")

        @block.tensor
        def _(e):
            dv.wait(e, "gate")
            for c in range(TC):
                r = rows_of(c)
                tok = slice(c * P, c * P + r)
                n = 0
                for a, b in ((xl, gh), (xh, gl), (xh, gh)):
                    for k in range(KC):
                        m = e.matmul(bank[0][0:r, c * EX:(c + 1) * EX], a[:, k, tok], b[:, k],
                                     start=n == 0, stop=n == 3 * KC - 1)
                        n += 1
            pe.mark(m, "logits")

        @block.vector
        def _(e):
            ld.wait(e, "gate")
            e.tensor_copy(gh[:], gr[:])
            e.drain()
            dv.mark(e.tensor_tensor(gl[:], gr[:], gh[:].bitcast(F32), ALU.subtract), "gate")
            pl.wait(e, "iota")
            pe.wait(e, "logits")
            b = bank[0][:, 0:TC * EX].rearrange("p (c x) -> p c x", x=EX)
            e.tensor_copy(lg[:, 0:TC - 1], b[:, 0:TC - 1])
            e.tensor_copy(lg[0:LAST, TC - 1], b[0:LAST, TC - 1])
            e.drain()
            for c in range(TC):
                e.max(top[:, c], lg[:, c])
            e.drain()
            for c in range(TC):
                e.max_index(at[:, c], top[:, c], lg[:, c])
            dv.mark(e.tensor_tensor(df[:], top[:, :, 1], top[:, :, 0], ALU.subtract), "df")
            e.drain()
            e.tensor_copy(af[:], at[:])
            ac.wait(e, "exp")
            e.tensor_scalar(w2[:], ex[:], 1.0, None, ALU.add)
            e.drain()
            e.reciprocal(w1[:], w2[:])
            e.drain()
            e.tensor_tensor(w2[:], w1[:], ex[:], ALU.mult)
            wide = lambda t: t.unsqueeze(2).broadcast_to([P, TC, EX])
            iow = io[:].unsqueeze(1).broadcast_to([P, TC, EX])
            e.tensor_tensor(hot[:], wide(af[:, :, 0]), iow, ALU.is_equal)
            e.drain()
            e.tensor_tensor(tw[:], hot[:], wide(w1[:]), ALU.mult)
            e.drain()
            e.tensor_tensor(hot[:], wide(af[:, :, 1]), iow, ALU.is_equal)
            e.drain()
            e.tensor_tensor(hot[:], hot[:], wide(w2[:]), ALU.mult)
            e.drain()
            e.tensor_tensor(tw[:], tw[:], hot[:], ALU.add)


def gated_mlp(nc, known, tag, x, xh, xl, w_dram, hc, experts=None, dtype=F32, scale=None):
    count, tw = experts or (1, None)
    with Phase(nc, known, tag) as p:
        w = Weights(nc, p.ctx, tag + "_w", 2, D, lambda n, each=1: p.new(n, each), dtype, scale)
        pl, pe, pe_wb, dv, dv_d, ac, ac_wb = (p.new(n) for n in ("pool", "pe", "pwb", "dve", "dd", "act", "awb"))
        hh, hl = p.sb("hh", [P, hc, TM], F32R), p.sb("hl", [P, hc, TM], F32R)
        sg, hf = p.sb("sg", [P, NT, TW]), p.sb("hf", [P, NT, TW])
        if tw is not None:
            wb = p.sb("wb", [P, TM])
            ident, ones = p.sb("ident", [P, P]), p.sb("ones", [P, P])
            diag = p.sb("diag", [P, TC, P])
        bank = p.banks(8)
        block = p.block()
        downs = KC // 4
        per = 2 * hc + 2 * downs
        total = count * per
        flat = lambda ap: ap.rearrange("p a b -> p (a b)")

        @block.sync
        def _(e):
            w.load(e, 0, w_dram[0], "first")
            with p.loops.run(e, "experts", count) as x_:
                for kind, at, turns in (("u", 0, hc), ("d", 2 * hc, downs)):
                    with p.loops.run(e, kind, turns) as i:
                        w.los.wait(e, kind + "1", back=1)
                        w.load(e, 1, w_dram[x_ * per + i * 2 + (at + 1)], kind + "1")
                        w.los.wait(e, kind + "0", back=1)
                        w.load(e, 0, w_dram[(x_ * per + i * 2 + (at + 2)) % total], kind + "0")

        @block.gpsimd
        def _(e):
            if tw is not None:
                e.memset(ones[:], 1.0)
                pl.mark(e.memset(ident[:], 1.0), "one")
                pl.wait(e, "one")
                pl.mark(e.affine_select(out=ident[:], in_=ident[:], compare_op=ALU.is_equal, fill=0.0, base=0,
                                        pattern=[[1, P]], channel_multiplier=-1), "ident")

        @block.tensor
        def _(e):
            with p.loops.run(e, "experts", count):
                dv.wait(e, "x112", back={"experts": 1})
                if tw is not None:
                    dv_d.wait(e, "diag")
                    for t in range(NT):
                        if t == 2:
                            ac_wb.wait(e, "wb0")
                        pe_wb.mark(e.matmul(bank[6 + t % 2][:, 0:TW], ones[:], flat(diag[:])[:, tile(t)],
                                            start=True, stop=True), f"wb{t}")
                with p.loops.run(e, "u", hc):
                    w.los.wait(e, "u0", back=1)
                    for t in range(NT):
                        ac.wait(e, f"sg{t}", back=1)
                        m = product(e, bank[t][:, 0:TW], w.blocks(0, 0, KC), parts(xh, xl, t))
                        pe.mark(m, f"g{t}")
                    w.los.wait(e, "u1")
                    for t in range(NT):
                        dv.wait(e, f"h{t}", back=1)
                        m = product(e, bank[3 + t][:, 0:TW], w.blocks(1, 0, KC), parts(xh, xl, t))
                        pe.mark(m, f"u{t}")
                dv.wait(e, "lo2")
                with p.loops.run(e, "d", downs):
                    for b in range(2):
                        w.los.wait(e, f"d{b}", back=1 - b)
                        for r in range(2):
                            for t in range(NT):
                                dv.wait(e, f"x{1 - b}{r}{t}", back=1 - b)
                                m = product(e, bank[3 * r + t][:, 0:TW], w.blocks(b, r * hc, hc),
                                            parts(hh, hl, t, hc))
                                pe.mark(m, f"d{b}{r}{t}")

        @block.scalar
        def _(e):
            ac.start(e, 6)
            w.make_hi(e, 0, "first")
            with p.loops.run(e, "experts", count):
                if tw is not None:
                    dv.wait(e, "x112", back={"experts": 1})
                    for t in range(NT):
                        pe_wb.wait(e, f"wb{t}")
                        ac_wb.mark(e.activation(wb[:, tile(t)], bank[6 + t % 2][:, 0:TW], ACT.Copy), f"wb{t}")
                with p.loops.run(e, "u", hc) as i:
                    pe.wait(e, "u2", back=1)
                    w.make_hi(e, 1, "u1")
                    for t in range(NT):
                        pe.wait(e, f"g{t}")
                        dv.wait(e, f"h{t}", back=1)
                        ac.mark(e.activation(sg[:, t], bank[t][:, 0:TW], ACT.Silu), f"sg{t}")
                    w.make_hi(e, 0, "u0")
                    for t in range(NT):
                        dv.wait(e, f"f{t}")
                        ac.mark(e.activation(flat(hh[:, bass.ds(i, 1), tile(t)]), hf[:, t], ACT.Copy), f"hh{t}")
                with p.loops.run(e, "d", downs):
                    pe.wait(e, "d112", back=1)
                    w.make_hi(e, 1, "d1")
                    pe.wait(e, "d012")
                    w.make_hi(e, 0, "d0")

        @block.vector
        def _(e):
            dv.start(e, 12)
            w.make_lo(e, 0, "first")
            if tw is not None:
                pl.wait(e, "ident")
            with p.loops.run(e, "experts", count) as x_:
                if tw is not None:
                    pe_wb.wait(e, "wb2", back=1)
                    col = tw[:, :, bass.ds(x_, 1)].broadcast_to([P, TC, P])
                    dv_d.mark(e.tensor_tensor(diag[:], ident[:].unsqueeze(1).broadcast_to([P, TC, P]), col,
                                              ALU.mult), "diag")
                    ac_wb.wait(e, "wb2")
                with p.loops.run(e, "u", hc) as i:
                    w.make_lo(e, 1, "u1")
                    for t in range(NT):
                        pe.wait(e, f"u{t}")
                        ac.wait(e, f"sg{t}")
                        dv.mark(e.tensor_tensor(hf[:, t], sg[:, t], bank[3 + t][:, 0:TW], ALU.mult), f"h{t}")
                        if tw is None:
                            dv.alias(f"f{t}", f"h{t}")
                        else:
                            e.drain()
                            dv.mark(e.tensor_tensor(hf[:, t], hf[:, t], wb[:, tile(t)], ALU.mult), f"f{t}")
                    w.make_lo(e, 0, "u0")
                    for t in range(NT):
                        ac.wait(e, f"hh{t}")
                        dv.mark(e.tensor_tensor(flat(hl[:, bass.ds(i, 1), tile(t)]), hf[:, t],
                                                flat(hh[:, bass.ds(i, 1), tile(t)]).bitcast(F32), ALU.subtract),
                                f"lo{t}")
                with p.loops.run(e, "d", downs) as i:
                    for b in range(2):
                        w.make_lo(e, 1 - b, f"d{1 - b}")
                        for r in range(2):
                            for t in range(NT):
                                pe.wait(e, f"d{b}{r}{t}")
                                o = flat(x[:, bass.ds(i * 4 + (2 * b + r), 1), tile(t)])
                                dv.mark(e.tensor_tensor(o, o, bank[3 * r + t][:, 0:TW], ALU.add), f"x{b}{r}{t}")


def build(nc, io, known):
    dram = lambda n, shape, d=F32: nc.dram_tensor("scratch_" + n, shape, d).ap()
    slots = dram("slots", (P, NCH * 4))
    graph = dict(src=io["src"], dst=io["dst"], edge_weight=io["edge_weight"], slots=slots,
                 slot_rows=slots.rearrange("p (c f) -> (p c) f", f=4), offs=dram("offs", (P, 4), I32),
                 counts=dram("counts", (P, NBUCK * P), U16), wmat=dram("wmat", (KC, P, D)))
    x1 = dram("x1", (GC, P, TM))
    xs = dram("xs", (KC, P, N))
    graph_sort(nc, known, graph)
    graph_build(nc, known, graph)
    with ExitStack() as ctx:
        x = ctx.enter_context(nc.sbuf_tensor("x", [P, KC, TM], F32))

        @contextmanager
        def normed(layer):
            with (nc.sbuf_tensor(f"xh{layer}", [P, KC, TM], F32R) as xh,
                  nc.sbuf_tensor(f"xl{layer}", [P, KC, TM], F32R) as xl):
                yield xh, xl

        with normed(0) as (xh, xl):
            layer_norm(nc, known, "n0", x, xh, xl, io["x"])
            dense(nc, known, "w1", xh, xl, io["w1"], GC, io["b1"], store=x1)
            attention(nc, known, "m0", xh, xl, x, io["qkv0"], io["bq0"], io["bkv0"], True)
            dense(nc, known, "o0", xh, xl, io["wo0"], KC, io["bo0"], out=x, base=io["x"])
        graph_layer(nc, known, "gl", x, dict(x1=x1, counts=graph["counts"], gate_w=io["gate_w"],
                                             gate_b=io["gate_b"]))
        with normed(1) as (xh, xl):
            layer_norm(nc, known, "n1", x, xh, xl)
            with nc.sbuf_tensor("tw", [P, TC, 8], F32) as tw:
                router(nc, known, "ro", xh, xl, io["gate"], tw)
                gated_mlp(nc, known, "ex", x, xh, xl, io["experts"], 4, experts=(8, tw))
            layer_norm(nc, known, "n2", x, xh, xl)
            dense(nc, known, "gw", xh, xl, graph["wmat"], KC, io["gnn_bias"], out=x, spill=xs)
            attention(nc, known, "m1", xh, xl, x, io["qkv1"], io["bq1"], io["bkv1"], False)
            dense(nc, known, "o1", xh, xl, io["wo1"], KC, io["bo1"], out=x, base=xs)
            layer_norm(nc, known, "n3", x, xh, xl)
            gated_mlp(nc, known, "ff", x, xh, xl, io["ffn"], 3, dtype=I32, scale=1.0 / 127.0)
        with Phase(nc, known, "fin") as p:
            st = p.new("st", 16)
            block = p.block()

            @block.sync
            def _(e):
                for k in range(KC):
                    st.mark(e.dma_start(io["out"][k], x[:, k, 0:N]), f"y{k}")
                st.wait(e, f"y{KC - 1}")


def kernel(**a):
    import numpy as _np
    import concourse.bacc as _bacc
    from concourse.bass_utils import run_bass_kernel_spmd as _run

    a = {k: _np.asarray(v) for k, v in a.items()}

    def units(w):
        i, o = w.shape
        return w.reshape(i // P, P, o // P, P).transpose(2, 1, 0, 3).reshape(o // P, P, i)

    def downs(w):
        u = units(w)
        u = u.reshape(u.shape[0] // 2, 2, P, u.shape[2]).transpose(0, 2, 1, 3).reshape(u.shape[0] // 2, P, -1)
        return _np.concatenate([u, _np.zeros(u.shape[:2] + (D - u.shape[2],), u.dtype)], 2)

    def qkv(q, k, v):
        return _np.stack([units(k.T), units(v.T), units(q.T)], 1).reshape(3 * KC, P, D)

    def mlp(w1, w3, w2):
        up = _np.stack([units(w1), units(w3)], 1)
        return _np.concatenate([up.reshape(-1, P, D), downs(w2)], 0)

    col = lambda b: b.reshape(-1, P).T
    pair = lambda k, v: _np.stack([k.reshape(KC, P), v.reshape(KC, P)], 1).reshape(KC, 2 * P)
    g = lambda n: a[n]
    ins = dict(
        x=g("x").T.reshape(KC, P, N),
        src=g("src").reshape(EP, EK), dst=g("dst").reshape(EP, EK), edge_weight=g("edge_weight").reshape(EP, EK),
        w1=units(g("L0_gnn_W1")), b1=col(g("L0_gnn_b1")),
        gate_w=g("L0_gnn_gate_w").reshape(4, 2 * NH), gate_b=g("L0_gnn_gate_b").reshape(1, -1),
        qkv0=qkv(g("L0_mix_Wq"), g("L0_mix_Wk"), g("L0_mix_Wv")), bq0=col(g("L0_mix_bq")),
        bkv0=pair(g("L0_mix_bk"), g("L0_mix_bv")), wo0=units(g("L0_mix_Wo").T), bo0=col(g("L0_mix_bo")),
        gate=g("L0_ffn_gate").reshape(KC, P, 8).transpose(1, 0, 2).reshape(P, -1),
        experts=_np.concatenate([mlp(*w) for w in zip(g("L0_ffn_experts_w1"), g("L0_ffn_experts_w3"),
                                                      g("L0_ffn_experts_w2"))], 0),
        gnn_bias=col(g("L1_gnn_bias")),
        qkv1=qkv(g("L1_mix_q_w"), g("L1_mix_k_w"), g("L1_mix_v_w")), bq1=col(g("L1_mix_q_b")),
        bkv1=pair(g("L1_mix_k_b"), g("L1_mix_v_b")), wo1=units(g("L1_mix_o_w").T), bo1=col(g("L1_mix_o_b")),
        ffn=mlp(g("L1_ffn_w_gate").T, g("L1_ffn_w_up").T, g("L1_ffn_w_down").T),
    )
    ins = {n: _np.ascontiguousarray(v) for n, v in ins.items()}
    known = {}
    for _ in range(2):
        nc = _bacc.Bacc("TRN2", target_bir_lowering=False, num_devices=1)
        io = {n: nc.dram_tensor("in_" + n, v.shape, mybir.dt.from_np(v.dtype), kind="ExternalInput").ap()
              for n, v in ins.items()}
        io["out"] = nc.dram_tensor("out_y", (KC, P, N), F32, kind="ExternalOutput").ap()
        build(nc, io, known)
    r = _run(nc, [{"in_" + n: v for n, v in ins.items()}], core_ids=[0])
    y = r.results[0]["out_y"]
    return _np.ascontiguousarray(y.reshape(D, N).T)
```

```python
from contextlib import contextmanager, ExitStack

import numpy as np
import concourse.bass as bass
from concourse import mybir

F32, F32R, I32, U32, U16, BF16 = (mybir.dt.float32, mybir.dt.float32r, mybir.dt.int32, mybir.dt.uint32,
                                  mybir.dt.uint16, mybir.dt.bfloat16)
ALU = mybir.AluOpType
ACT = mybir.ActivationFunctionType
AX = mybir.AxisListType

P = 128
N = 1250
E = 20000
D = 1024
NH = 512
KC = D // P
GC = NH // P
NT = 3
TW = 418
TM = NT * TW
TC = 10
LAST = N - (TC - 1) * P
EPS = 1e-5
EP, EK = 125, 160
NBUCK = TC * TC
HOME = 3
NST = HOME * NBUCK
NOV = 160
NCH = NST + NOV
RANK = 1 << 15
assert E // P < NOV and EP * EK == E and E < RANK and RANK * NOV < 1 << 24


def rows_of(c):
    return P if c < TC - 1 else LAST


class Loops:

    def __init__(self):
        self.active, self.counts, self.steps = {}, {}, []

    @contextmanager
    def run(self, engine, name, count):
        self.counts[name] = count
        before = [s.count for s in self.steps]
        with engine.Fori(0, count) as i:
            self.active[name] = i
            yield i
        del self.active[name]
        for s, b in zip(self.steps, before):
            s.close(name, b, count)


class Steps:

    def __init__(self, nc, ctx, loops, name, known, each=1):
        self.sem = nc.alloc_semaphore(name)
        self.loops, self.each, self.name = loops, each, name
        self.known = known.get(name, ({}, {}))
        self.count, self.at, self.slope = 0, {}, {}
        if not loops.steps:
            loops.spare = nc.alloc_semaphore(name + "_spare")
        loops.steps.append(self)

    def mark(self, instruction, step):
        assert step not in self.at, step
        instruction.then_inc(self.sem, self.each)
        self.count += self.each
        self.at[step] = (self.count, tuple(self.loops.active))
        return instruction

    def alias(self, step, of):
        self.at[step] = self.at[of]

    def start(self, engine, by):
        engine.sem_inc(self.sem, by)
        self.count = by

    def close(self, loop, before, turns):
        if self.count > before:
            self.slope[loop] = self.count - before
            self.count = before + turns * (self.count - before)

    def wait(self, engine, step, back=0):
        at, slope = self.known
        if not at:
            return
        value, around = at[step]
        for n, loop in enumerate(around):
            shift = back.get(loop, 0) if isinstance(back, dict) else back if n == len(around) - 1 else 0
            i = self.loops.active.get(loop)
            if i is None:
                value += slope[loop] * (self.loops.counts[loop] - 1 - shift)
            else:
                value -= slope[loop] * shift
        assert value >= 0, (self.name, step, value)
        assert value or not any(l in self.loops.active for l in around), (self.name, step)
        for loop in around:
            i = self.loops.active.get(loop)
            if i is not None:
                value = i * slope[loop] + value
        engine.wait_ge(self.sem, value)
        if not isinstance(value, int):
            engine.sem_inc(self.loops.spare, 1)

    def learned(self):
        return self.at, self.slope



class Weights:

    def __init__(self, nc, ctx, tag, slots, width, new, dtype=F32, scale=None):
        t = lambda n, d: ctx.enter_context(nc.sbuf_tensor(f"{tag}_{n}", [P, slots, width], d))
        self.raw, self.hi, self.lo, self.scale = t("raw", dtype), t("hi", F32R), t("lo", F32R), scale
        self.loaded = [new(f"{tag}_ld{s}", 16) for s in range(slots)]
        self.his, self.los = new(f"{tag}_hi"), new(f"{tag}_lo")

    def load(self, e, slot, src, step):
        self.loaded[slot].mark(e.dma_start(self.raw[:, slot], src), step)

    def make_hi(self, e, slot, step, back=0):
        self.loaded[slot].wait(e, step, back)
        self.his.mark(e.activation(self.hi[:, slot], self.raw[:, slot], ACT.Copy, scale=self.scale or 1.0), step)

    def make_lo(self, e, slot, step, back=0):
        self.his.wait(e, step, back)
        hi = self.hi[:, slot].bitcast(F32)
        if self.scale is None:
            i = e.tensor_tensor(self.lo[:, slot], self.raw[:, slot], hi, ALU.subtract)
        else:
            i = e.scalar_tensor_tensor(self.lo[:, slot], self.raw[:, slot], self.scale, hi, ALU.mult, ALU.subtract)
        self.los.mark(i, step)

    def blocks(self, slot, first, count):
        cut = lambda w: [w[:, slot, (first + k) * P:(first + k + 1) * P] for k in range(count)]
        return cut(self.hi), cut(self.lo)


def product(e, out, w, x):
    (wh, wl), (xh, xl) = w, x
    terms = list(zip(wl, xh)) + list(zip(wh, xl)) + list(zip(wh, xh))
    for n, (a, b) in enumerate(terms):
        i = e.matmul(out, a, b, start=n == 0, stop=n == len(terms) - 1)
    return i


class Phase:

    def __init__(self, nc, known, tag):
        self.nc, self.known, self.tag = nc, known, tag
        self.ctx, self.loops, self.got = ExitStack(), Loops(), {}
        self.loops.counts = known.setdefault(tag + "_turns", {})

    def __enter__(self):
        return self

    def __exit__(self, *a):
        self.ctx.close()
        if a[0] is None:
            self.nc.clear_and_free_semaphores([self.loops.spare] + [s.sem for s in self.got.values()])
            self.nc.all_engine_barrier()
        self.known.update({n: s.learned() for n, s in self.got.items()})

    def new(self, n, each=1):
        n = f"{self.tag}_{n}"
        s = self.got[n] = Steps(self.nc, self.ctx, self.loops, n, self.known, each)
        return s

    def sb(self, n, shape, d=F32):
        return self.ctx.enter_context(self.nc.sbuf_tensor(f"{self.tag}_{n}", shape, d))

    def banks(self, count):
        return [self.ctx.enter_context(self.nc.psum_tensor(f"{self.tag}_bank{i}", [P, 512], F32))
                for i in range(count)]

    def block(self):
        return self.ctx.enter_context(self.nc.Block())


def tile(t):
    return slice(t * TW, (t + 1) * TW)


def parts(xh, xl, t, count=KC):
    return [xh[:, k, tile(t)] for k in range(count)], [xl[:, k, tile(t)] for k in range(count)]


def layer_norm(nc, known, tag, x, xh, xl, beside=None):
    with Phase(nc, known, tag) as p:
        pl, dv, pe, ac = p.new("pool"), p.new("dve"), p.new("pe"), p.new("act")
        ones = p.sb("ones", [P, P])
        xc = p.sb("xc", [P, NT, KC, TW])
        sq = p.sb("sq", [P, 2, KC, TW])
        ve, rv, y = (p.sb(n, [P, NT, TW]) for n in ("ve", "rv", "y"))
        z = p.sb("z", [P, TW])
        HK = KC // 2
        bank = p.banks(6)
        block = p.block()

        def low(e, t, steps):
            for k in range(0, KC, HK):
                ac.wait(e, f"hi{t}{k}")
                steps.mark(e.tensor_tensor(xl[:, k:k + HK, tile(t)], xc[:, t, k:k + HK],
                                           xh[:, k:k + HK, tile(t)].bitcast(F32), ALU.subtract), f"lo{t}{k}")

        @block.gpsimd
        def _(e):
            pl.mark(e.memset(ones[:], 1.0 / D), "ones")
            if beside:
                beside(e, p)
            for t in range(NT - 1):
                low(e, t, pl)

        @block.tensor
        def _(e):
            pl.wait(e, "ones")
            for t in range(NT):
                for k in range(KC):
                    m = e.matmul(bank[t][:, 0:TW], ones[:], x[:, k, tile(t)], start=k == 0, stop=k == KC - 1)
                pe.mark(m, f"mean{t}")
            for t in range(NT):
                ac.wait(e, f"sq{t}")
                for k in range(KC):
                    m = e.matmul(bank[3 + t][:, 0:TW], ones[:], sq[:, t % 2, k], start=k == 0, stop=k == KC - 1)
                pe.mark(m, f"var{t}")

        @block.scalar
        def _(e):
            for t in range(NT):
                dv.wait(e, f"centred{t}")
                if t == 2:
                    pe.wait(e, "var0")
                ac.mark(e.activation(sq[:, t % 2], xc[:, t], ACT.Square), f"sq{t}")
            for t in range(NT):
                dv.wait(e, f"rv{t}")
                ac.mark(e.activation(y[:, t], rv[:, t], ACT.Sqrt), f"root{t}")
                for k in range(0, KC, HK):
                    dv.wait(e, f"normed{t}{k}")
                    ac.mark(e.activation(xh[:, k:k + HK, tile(t)], xc[:, t, k:k + HK], ACT.Copy), f"hi{t}{k}")

        @block.vector
        def _(e):
            pl.wait(e, "ones")
            for t in range(NT):
                pe.wait(e, f"mean{t}")
                dv.mark(e.tensor_tensor(xc[:, t], x[:, :, tile(t)],
                                        bank[t][:, 0:TW].unsqueeze(1).broadcast_to([P, KC, TW]),
                                        ALU.subtract), f"centred{t}")
            for t in range(NT):
                pe.wait(e, f"var{t}")
                e.tensor_scalar(ve[:, t], bank[3 + t][:, 0:TW], EPS, None, ALU.add)
                e.drain()
                dv.mark(e.reciprocal(rv[:, t], ve[:, t]), f"rv{t}")
                ac.wait(e, f"root{t}")
                e.tensor_tensor(z[:], y[:, t], y[:, t], ALU.mult)
                e.drain()
                e.tensor_tensor(z[:], z[:], ve[:, t], ALU.mult)
                e.drain()
                e.tensor_scalar(z[:], z[:], -0.5, 1.5, ALU.mult, ALU.add)
                e.drain()
                e.tensor_tensor(y[:, t], y[:, t], z[:], ALU.mult)
                e.drain()
                for k in range(0, KC, HK):
                    dv.mark(e.tensor_tensor(xc[:, t, k:k + HK], xc[:, t, k:k + HK],
                                            y[:, t].unsqueeze(1).broadcast_to([P, HK, TW]), ALU.mult),
                            f"normed{t}{k}")
            low(e, NT - 1, dv)


def dense(nc, known, tag, xh, xl, w_dram, units, bias_dram, out=None, store=None, base=None, spill=None,
          beside=None):
    with Phase(nc, known, tag) as p:
        w = Weights(nc, p.ctx, tag + "_w", 2, D, lambda n, each=1: p.new(n, each))
        ld, st, dv, pe, ac, pl = (p.new("ld", 16), p.new("st", 16), p.new("dve"), p.new("pe"), p.new("act"),
                                  p.new("pool"))
        bs, at = p.new("base", 16), p.new("at")
        sts = [p.new(f"st{b}", 16) for b in range(2)]
        bias = p.sb("bias", [P, units])
        to_dram = store is not None
        res = p.sb("res", [P, 2, NT, TW]) if to_dram else None
        bank = p.banks(6)
        block = p.block()
        turns = units // 2

        if beside:
            @block.gpsimd
            def _(e):
                beside(e, p)

        @block.sync
        def _(e):
            ld.mark(e.dma_start(bias[:], bias_dram, allow_slow_non_contiguous=True), "bias")
            if to_dram:
                for s in sts:
                    s.start(e, 1)
            w.load(e, 0, w_dram[0], "first")
            if base is not None:
                at.wait(e, "split")
                for k in range(KC):
                    bs.mark(e.dma_start(out[:, k, 0:N], base[k]), f"base{k}")
            with p.loops.run(e, "units", turns) as i:
                w.los.wait(e, "w1", back=1)
                w.load(e, 1, w_dram[i * 2 + 1], "w1")
                w.los.wait(e, "w0", back=1)
                w.load(e, 0, w_dram[(i * 2 + 2) % units], "w0")
                if to_dram:
                    for b in range(2):
                        for t in range(NT):
                            ac.wait(e, f"ev{b}{t}")
                        sts[b].mark(e.dma_start(store[i * 2 + b], res[:, b].rearrange("p t n -> p (t n)")), f"st{b}")
            if to_dram:
                sts[0].wait(e, "st0")
                sts[1].wait(e, "st1")
            if spill is not None:
                dv.wait(e, "ev12")
                for k in range(KC):
                    st.mark(e.dma_start(spill[k], out[:, k, 0:N]), f"spill{k}")
                st.wait(e, f"spill{KC - 1}")

        @block.scalar
        def _(e):
            if base is not None:
                for k in range(KC):
                    ac.mark(e.activation(xh[:, k], out[:, k], ACT.Copy), f"ah{k}")
            if to_dram:
                ac.start(e, 6)
            ld.wait(e, "bias")
            w.make_hi(e, 0, "first")
            with p.loops.run(e, "units", turns) as i:
                for b in range(2):
                    if b == 0:
                        pe.wait(e, "t12", back=1)
                        w.make_hi(e, 1, "w1")
                    else:
                        pe.wait(e, "t02")
                        w.make_hi(e, 0, "w0")
                    if to_dram:
                        sts[b].wait(e, f"st{b}", back=1)
                        for t in range(NT):
                            pe.wait(e, f"t{b}{t}")
                            ac.mark(e.activation(res[:, b, t], bank[3 * b + t][:, 0:TW], ACT.Identity,
                                                 bias=bias[:, bass.ds(i * 2 + b, 1)]), f"ev{b}{t}")

        @block.vector
        def _(e):
            if not to_dram:
                dv.start(e, 6)
            if base is not None:
                for k in range(KC):
                    ac.wait(e, f"ah{k}")
                    m = e.tensor_tensor(xl[:, k], out[:, k], xh[:, k].bitcast(F32), ALU.subtract)
                    at.mark(m, f"al{k}" if k < KC - 1 else "split")
            ld.wait(e, "bias")
            w.los.start(e, 1)
            w.make_lo(e, 0, "first")
            if base is not None:
                bs.wait(e, f"base{KC - 1}")
            with p.loops.run(e, "units", turns) as i:
                for b in range(2):
                    w.make_lo(e, 1 - b, f"w{1 - b}")
                    if not to_dram:
                        for t in range(NT):
                            pe.wait(e, f"t{b}{t}")
                            o = out[:, i * 2 + b, tile(t)]
                            dv.mark(e.scalar_tensor_tensor(o, bank[3 * b + t][:, 0:TW],
                                                           bias[:, bass.ds(i * 2 + b, 1)], o, ALU.add, ALU.add),
                                    f"ev{b}{t}")

        @block.tensor
        def _(e):
            pe.start(e, 1)
            if base is not None:
                at.wait(e, "split")
            with p.loops.run(e, "units", turns):
                for b in range(2):
                    w.los.wait(e, f"w{b}", back=1 - b)
                    for t in range(NT):
                        (ac if to_dram else dv).wait(e, f"ev{b}{t}", back=1)
                        m = product(e, bank[3 * b + t][:, 0:TW], w.blocks(b, 0, KC), parts(xh, xl, t))
                        pe.mark(m, f"t{b}{t}")


def graph_sort(nc, known, dram, x, x_dram, idx, pay, spill):
    with Phase(nc, known, "gs") as p:
        sb, new, ctx = p.sb, p.new, p.ctx
        ld, pl, dv, pe = new("ld", 16), new("pool"), new("dve"), new("pe")
        fill, offs, xs = new("fill", 16), new("offs", 16), new("x", 16)
        src, dst, wgt = sb("src", [EP, EK], I32), sb("dst", [EP, EK], I32), sb("wgt", [EP, EK])
        hs, hd = sb("hs", [EP, EK], I32), sb("hd", [EP, EK], I32)
        fs, fd, fhs, fhd = sb("fs", [EP, EK]), sb("fd", [EP, EK]), sb("fhs", [EP, EK]), sb("fhd", [EP, EK])
        key = sb("key", [EP, EK])
        iob = sb("iob", [P, NBUCK])
        cid = sb("cid", [P, 2])
        hot = sb("hot", [EP, NBUCK, EK], BF16)
        run = sb("run", [EP, NBUCK, EK])
        cnt = sb("cnt", [EP, NBUCK])
        tri = sb("tri", [EP, P])
        ones = sb("ones", [EP, P])
        tot, toti = sb("tot", [P, NBUCK]), sb("toti", [P, NBUCK], I32)
        nch, incl = sb("nch", [P, NBUCK]), sb("incl", [P, NBUCK])
        base = sb("base", [EP, NBUCK])
        pos, posi = sb("pos", [EP, EK]), sb("posi", [EP, EK], I32)
        ranki, obi = sb("ranki", [EP, EK], I32), sb("obi", [EP, EK], I32)
        rank, ob, over = sb("rank", [EP, EK]), sb("ob", [EP, EK]), sb("over", [EP, EK])
        lo7, hi7, idf = sb("lo7", [EP, EK], I32), sb("hi7", [EP, EK], I32), sb("idf", [EP, EK])
        empty = sb("empty", [P, NCH * 4])
        cmp = sb("cmp", [P, NBUCK])
        bk = sb("bk", [P, 2])
        bki, sbi = sb("bki", [P, 2], I32), sb("sbi", [P, 2], I32)
        bkb, far = sb("bkb", [P, 2]), sb("far", [P, 2])
        sbf, offc, offw = sb("sbf", [P, 2]), sb("offc", [P, 2]), sb("offw", [P, 2])
        off = sb("off", [P, 2, 2], I32)
        pp = ctx.enter_context(nc.psum_tensor("gs_pp", [P, NBUCK], F32))
        pt = ctx.enter_context(nc.psum_tensor("gs_pt", [P, NBUCK], F32))
        block = p.block()

        @block.sync
        def _(e):
            ld.mark(e.dma_start(src[:], dram["src"]), "src")
            ld.mark(e.dma_start(dst[:], dram["dst"]), "dst")
            ld.mark(e.dma_start(wgt[:], dram["edge_weight"]), "wgt")
            for k in range(KC):
                xs.mark(e.dma_start(x[:, k, 0:N], x_dram[k]), f"x{k}")
            pl.wait(e, "empty")
            fill.mark(e.dma_start(dram["slots"], empty[:]), "fill")
            dv.wait(e, "off")
            offs.mark(e.dma_start(dram["offs"], off[:]), "off")
            offs.wait(e, "off")
            fill.wait(e, "fill")
            xs.wait(e, f"x{KC - 1}")

        @block.gpsimd
        def _(e):
            e.iota(iob[:], [[1, NBUCK]], base=0, channel_multiplier=0, allow_small_or_imprecise_dtypes=True)
            e.iota(cid[:], [[P, 2]], base=0, channel_multiplier=1, allow_small_or_imprecise_dtypes=True)
            e.memset(ones[:], 1.0)
            e.memset(tri[:], 1.0)
            pl.mark(e.memset(empty[:], -1.0), "empty")
            pl.wait(e, "empty")
            pl.mark(e.affine_select(out=tri[:], in_=tri[:], compare_op=ALU.is_gt, fill=0.0, base=0,
                                    pattern=[[1, P]], channel_multiplier=-1), "tri")
            e.memset(x[:, :, N:TM], 0.0)

        @block.tensor
        def _(e):
            dv.wait(e, "cnt")
            pl.wait(e, "tri")
            e.matmul(pp[0:EP, :], tri[:, 0:EP], cnt[:], start=True, stop=True)
            pe.mark(e.matmul(pt[:], ones[:], cnt[:], start=True, stop=True), "sums")

        @block.vector
        def _(e):
            def d(i=None):
                e.drain()
            ld.wait(e, "wgt")
            e.tensor_scalar(hs[:], src[:], 7, None, ALU.arith_shift_right)
            e.tensor_scalar(hd[:], dst[:], 7, None, ALU.arith_shift_right)
            e.tensor_copy(fs[:], src[:])
            e.tensor_copy(fd[:], dst[:])
            d()
            e.tensor_copy(fhs[:], hs[:])
            e.tensor_copy(fhd[:], hd[:])
            d()
            e.scalar_tensor_tensor(key[:], fhs[:], float(TC), fhd[:], ALU.mult, ALU.add)
            e.scalar_tensor_tensor(pay[:, :, 0], fhs[:], -float(P), fs[:], ALU.mult, ALU.add)
            e.scalar_tensor_tensor(pay[:, :, 1], fhd[:], -float(P), fd[:], ALU.mult, ALU.add)
            e.tensor_copy(pay[:, :, 2], wgt[:])
            e.memset(pay[:, :, 3], 0.0)
            pl.wait(e, "tri")
            d()
            e.tensor_tensor(hot[:], key[:].unsqueeze(1).broadcast_to([EP, NBUCK, EK]),
                            iob[0:EP, :].unsqueeze(2).broadcast_to([EP, NBUCK, EK]), ALU.is_equal)
            d()
            flat = lambda t: t[:].rearrange("p b k -> p (b k)")
            e.tensor_tensor_scan(flat(run), flat(hot), flat(hot), 0.0, ALU.add, ALU.max)
            d()
            e.tensor_copy(cnt[:, 0:1], run[:, 0, EK - 1:EK])
            dv.mark(e.tensor_tensor(cnt[:, 1:NBUCK], run[:, 1:NBUCK, EK - 1], run[:, 0:NBUCK - 1, EK - 1],
                                    ALU.subtract), "cnt")
            pe.wait(e, "sums")
            e.tensor_scalar(tot[:], pt[:], float(HOME * P), 0.0, ALU.subtract, ALU.max)
            d()
            e.tensor_scalar(toti[:], tot[:], float(P - 1), None, ALU.add)
            d()
            e.tensor_scalar(toti[:], toti[:], 7, None, ALU.arith_shift_right)
            d()
            e.tensor_copy(nch[:], toti[:])
            d()
            e.tensor_tensor_scan(incl[:], nch[:], nch[:], 0.0, ALU.add, ALU.max)
            d()
            e.tensor_tensor(nch[:], incl[:], nch[:], ALU.subtract)
            e.tensor_copy(spill[:], incl[:, NBUCK - 1:NBUCK])
            d()
            e.scalar_tensor_tensor(base[:], nch[0:EP, :], float(RANK), pp[0:EP, :], ALU.mult, ALU.add)
            d()
            e.tensor_tensor(base[:, 1:NBUCK], base[:, 1:NBUCK], run[:, 0:NBUCK - 1, EK - 1], ALU.subtract)
            d()
            e.tensor_scalar(base[:], base[:], -1.0, None, ALU.add)
            for t in range(2):
                e.tensor_scalar(cmp[:], incl[:], cid[:, t:t + 1], 0.0, ALU.is_le, ALU.add,
                                accum_out=bk[:, t:t + 1])
                d()
            e.tensor_tensor(run[:], run[:], base[:].unsqueeze(2).broadcast_to([EP, NBUCK, EK]), ALU.add)
            d()
            e.tensor_tensor(run[:], run[:], hot[:], ALU.mult)
            e.tensor_copy(bki[:], bk[:])
            d()
            e.tensor_reduce(pos[:], run[:].rearrange("p b k -> p k b"), AX.X, ALU.add)
            d()
            e.tensor_copy(posi[:], pos[:])
            d()
            e.tensor_scalar(ranki[:], posi[:], RANK - 1, None, ALU.bitwise_and)
            e.tensor_scalar(obi[:], posi[:], 15, None, ALU.arith_shift_right)
            d()
            e.tensor_copy(rank[:], ranki[:])
            e.tensor_copy(ob[:], obi[:])
            d()
            e.tensor_scalar(over[:], rank[:], float(HOME * P), None, ALU.is_ge)
            e.scalar_tensor_tensor(pos[:], key[:], float(HOME * P), rank[:], ALU.mult, ALU.add)
            e.tensor_scalar(ob[:], ob[:], float(P), float(P * NST - HOME * P), ALU.mult, ALU.add)
            d()
            e.scalar_tensor_tensor(ob[:], key[:], -float(HOME * P), ob[:], ALU.mult, ALU.add)
            d()
            e.tensor_tensor(ob[:], ob[:], over[:], ALU.mult)
            d()
            e.tensor_tensor(posi[:], pos[:], ob[:], ALU.add)
            d()
            e.tensor_scalar(lo7[:], posi[:], P - 1, None, ALU.bitwise_and)
            e.tensor_scalar(hi7[:], posi[:], 7, None, ALU.arith_shift_right)
            d()
            e.tensor_copy(idf[:], lo7[:])
            e.tensor_copy(rank[:], hi7[:])
            d()
            e.scalar_tensor_tensor(idx[:], idf[:], float(NCH), rank[:], ALU.mult, ALU.add)
            e.tensor_scalar(bkb[:], bk[:], 103.0, None, ALU.mult)
            e.tensor_scalar(offc[:], bk[:], float(P), None, ALU.mult)
            d()
            e.tensor_copy(sbi[:], bkb[:])
            d()
            e.tensor_scalar(sbi[:], sbi[:], 10, None, ALU.arith_shift_right)
            d()
            e.tensor_copy(sbf[:], sbi[:])
            d()
            e.scalar_tensor_tensor(far[:], sbf[:], -float(TC), bk[:], ALU.mult, ALU.add)
            d()
            e.scalar_tensor_tensor(offw[:], sbf[:], float(KC), far[:], ALU.mult, ALU.add)
            d()
            e.tensor_scalar(far[:], far[:], float(KC), float(KC * KC), ALU.is_ge, ALU.mult)
            d()
            e.tensor_tensor(offw[:], offw[:], far[:], ALU.add)
            d()
            e.tensor_scalar(offw[:], offw[:], float(KC * KC), float(P), ALU.min, ALU.mult)
            d()
            e.tensor_copy(off[:, 0, :], offc[:])
            dv.mark(e.tensor_copy(off[:, 1, :], offw[:]), "off")


def scatter(e, p, dram, idx, pay, first, last):
    scat = p.new("scat", 16)
    for k in range(first, last):
        scat.mark(e.indirect_dma_start(dram["slot_rows"],
                                       bass.IndirectOffsetOnAxis(idx[:, k:k + 1].bitcast(U32), 0),
                                       pay[:, k, :], None), f"scatter{k}")
    scat.wait(e, f"scatter{last - 1}")


def graph_home(nc, known, dram):
    HD = TC // 2
    HC = HD * HOME
    NW = (HD, KC - HD)
    with Phase(nc, known, "gh") as p:
        ld, st, pl, pe, ac, ac_e = (p.new("ld", 16), p.new("st", 16), p.new("pool"), p.new("pe"),
                                    p.new("act"), p.new("ev"))
        dv = p.new("dve")
        slots = p.sb("slots", [P, NST, 4])
        whi, wlo = p.sb("whi", [P, NST], F32R), p.sb("wlo", [P, NST])
        iot = p.sb("iot", [P, P])
        hs, hd, wh, wl = (p.sb(n, [P, 2, HC, P], F32R) for n in ("hs", "hd", "wh", "wl"))
        c16 = p.sb("c16", [P, TC, TC * P], U16)
        wacc = p.sb("wacc", [P, TC, D])
        pc = [p.ctx.enter_context(nc.psum_tensor(f"gh_pc{h}", [P, 8, P], F32)) for h in range(2)]
        pw = [p.ctx.enter_context(nc.psum_tensor(f"gh_pw{h}", [P, 8, P], F32)) for h in range(2)]
        block = p.block()

        @block.sync
        def _(e):
            ld.mark(e.dma_start(slots[:], dram["slots"].rearrange("p (c f) -> p c f", f=4)[:, 0:NST]), "slots")
            ac_e.wait(e, "w1")
            st.mark(e.dma_start(dram["counts"], c16[:].rearrange("p a b -> p (a b)")), "counts")
            st.mark(e.dma_start(dram["wmat"].rearrange("m p n -> p m n"), wacc[:, 0:KC]), "wmat")
            st.wait(e, "wmat")

        @block.gpsimd
        def _(e):
            pl.mark(e.iota(iot[:], [[1, P]], base=0, channel_multiplier=0,
                           allow_small_or_imprecise_dtypes=True), "iota")

        @block.scalar
        def _(e):
            ac_e.start(e, 4)
            dv.wait(e, "wlo")
            with p.loops.run(e, "rows", TC) as i:
                for h in range(2):
                    pe.wait(e, f"w{h}", back=1)
                    dv.wait(e, f"hs{h}")
                    for u in range(NW[h] * HOME):
                        c = i * (2 * HC) + (h * HC + u)
                        a = e.activation(wh[:, h, u], hs[:, h, u].bitcast(F32), ACT.Copy,
                                         scale=whi[:, bass.ds(c, 1)].bitcast(F32))
                    ac.mark(a, f"wh{h}")
                for h in range(2):
                    pe.wait(e, f"w{h}")
                    o = c16[:, bass.ds(i, 1), h * HD * P:(h + 1) * HD * P].rearrange("p a b -> p (a b)")
                    ac_e.mark(e.activation(o, pc[h][:, 0:HD].rearrange("p a b -> p (a b)"), ACT.Copy), f"c{h}")
                    o = wacc[:, bass.ds(i, 1), h * HD * P:(h * HD + NW[h]) * P].rearrange("p a b -> p (a b)")
                    ac_e.mark(e.activation(o, pw[h][:, 0:NW[h]].rearrange("p a b -> p (a b)"), ACT.Copy), f"w{h}")

        @block.tensor
        def _(e):
            pe.start(e, 4)
            with p.loops.run(e, "rows", TC):
                for h in range(2):
                    ac_e.wait(e, f"w{h}", back=1)
                    dv.wait(e, f"wl{h}")
                    for d in range(HD):
                        for n in range(HOME):
                            u = d * HOME + n
                            e.matmul(pc[h][:, d], hs[:, h, u], hd[:, h, u], start=n == 0, stop=n == HOME - 1)
                    ac.wait(e, f"wh{h}")
                    for d in range(NW[h]):
                        for n in range(HOME):
                            u = d * HOME + n
                            e.matmul(pw[h][:, d], hd[:, h, u], wh[:, h, u], start=n == 0, stop=False)
                            m = e.matmul(pw[h][:, d], hd[:, h, u], wl[:, h, u], start=False, stop=n == HOME - 1)
                    pe.mark(m, f"w{h}")

        @block.vector
        def _(e):
            ld.wait(e, "slots")
            e.tensor_copy(whi[:], slots[:, :, 2])
            e.drain()
            dv.mark(e.tensor_tensor(wlo[:], slots[:, :, 2], whi[:].bitcast(F32), ALU.subtract), "wlo")
            pl.wait(e, "iota")
            with p.loops.run(e, "rows", TC) as i:
                for h in range(2):
                    pe.wait(e, f"w{h}", back=1)
                    cut = bass.ds(i * (2 * HC) + h * HC, HC)
                    wide = lambda t, n=HC: t.unsqueeze(2).broadcast_to([P, n, P])
                    for field, out, step in ((0, hs, "hs"), (1, hd, "hd")):
                        dv.mark(e.tensor_tensor(out[:, h], wide(slots[:, cut, field]),
                                                iot[:].unsqueeze(1).broadcast_to([P, HC, P]), ALU.is_equal),
                                f"{step}{h}")
                    e.drain()
                    n = NW[h] * HOME
                    cut = bass.ds(i * (2 * HC) + h * HC, n)
                    dv.mark(e.tensor_tensor(wl[:, h, 0:n], hs[:, h, 0:n].bitcast(F32), wide(wlo[:, cut], n),
                                            ALU.mult), f"wl{h}")


def graph_overflow(nc, known, dram, spill):
    UN = 8
    BODY = 2 * UN
    with Phase(nc, known, "gb") as p:
        sb, new, ctx, loops = p.sb, p.new, p.ctx, p.loops
        ld, pl, dv, pe, act, st = new("ld", 16), new("pool"), new("dve"), new("pe"), new("act"), new("st", 16)
        slots = sb("slots", [P, NOV, 4])
        whi, wlo = sb("whi", [P, NOV], F32R), sb("wlo", [P, NOV])
        offc, offw = sb("offc", [1, 2 * P], I32), sb("offw", [1, 2 * P], I32)
        iot = sb("iot", [P, P])
        hs = sb("hs", [P, 2, UN, P], F32R)
        hd = sb("hd", [P, 2, UN, P], F32R)
        wh = sb("wh", [P, 2, UN, P], F32R)
        wl = sb("wl", [P, 2, UN, P], F32R)
        cacc = sb("cacc", [P, (NBUCK + 1) * P])
        wacc = sb("wacc", [P, (KC * KC + 1) * P])
        c16 = sb("c16", [P, NBUCK * P], U16)
        pc = [ctx.enter_context(nc.psum_tensor(f"gb_pc{i}", [P, 4, P], F32)) for i in range(4)]
        pw = [ctx.enter_context(nc.psum_tensor(f"gb_pw{i}", [P, 4, P], F32)) for i in range(4)]
        block = p.block()

        def some(e):
            return e.If(e.value_load(spill[0:1, 0:1], min_val=0, max_val=NOV) > 0)

        @block.sync
        def _(e):
            with some(e):
                ld.mark(e.dma_start(slots[:], dram["slots"].rearrange("p (c f) -> p c f", f=4)[:, NST:]), "slots")
                ld.mark(e.dma_start(c16[:], dram["counts"]), "counts")
                ld.mark(e.dma_start(wacc[:, 0:KC * KC * P].rearrange("p (m n) -> p m n", m=KC),
                                    dram["wmat"].rearrange("m p n -> p m n")), "wmat")
                o = dram["offs"].rearrange("p (a t) -> a t p", a=2)
                ld.mark(e.dma_start(offc[:], o[0:1], allow_slow_non_contiguous=True), "offc")
                ld.mark(e.dma_start(offw[:], o[1:2], allow_slow_non_contiguous=True), "offw")
                dv.wait(e, "c16")
                st.mark(e.dma_start(dram["counts"], c16[:]), "counts")
                st.mark(e.dma_start(dram["wmat"].rearrange("m p n -> p m n"),
                                    wacc[:, 0:KC * KC * P].rearrange("p (m n) -> p m n", m=KC)), "wmat")
                st.wait(e, "wmat")

        @block.gpsimd
        def _(e):
            with some(e):
                pl.mark(e.iota(iot[:], [[1, P]], base=0, channel_multiplier=0,
                               allow_small_or_imprecise_dtypes=True), "iota")
                e.memset(cacc[:, NBUCK * P:], 0.0)
                pl.mark(e.memset(wacc[:, KC * KC * P:], 0.0), "zero")

        @block.scalar
        def _(e):
            with some(e):
                dv.wait(e, "wlo")
                with loops.run(e, "chunks", NOV // BODY) as i:
                    for h in range(2):
                        pe.wait(e, f"w{h}", back=1)
                        dv.wait(e, f"hs{h}")
                        for u in range(UN):
                            c = i * BODY + (h * UN + u)
                            e.activation(wh[:, h, u], hs[:, h, u].bitcast(F32), ACT.Copy,
                                         scale=whi[:, bass.ds(c, 1)].bitcast(F32))
                            a = e.activation(wl[:, h, u], hs[:, h, u].bitcast(F32), ACT.Copy,
                                             scale=wlo[:, bass.ds(c, 1)])
                        act.mark(a, f"wh{h}")

        @block.tensor
        def _(e):
            with some(e):
                pe.start(e, 2)
                with loops.run(e, "chunks", NOV // BODY):
                    for h in range(2):
                        dv.wait(e, f"add{h}", back=1)
                        dv.wait(e, f"hd{h}")
                        for u in range(UN):
                            e.matmul(pc[2 * h + u // 4][:, u % 4], hs[:, h, u], hd[:, h, u], start=True, stop=True)
                        act.wait(e, f"wh{h}")
                        for u in range(UN):
                            o = pw[2 * h + u // 4][:, u % 4]
                            e.matmul(o, hd[:, h, u], wh[:, h, u], start=True, stop=False)
                            m = e.matmul(o, hd[:, h, u], wl[:, h, u], start=False, stop=True)
                        pe.mark(m, f"w{h}")

        @block.vector
        def _(e):
            with some(e):
                dv.start(e, 8)
                ld.wait(e, "offw")
                e.tensor_copy(whi[:], slots[:, :, 2])
                e.drain()
                dv.mark(e.tensor_tensor(wlo[:], slots[:, :, 2], whi[:].bitcast(F32), ALU.subtract), "wlo")
                pl.wait(e, "iota")
                pl.wait(e, "zero")
                e.tensor_copy(cacc[:, 0:NBUCK * P], c16[:])

                def hot(i, h):
                    for field, out, step in ((0, hs, "hs"), (1, hd, "hd")):
                        t = slots[:, bass.ds(i * BODY + h * UN, UN), field]
                        dv.mark(e.tensor_tensor(out[:, h], t.unsqueeze(2).broadcast_to([P, UN, P]),
                                                iot[:].unsqueeze(1).broadcast_to([P, UN, P]), ALU.is_equal),
                                f"{step}{h}")

                with loops.run(e, "chunks", NOV // BODY) as i:
                    for h in range(2):
                        pe.wait(e, f"w{h}", back=1)
                        hot(i, h)
                    for h in range(2):
                        pe.wait(e, f"w{h}")
                        for u in range(UN):
                            c = i * BODY + (h * UN + u)
                            oc = e.value_load(offc[0:1, bass.ds(c, 1)], min_val=0, max_val=NBUCK * P)
                            ow = e.value_load(offw[0:1, bass.ds(c, 1)], min_val=0, max_val=KC * KC * P)
                            a, b = cacc[:, bass.ds(oc, P)], wacc[:, bass.ds(ow, P)]
                            e.tensor_tensor(a, a, pc[2 * h + u // 4][:, u % 4], ALU.add)
                            last = e.tensor_tensor(b, b, pw[2 * h + u // 4][:, u % 4], ALU.add)
                            if u < UN - 1:
                                e.drain()
                        dv.mark(last, f"add{h}")
                        e.drain()
                dv.mark(e.tensor_copy(c16[:], cacc[:, 0:NBUCK * P]), "c16")


def attention(nc, known, tag, xh, xl, at, w_dram, bq_dram, bkv_dram, softly, beside=None):
    PAIRS, W2 = KC, 2 * P
    KW = W2 + 2
    Q, K, V = 0, 1, 2
    with Phase(nc, known, tag) as p:
        w = Weights(nc, p.ctx, tag + "_w", 3, D, lambda n, each=1: p.new(n, each))
        ld, pl = p.new("ld", 16), p.new("pool")
        dv_kv, dv_q, dv_m, dv_at = p.new("dkv"), p.new("dq"), p.new("dm"), p.new("dat")
        ac_kv, ac_q, ac_m = p.new("akv"), p.new("aq"), p.new("am")
        pe_kv, pe_q, pe_m, pe_at = p.new("pkv"), p.new("pq"), p.new("pm"), p.new("pat")
        bq = p.sb("bq", [P, KC])
        bkv = p.sb("bkv", [P, W2])
        bld = p.new("bld", 16)
        mask = p.sb("mask", [P, P])
        kvf = p.sb("kvf", [P, 4, W2])
        neg = p.sb("neg", [P, 4, P])
        kvh, kvl = p.sb("kvh", [P, TC, KW], F32R), p.sb("kvl", [P, TC, KW], F32R)
        qf = p.sb("qf", [P, NT, TW])
        qn = p.sb("qn", [P, NT, TW])
        qh, ql = p.sb("qh", [P, TM], F32R), p.sb("ql", [P, TM], F32R)
        ks = p.sb("ks", [P, 1])
        mf = p.sb("mf", [P, W2])
        mh, ml = p.sb("mh", [P, W2], F32R), p.sb("ml", [P, W2], F32R)
        bank = p.banks(8)
        NUM, DEN = (7, 0, 2), (5, 1, 6)
        KVB, QB = 0, 3
        MW = W2 if softly else P
        block = p.block()

        @block.sync
        def _(e):
            ld.mark(e.dma_start(bq[:], bq_dram, allow_slow_non_contiguous=True), "bq")
            bld.mark(e.dma_start(bkv[:], bkv_dram[0:1].broadcast_to([P, W2])), "first")
            for n, s in ((2, Q), (0, K), (1, V)):
                w.load(e, s, w_dram[n], f"first{s}")
            with p.loops.run(e, "pairs", PAIRS) as j:
                for n, s in ((2, Q), (0, K), (1, V)):
                    w.los.wait(e, f"w{s}", back=1)
                    w.load(e, s, w_dram[(j * 3 + (3 + n)) % (3 * PAIRS)], f"w{s}")
                    if s == V:
                        dv_kv.wait(e, f"kv{TC - 1}")
                        bld.mark(e.dma_start(bkv[:], bkv_dram[bass.ds((j + 1) % PAIRS, 1)].broadcast_to([P, W2])),
                                 "next")
            bld.wait(e, "next")

        @block.gpsimd
        def _(e):
            for a in range(2):
                for b in range(2):
                    i = e.memset(mask[64 * a:64 * a + 64, 64 * b:64 * b + 64], 1.0 if a == b else 0.0)
                pl.mark(i, f"mask{a}")
                pl.wait(e, f"mask{a}")
            e.memset(kvh[:, :, W2:KW].bitcast(F32), 1.0)
            pl.mark(e.memset(kvl[:, :, W2:KW].bitcast(F32), 0.0), "consts")
            if beside:
                beside(e, p)

        @block.tensor
        def _(e):
            pe_m.start(e, 1)
            pe_at.start(e, 1)
            pl.wait(e, "consts")
            with p.loops.run(e, "pairs", PAIRS):
                w.los.wait(e, f"w{Q}", back=1)
                for t in range(NT):
                    if QB + t == DEN[0]:
                        dv_at.wait(e, "at0", back=1)
                    m = product(e, bank[QB + t][:, 0:TW], w.blocks(Q, 0, KC), parts(xh, xl, t))
                    pe_q.mark(m, f"q{t}")
                w.los.wait(e, f"w{V}", back=1)
                dv_at.wait(e, "at2", back=1)
                for c in range(TC):
                    r = rows_of(c)
                    if c < 3:
                        dv_kv.wait(e, f"kv{TC - 3 + c}", back=1)
                    else:
                        dv_kv.wait(e, f"kv{c - 3}")
                    tok = slice(c * P, c * P + r)
                    n = 0
                    for a, b in ((xh, w.lo), (xl, w.hi), (xh, w.hi)):
                        for k in range(KC):
                            m = e.matmul(bank[KVB + c % 3][0:r, 0:W2], a[:, k, tok],
                                         b[:, K:V + 1, k * P:(k + 1) * P], start=n == 0, stop=n == 3 * KC - 1)
                            n += 1
                    pe_kv.mark(m, f"kv{c}")
                for c in range(TC):
                    dv_kv.wait(e, f"lo{c}")
                    r = rows_of(c)
                    for n, (a, b) in enumerate(((kvl, kvh), (kvh, kvl), (kvh, kvh))):
                        m = e.matmul(bank[6][:, 0:P + 2], a[0:r, c, 0:P], b[0:r, c, P:KW],
                                     start=c == 0 and n == 0, stop=c == TC - 1 and n == 2)
                pe_m.mark(m, "m")
                dv_q.wait(e, "lo2")
                dv_m.wait(e, "lo")
                for t in range(NT):
                    for cut, b in ((slice(0, P), NUM[t]), (slice(P, W2), DEN[t]))[:2 if softly else 1]:
                        e.matmul(bank[b][:, 0:TW], ml[:, cut], qh[:, tile(t)], start=True, stop=False)
                        e.matmul(bank[b][:, 0:TW], mh[:, cut], ql[:, tile(t)], start=False, stop=False)
                        m = e.matmul(bank[b][:, 0:TW], mh[:, cut], qh[:, tile(t)], start=False, stop=True)
                    pe_at.mark(m, f"at{t}")

        @block.scalar
        def _(e):
            ac_q.start(e, 16)
            for s in (Q, K, V):
                w.make_hi(e, s, f"first{s}")
            ld.wait(e, "bq")
            with p.loops.run(e, "pairs", PAIRS) as j:
                for t in range(NT):
                    pe_q.wait(e, f"q{t}")
                    ac_q.mark(e.activation(qf[:, t], bank[QB + t][:, 0:TW], ACT.Identity if softly else ACT.Relu,
                                           bias=bq[:, bass.ds(j, 1)]), f"q{t}")
                if softly:
                    for t in range(NT):
                        dv_q.wait(e, f"neg{t}")
                        ac_q.mark(e.activation(qn[:, t], qn[:, t], ACT.Exp), f"exp{t}")
                else:
                    e.drain()
                pe_at.wait(e, "at2", back=1)
                for t in range(NT):
                    if softly:
                        dv_q.wait(e, f"map{t}")
                    ac_q.mark(e.activation(qh[:, tile(t)], qf[:, t], ACT.Copy), f"hi{t}")
                w.make_hi(e, Q, f"w{Q}")
                for s in range(TC + 1):
                    if s < TC and softly:
                        dv_kv.wait(e, f"kv{s}")
                        r = rows_of(s)
                        ac_kv.mark(e.activation(neg[0:r, s % 4], neg[0:r, s % 4], ACT.Exp), f"exp{s}")
                    if s >= 1:
                        c = s - 1
                        r = rows_of(c)
                        dv_kv.wait(e, f"map{c}")
                        if c == 0:
                            pe_m.wait(e, "m", back=1)
                        ac_kv.mark(e.activation(kvh[0:r, c, 0:W2], kvf[0:r, c % 4], ACT.Copy), f"hi{c}")
                pe_kv.wait(e, f"kv{TC - 1}")
                w.make_hi(e, K, f"w{K}")
                w.make_hi(e, V, f"w{V}")
                dv_m.wait(e, "m")
                ac_m.mark(e.activation(mh[:, 0:MW], mf[:, 0:MW], ACT.Copy), "hi")

        @block.vector
        def _(e):
            dv_kv.start(e, 64)
            dv_at.start(e, 3)
            pl.wait(e, "consts")
            for s in (Q, K, V):
                w.make_lo(e, s, f"first{s}")
            with p.loops.run(e, "pairs", PAIRS) as j:
                if softly:
                    for t in range(NT):
                        ac_q.wait(e, f"q{t}")
                        dv_q.mark(e.tensor_scalar(qn[:, t], qf[:, t], 0.0, None, ALU.min), f"neg{t}")
                    for t in range(NT):
                        ac_q.wait(e, f"exp{t}")
                        dv_q.mark(e.scalar_tensor_tensor(qf[:, t], qf[:, t], 0.0, qn[:, t], ALU.max, ALU.add),
                                  f"map{t}")
                for t in range(NT):
                    ac_q.wait(e, f"hi{t}")
                    dv_q.mark(e.tensor_tensor(ql[:, tile(t)], qf[:, t], qh[:, tile(t)].bitcast(F32),
                                              ALU.subtract), f"lo{t}")
                w.make_lo(e, Q, f"w{Q}")
                bld.wait(e, "next", back=1)
                for s in range(TC + 2):
                    if s < TC:
                        r = rows_of(s)
                        pe_kv.wait(e, f"kv{s}")
                        f = kvf[0:r, s % 4]
                        i = e.tensor_tensor(f, bank[KVB + s % 3][0:r, 0:W2], bkv[0:r], ALU.add)
                        e.drain()
                        if softly:
                            i = e.tensor_scalar(neg[0:r, s % 4], f[:, 0:P], 0.0, None, ALU.min)
                            dv_kv.mark(i, f"kv{s}")
                        else:
                            dv_kv.mark(e.tensor_scalar(f[:, 0:P], f[:, 0:P], 0.0, None, ALU.max), f"kv{s}")
                    if 1 <= s <= TC:
                        c = s - 1
                        r = rows_of(c)
                        f = kvf[0:r, c % 4]
                        if softly:
                            ac_kv.wait(e, f"exp{c}")
                            dv_kv.mark(e.scalar_tensor_tensor(f[:, 0:P], f[:, 0:P], 0.0, neg[0:r, c % 4],
                                                              ALU.max, ALU.add), f"map{c}")
                        else:
                            dv_kv.alias(f"map{c}", f"kv{c}")
                    if s >= 2:
                        c = s - 2
                        r = rows_of(c)
                        ac_kv.wait(e, f"hi{c}")
                        dv_kv.mark(e.tensor_tensor(kvl[0:r, c, 0:W2], kvf[0:r, c % 4],
                                                   kvh[0:r, c, 0:W2].bitcast(F32), ALU.subtract), f"lo{c}")
                w.make_lo(e, K, f"w{K}")
                w.make_lo(e, V, f"w{V}")
                pe_m.wait(e, "m")
                if softly:
                    e.tensor_copy(ks[:], bank[6][:, P:P + 1])
                    e.drain()
                    e.tensor_scalar(mf[:, P:W2], mask[:], ks[:, 0:1], None, ALU.mult)
                dv_m.mark(e.tensor_tensor(mf[:, 0:P], bank[6][:, 0:P], mask[:], ALU.mult), "m")
                ac_m.wait(e, "hi")
                dv_m.mark(e.tensor_tensor(ml[:, 0:MW], mf[:, 0:MW], mh[:, 0:MW].bitcast(F32), ALU.subtract), "lo")
                for t in range(NT):
                    pe_at.wait(e, f"at{t}")
                    o = at[:, bass.ds(j, 1), tile(t)].rearrange("p a b -> p (a b)")
                    if softly:
                        e.tensor_scalar(qn[:, t], bank[DEN[t]][:, 0:TW], 1e-6, None, ALU.add)
                        e.drain()
                        e.reciprocal(qn[:, t], qn[:, t])
                        e.drain()
                        i = e.tensor_tensor(o, bank[NUM[t]][:, 0:TW], qn[:, t], ALU.mult)
                    else:
                        i = e.tensor_copy(o, bank[NUM[t]][:, 0:TW])
                    dv_at.mark(i, f"at{t}")
                e.drain()


def graph_layer(nc, known, tag, x, dram):
    HOPS, HALF = 4, TC // 2
    HWID = (HALF * P, N - HALF * P)
    with Phase(nc, known, tag) as p:
        ld, pl = p.new("ld", 16), p.new("pool")
        x1s = p.new("x1", 16)
        pe_t, dv_t = p.new("pt"), p.new("dt")
        pe_s, dv_s, ac_s = p.new("ps"), p.new("ds"), p.new("as")
        pe_g, dv_g, dv_o, ac_g = p.new("pg"), p.new("dg"), p.new("do"), p.new("ag")
        dv_f, ac_f = p.new("df"), p.new("af")
        dv_a, ac_a, pe_a = p.new("da"), p.new("aa"), p.new("pa")
        x1 = p.sb("x1", [P, GC, TM])
        cnt = p.sb("cnt", [P, TC, TC * P], U16)
        g = p.sb("g", [P, TC, NH])
        gf = p.sb("gf", [P, 4, NH])
        gh, gl = p.sb("gh", [P, TC, NH], F32R), p.sb("gl", [P, TC, NH], F32R)
        gw = p.sb("gw", [P, 2, NH])
        dump = p.sb("dump", [P, HALF, NH], BF16)
        gld = p.new("gld", 16)
        gb = p.sb("gb", [P, HOPS])
        ident, ones = p.sb("ident", [P, P]), p.sb("ones", [P, P])
        deg, rdeg, dis, z = (p.sb(n, [P, TC]) for n in ("deg", "rdeg", "dis", "z"))
        ga, gs, gsb = p.sb("ga", [P, TC]), p.sb("gs", [P, TC]), p.sb("gsb", [P, TC])
        diag = p.sb("diag", [P, TC, P])
        ab = p.sb("ab", [P, TM])
        th = p.sb("th", [P, 2, HALF * P])
        af = p.sb("af", [P, 4, HALF * P])
        ah, al = p.sb("ah", [P, 2, HALF * P], F32R), p.sb("al", [P, 2, HALF * P], F32R)
        bank = p.banks(8)
        block = p.block()
        BANKS = ((0, 1, 2, 3, 4), (5, 6, 7, 0, 1))
        cols = lambda h: slice(h * HALF * P, h * HALF * P + HWID[h])

        @block.sync
        def _(e):
            x1s.mark(e.dma_start(x1[:], dram["x1"].rearrange("m p n -> p m n")), "x1")
            ld.mark(e.dma_start(cnt[:].rearrange("p a b -> p (a b)"), dram["counts"]), "cnt")
            ld.mark(e.dma_start(gb[:], dram["gate_b"].broadcast_to([P, HOPS])), "gb")
            gwf = gw[:].rearrange("p b c -> p (b c)")
            gld.mark(e.dma_start(gwf, dram["gate_w"][0:1].broadcast_to([P, 2 * NH])), "first")
            with p.loops.run(e, "hops", HOPS) as k:
                dv_g.wait(e, "gs", back=1)
                gld.mark(e.dma_start(gwf, dram["gate_w"][bass.ds((k + 1) % HOPS, 1)].broadcast_to([P, 2 * NH])),
                         "next")
            gld.wait(e, "next")

        @block.gpsimd
        def _(e):
            e.memset(ones[:], 1.0)
            e.memset(ga[:], 0.0)
            e.memset(gs[:], 0.0)
            e.memset(g[:, TC - 1], 0.0)
            e.memset(ab[:, N:TM], 0.0)
            pl.mark(e.memset(ident[:], 1.0), "one")
            pl.wait(e, "one")
            pl.mark(e.affine_select(out=ident[:], in_=ident[:], compare_op=ALU.is_equal, fill=0.0, base=0,
                                    pattern=[[1, P]], channel_multiplier=-1), "ident")

        GROUPS = [(m, c, min(c + 4, TC)) for m in range(GC) for c in (0, 4, 8)]
        width = lambda a, b: sum(rows_of(c) for c in range(a, b))

        @block.tensor
        def _(e):
            pe_a.start(e, 2)
            pl.wait(e, "ident")
            x1s.wait(e, "x1")
            for c in range(TC):
                r = rows_of(c)
                if c >= 4:
                    dv_t.wait(e, f"g{c - 4}")
                for m in range(GC):
                    i = e.transpose(bank[c % 4][0:r, m * P:(m + 1) * P], x1[:, m, c * P:c * P + r], ident[:])
                pe_t.mark(i, f"t{c}")
            dv_s.wait(e, "sum")
            for t in range(NT):
                m = e.matmul(bank[4 + t][:, 0:TW], ones[:], ab[:, tile(t)], start=True, stop=True)
            pe_s.mark(m, "row")
            dv_s.wait(e, "row")
            for c in range(TC):
                r = rows_of(c)
                m = e.matmul(bank[7][0:r, c:c + 1], ab[0:1, c * P:c * P + r], ones[0:1, 0:1], start=True, stop=True)
            pe_s.mark(m, "deg")
            with p.loops.run(e, "hops", HOPS):
                dv_g.wait(e, "diag", back=1)
                dv_o.wait(e, "out1", back=1)
                for t in range(NT):
                    m = e.matmul(bank[5 + t][:, 0:TW], ones[:], diag[:].rearrange("p a b -> p (a b)")[:, tile(t)],
                                 start=True, stop=True)
                pe_g.mark(m, "ab")
                for h in range(2):
                    for c in range(TC):
                        r = rows_of(c)
                        dv_a.wait(e, f"al{h}{c}")
                        if c == 0 and h == 1:
                            ac_g.wait(e, "ab")
                            dv_o.wait(e, "out0")
                        for d in range(HALF):
                            q = rows_of(h * HALF + d)
                            cut = slice(d * P, d * P + q)
                            o = bank[BANKS[h][d]][0:q, :]
                            e.matmul(o, al[0:r, c % 2, cut], gh[0:r, c], start=c == 0, stop=False)
                            e.matmul(o, ah[0:r, c % 2, cut], gl[0:r, c], start=False, stop=False)
                            m = e.matmul(o, ah[0:r, c % 2, cut], gh[0:r, c], start=False, stop=c == TC - 1)
                        pe_a.mark(m, f"a{h}{c}")
            dv_o.wait(e, "out1")
            for n, (m, a, b) in enumerate(GROUPS):
                if n >= 8:
                    dv_t.wait(e, f"x{n - 8}")
                for c in range(a, b):
                    r, at = rows_of(c), (c - a) * P
                    i = e.transpose(bank[n % 8][:, at:at + r], g[0:r, c, m * P:(m + 1) * P], ident[0:r, 0:r])
                pe_t.mark(i, f"b{n}")

        @block.scalar
        def _(e):
            dv_s.wait(e, "rdeg")
            ac_s.mark(e.activation(dis[:], rdeg[:], ACT.Sqrt), "root")
            with p.loops.run(e, "hops", HOPS):
                pe_g.wait(e, "ab")
                for t in range(NT):
                    i = e.activation(ab[:, tile(t)], bank[5 + t][:, 0:TW], ACT.Copy)
                ac_g.mark(i, "ab")
                e.drain()
                dv_g.wait(e, "gs", back=1)
                for h in range(2):
                    for s in range(TC + 1):
                        if s < TC:
                            r, b = rows_of(s), s % 2
                            if s >= 2:
                                dv_a.wait(e, f"af{h}{s - 2}")
                            ac_a.mark(e.activation(th[0:r, b, 0:HWID[h]], ab[0:r, cols(h)], ACT.Tanh,
                                                   bias=gsb[0:r, s:s + 1]), f"th{h}{s}")
                            if h == 0:
                                dv_f.wait(e, f"gf{s}")
                                ac_f.mark(e.activation(gh[0:r, s], gf[0:r, s % 4], ACT.Copy), f"gh{s}")
                        if s >= 1:
                            c = s - 1
                            r, b = rows_of(c), c % 2
                            dv_a.wait(e, f"af{h}{c}")
                            if c >= 2:
                                pe_a.wait(e, f"a{h}{c - 2}")
                            elif h == 1:
                                pe_a.wait(e, f"a0{TC - 2 + c}")
                            else:
                                pe_a.wait(e, f"a1{TC - 2 + c}", back=1)
                            ac_a.mark(e.activation(ah[0:r, b, 0:HWID[h]], af[0:r, c % 4, 0:HWID[h]], ACT.Copy),
                                      f"ah{h}{c}")

        @block.vector
        def _(e):
            dv_o.start(e, 2)
            dv_a.start(e, 1)
            pl.wait(e, "ident")
            for c in range(TC):
                pe_t.wait(e, f"t{c}")
                r = rows_of(c)
                dv_t.mark(e.tensor_copy(g[0:r, c], bank[c % 4][0:r, :]), f"g{c}")
            ld.wait(e, "gb")
            dv_s.mark(e.tensor_reduce(ab[:, 0:N], cnt[:, :, 0:N].rearrange("p c n -> p n c"), AX.X, ALU.add), "sum")
            e.tensor_tensor(x[:, 0:GC], x[:, 0:GC], x1[:], ALU.add)
            pe_s.wait(e, "row")
            for t in range(NT):
                i = e.tensor_copy(ab[0:1, tile(t)], bank[4 + t][0:1, 0:TW])
            dv_s.mark(i, "row")
            e.memset(deg[:], 1.0)
            pe_s.wait(e, "deg")
            e.drain()
            e.tensor_scalar(deg[:, 0:TC - 1], bank[7][:, 0:TC - 1], 1.0, None, ALU.max)
            e.tensor_scalar(deg[0:LAST, TC - 1:TC], bank[7][0:LAST, TC - 1:TC], 1.0, None, ALU.max)
            e.drain()
            dv_s.mark(e.reciprocal(rdeg[:], deg[:]), "rdeg")
            ac_s.wait(e, "root")
            e.tensor_tensor(z[:], dis[:], dis[:], ALU.mult)
            e.drain()
            e.tensor_tensor(z[:], z[:], deg[:], ALU.mult)
            e.drain()
            e.tensor_scalar(z[:], z[:], -0.5, 1.5, ALU.mult, ALU.add)
            e.drain()
            e.tensor_tensor(dis[:], dis[:], z[:], ALU.mult)
            e.drain()

            def dots(out, w, first, last):
                for c in range(first, last):
                    r = rows_of(c)
                    e.tensor_tensor_reduce(dump[0:r, c % HALF], g[0:r, c], gw[0:r, w],
                                           1.0, 0.0, ALU.mult, ALU.add, out[0:r, c:c + 1])

            def spread(first, last):
                n = last - first
                return e.tensor_tensor(diag[:, first:last], ident[:].unsqueeze(1).broadcast_to([P, n, P]),
                                       ga[:, first:last].unsqueeze(2).broadcast_to([P, n, P]), ALU.mult)

            def second_half(k, steps):
                dots(ga, 0, HALF, TC)
                e.drain()
                dv_g.mark(spread(HALF, TC), steps[0])
                dots(gs, 1, HALF, TC)
                e.drain()
                dv_g.mark(e.tensor_scalar(gsb[:], gs[:], gb[:, k], None, ALU.add), steps[1])

            gld.wait(e, "first")
            dots(ga, 0, 0, HALF)
            e.drain()
            dots(gs, 1, 0, HALF)
            e.drain()
            spread(0, HALF)
            e.drain()
            second_half(slice(0, 1), ("diag0", "gs0"))
            with p.loops.run(e, "hops", HOPS) as k:
                for h in range(2):
                    for s in range(TC + 1):
                        if s < TC:
                            r, b = rows_of(s), s % 2
                            if h == 0:
                                dv_f.mark(e.tensor_scalar(gf[0:r, s % 4], g[0:r, s], dis[0:r, s:s + 1], None,
                                                          ALU.mult), f"gf{s}")
                            ac_a.wait(e, f"th{h}{s}")
                            dv_a.mark(e.tensor_tensor(af[0:r, s % 4, 0:HWID[h]], th[0:r, b, 0:HWID[h]],
                                                      cnt[0:r, s, cols(h)], ALU.mult), f"af{h}{s}")
                        if s >= 1:
                            c = s - 1
                            r, b = rows_of(c), c % 2
                            if h == 0:
                                ac_f.wait(e, f"gh{c}")
                                e.tensor_tensor(gl[0:r, c], gf[0:r, c % 4], gh[0:r, c].bitcast(F32), ALU.subtract)
                            ac_a.wait(e, f"ah{h}{c}")
                            dv_a.mark(e.tensor_tensor(al[0:r, b, 0:HWID[h]], af[0:r, c % 4, 0:HWID[h]],
                                                      ah[0:r, b, 0:HWID[h]].bitcast(F32), ALU.subtract),
                                      f"al{h}{c}")
                    if h == 0:
                        gld.wait(e, "next")
                    pe_a.wait(e, f"a{h}{TC - 1}")
                    for d in range(HALF):
                        c = h * HALF + d
                        q = rows_of(c)
                        i = e.scalar_tensor_tensor(g[0:q, c], bank[BANKS[h][d]][0:q, :], dis[0:q, c:c + 1],
                                                   g[0:q, c], ALU.mult, ALU.add)
                    dv_o.mark(i, f"out{h}")
                    e.drain()
                    if h == 0:
                        dots(ga, 0, 0, HALF)
                        e.drain()
                        dots(gs, 1, 0, HALF)
                        e.drain()
                        spread(0, HALF)
                    else:
                        second_half(bass.ds((k + 1) % HOPS, 1), ("diag", "gs"))
            for n, (m, a, b) in enumerate(GROUPS):
                pe_t.wait(e, f"b{n}")
                w = width(a, b)
                o = x[:, GC + m, a * P:a * P + w]
                dv_t.mark(e.tensor_tensor(o, o, bank[n % 8][:, 0:w], ALU.add), f"x{n}")


def router(nc, known, tag, xh, xl, gate_dram, tw):
    EX = 8
    with Phase(nc, known, tag) as p:
        ld, pl, dv, pe, ac = p.new("ld", 16), p.new("pool"), p.new("dve"), p.new("pe"), p.new("act")
        gr = p.sb("gr", [P, KC, EX])
        gh, gl = p.sb("gh", [P, KC, EX], F32R), p.sb("gl", [P, KC, EX], F32R)
        lg, top = p.sb("lg", [P, TC, EX]), p.sb("top", [P, TC, EX])
        at = p.sb("at", [P, TC, EX], U32)
        af = p.sb("af", [P, TC, EX])
        io = p.sb("io", [P, EX])
        df, ex, w1, w2 = (p.sb(n, [P, TC]) for n in ("df", "ex", "w1", "w2"))
        hot = p.sb("hot", [P, TC, EX])
        row = p.sb("row", [EX, TM])
        ident = p.sb("ident", [EX, EX])
        bank = p.banks(4)
        block = p.block()

        @block.sync
        def _(e):
            ld.mark(e.dma_start(gr[:].rearrange("p a b -> p (a b)"), gate_dram), "gate")

        @block.gpsimd
        def _(e):
            e.memset(lg[:], 0.0)
            pl.mark(e.memset(ident[:], 1.0), "one")
            pl.wait(e, "one")
            e.affine_select(out=ident[:], in_=ident[:], compare_op=ALU.is_equal, fill=0.0, base=0,
                            pattern=[[1, EX]], channel_multiplier=-1)
            pl.mark(e.iota(io[:], [[1, EX]], base=0, channel_multiplier=0, allow_small_or_imprecise_dtypes=True),
                    "iota")

        @block.scalar
        def _(e):
            dv.wait(e, "df")
            ac.mark(e.activation(ex[:], df[:], ACT.Exp), "exp")

        @block.tensor
        def _(e):
            w = lambda g: [g[:, k] for k in range(KC)]
            dv.wait(e, "gate")
            for t in range(NT):
                m = product(e, bank[t][0:EX, 0:TW], (w(gh), w(gl)), parts(xh, xl, t))
                pe.mark(m, f"row{t}")
            pl.wait(e, "iota")
            for c in range(TC):
                if c in (0, 3, 6):
                    dv.wait(e, f"row{c // 3}")
                r = rows_of(c)
                m = e.transpose(bank[3][0:r, c * EX:(c + 1) * EX], row[:, c * P:c * P + r], ident[:])
            pe.mark(m, "logits")

        @block.vector
        def _(e):
            ld.wait(e, "gate")
            e.tensor_copy(gh[:], gr[:])
            e.drain()
            dv.mark(e.tensor_tensor(gl[:], gr[:], gh[:].bitcast(F32), ALU.subtract), "gate")
            pl.wait(e, "iota")
            for t in range(NT):
                pe.wait(e, f"row{t}")
                dv.mark(e.tensor_copy(row[:, tile(t)], bank[t][0:EX, 0:TW]), f"row{t}")
            pe.wait(e, "logits")
            b = bank[3][:, 0:TC * EX].rearrange("p (c x) -> p c x", x=EX)
            e.tensor_copy(lg[:, 0:TC - 1], b[:, 0:TC - 1])
            e.tensor_copy(lg[0:LAST, TC - 1], b[0:LAST, TC - 1])
            e.drain()
            for c in range(TC):
                e.max(top[:, c], lg[:, c])
            e.drain()
            for c in range(TC):
                e.max_index(at[:, c], top[:, c], lg[:, c])
            dv.mark(e.tensor_tensor(df[:], top[:, :, 1], top[:, :, 0], ALU.subtract), "df")
            e.drain()
            e.tensor_copy(af[:], at[:])
            ac.wait(e, "exp")
            e.tensor_scalar(w2[:], ex[:], 1.0, None, ALU.add)
            e.drain()
            e.reciprocal(w1[:], w2[:])
            e.drain()
            e.tensor_tensor(w2[:], w1[:], ex[:], ALU.mult)
            wide = lambda t: t.unsqueeze(2).broadcast_to([P, TC, EX])
            iow = io[:].unsqueeze(1).broadcast_to([P, TC, EX])
            e.tensor_tensor(hot[:], wide(af[:, :, 0]), iow, ALU.is_equal)
            e.drain()
            e.tensor_tensor(tw[:], hot[:], wide(w1[:]), ALU.mult)
            e.drain()
            e.tensor_tensor(hot[:], wide(af[:, :, 1]), iow, ALU.is_equal)
            e.drain()
            e.tensor_tensor(hot[:], hot[:], wide(w2[:]), ALU.mult)
            e.drain()
            e.tensor_tensor(tw[:], tw[:], hot[:], ALU.add)


def gated_mlp(nc, known, tag, x, xh, xl, w_dram, hc, experts=None, dtype=F32, scale=None):
    count, tw = experts or (1, None)
    with Phase(nc, known, tag) as p:
        w = Weights(nc, p.ctx, tag + "_w", 2, D, lambda n, each=1: p.new(n, each), dtype, scale)
        pl, pe, pe_wb, dv, dv_d, ac, ac_wb = (p.new(n) for n in ("pool", "pe", "pwb", "dve", "dd", "act", "awb"))
        hh, hl = p.sb("hh", [P, hc, TM], F32R), p.sb("hl", [P, hc, TM], F32R)
        sg, hf = p.sb("sg", [P, NT, TW]), p.sb("hf", [P, NT, TW])
        if tw is not None:
            wb = p.sb("wb", [P, TM])
            ident, ones = p.sb("ident", [P, P]), p.sb("ones", [P, P])
            diag = p.sb("diag", [P, TC, P])
        bank = p.banks(8)
        block = p.block()
        downs = KC // 4
        per = 2 * hc + 2 * downs
        total = count * per
        flat = lambda ap: ap.rearrange("p a b -> p (a b)")

        @block.sync
        def _(e):
            w.load(e, 0, w_dram[0], "first")
            with p.loops.run(e, "experts", count) as x_:
                for kind, at, turns in (("u", 0, hc), ("d", 2 * hc, downs)):
                    with p.loops.run(e, kind, turns) as i:
                        w.los.wait(e, kind + "1", back=1)
                        w.load(e, 1, w_dram[x_ * per + i * 2 + (at + 1)], kind + "1")
                        w.los.wait(e, kind + "0", back=1)
                        w.load(e, 0, w_dram[(x_ * per + i * 2 + (at + 2)) % total], kind + "0")

        @block.gpsimd
        def _(e):
            if tw is not None:
                e.memset(ones[:], 1.0)
                pl.mark(e.memset(ident[:], 1.0), "one")
                pl.wait(e, "one")
                pl.mark(e.affine_select(out=ident[:], in_=ident[:], compare_op=ALU.is_equal, fill=0.0, base=0,
                                        pattern=[[1, P]], channel_multiplier=-1), "ident")

        @block.tensor
        def _(e):
            def spread(name):
                dv_d.wait(e, "diag" + name)
                for t in range(NT):
                    if t == 2:
                        ac_wb.wait(e, f"wb0{name}")
                    pe_wb.mark(e.matmul(bank[6 + t % 2][:, 0:TW], ones[:], flat(diag[:])[:, tile(t)],
                                        start=True, stop=True), f"wb{t}{name}")

            pe.start(e, 1)
            if tw is not None:
                spread("first")
            with p.loops.run(e, "experts", count):
                with p.loops.run(e, "u", hc):
                    w.los.wait(e, "u0", back=1)
                    for t in range(NT):
                        ac.wait(e, f"sg{t}", back=1)
                        dv.wait(e, f"x10{t}", back={"experts": 1})
                        m = product(e, bank[t][:, 0:TW], w.blocks(0, 0, KC), parts(xh, xl, t))
                        pe.mark(m, f"g{t}")
                    w.los.wait(e, "u1")
                    for t in range(NT):
                        dv.wait(e, f"h{t}", back=1)
                        dv.wait(e, f"x11{t}", back={"experts": 1})
                        m = product(e, bank[3 + t][:, 0:TW], w.blocks(1, 0, KC), parts(xh, xl, t))
                        pe.mark(m, f"u{t}")
                with p.loops.run(e, "d", downs):
                    for b in range(2):
                        w.los.wait(e, f"d{b}", back=1 - b)
                        for r in range(2):
                            for t in range(NT):
                                if b == 0 and r == 0:
                                    dv.wait(e, f"lo{t}")
                                dv.wait(e, f"x{1 - b}{r}{t}", back=1 - b)
                                m = product(e, bank[3 * r + t][:, 0:TW], w.blocks(b, r * hc, hc),
                                            parts(hh, hl, t, hc))
                                pe.mark(m, f"d{b}{r}{t}")
                if tw is not None:
                    spread("")

        @block.scalar
        def _(e):
            def spread(name):
                for t in range(NT):
                    pe_wb.wait(e, f"wb{t}{name}")
                    ac_wb.mark(e.activation(wb[:, tile(t)], bank[6 + t % 2][:, 0:TW], ACT.Copy), f"wb{t}{name}")

            ac.start(e, 6)
            w.make_hi(e, 0, "first")
            if tw is not None:
                spread("first")
            with p.loops.run(e, "experts", count):
                with p.loops.run(e, "u", hc) as i:
                    pe.wait(e, "u2", back=1)
                    w.make_hi(e, 1, "u1")
                    for t in range(NT):
                        pe.wait(e, f"g{t}")
                        dv.wait(e, f"h{t}", back=1)
                        ac.mark(e.activation(sg[:, t], bank[t][:, 0:TW], ACT.Silu), f"sg{t}")
                    w.make_hi(e, 0, "u0")
                    for t in range(NT):
                        dv.wait(e, f"h{t}")
                        ac.mark(e.activation(flat(hh[:, bass.ds(i, 1), tile(t)]), hf[:, t], ACT.Copy), f"hh{t}")
                with p.loops.run(e, "d", downs):
                    pe.wait(e, "d112", back=1)
                    w.make_hi(e, 1, "d1")
                    pe.wait(e, "d012")
                    w.make_hi(e, 0, "d0")
                if tw is not None:
                    spread("")

        @block.vector
        def _(e):
            def spread(expert, name):
                col = tw[:, :, expert].broadcast_to([P, TC, P])
                dv_d.mark(e.tensor_tensor(diag[:], ident[:].unsqueeze(1).broadcast_to([P, TC, P]), col,
                                          ALU.mult), "diag" + name)

            dv.start(e, 12)
            w.los.start(e, 1)
            if tw is not None:
                pl.wait(e, "ident")
                spread(slice(0, 1), "first")
            w.make_lo(e, 0, "first")
            with p.loops.run(e, "experts", count) as x_:
                if tw is not None:
                    ac_wb.wait(e, "wb2", back=1)
                with p.loops.run(e, "u", hc) as i:
                    w.make_lo(e, 1, "u1")
                    if tw is not None:
                        for t in range(NT):
                            ac.wait(e, f"sg{t}")
                            e.tensor_tensor(sg[:, t], sg[:, t], wb[:, tile(t)], ALU.mult)
                    w.make_lo(e, 0, "u0")
                    e.drain()
                    for t in range(NT + 1):
                        if t < NT:
                            pe.wait(e, f"u{t}")
                            ac.wait(e, f"sg{t}")
                            dv.mark(e.tensor_tensor(hf[:, t], sg[:, t], bank[3 + t][:, 0:TW], ALU.mult), f"h{t}")
                        if t:
                            ac.wait(e, f"hh{t - 1}")
                            dv.mark(e.tensor_tensor(flat(hl[:, bass.ds(i, 1), tile(t - 1)]), hf[:, t - 1],
                                                    flat(hh[:, bass.ds(i, 1), tile(t - 1)]).bitcast(F32),
                                                    ALU.subtract), f"lo{t - 1}")
                if tw is not None:
                    spread(bass.ds((x_ + 1) % count, 1), "")
                with p.loops.run(e, "d", downs) as i:
                    for b in range(2):
                        w.make_lo(e, 1 - b, f"d{1 - b}")
                        for r in range(2):
                            for t in range(NT):
                                pe.wait(e, f"d{b}{r}{t}")
                                o = flat(x[:, bass.ds(i * 4 + (2 * b + r), 1), tile(t)])
                                dv.mark(e.tensor_tensor(o, o, bank[3 * r + t][:, 0:TW], ALU.add), f"x{b}{r}{t}")


def build(nc, io, known):
    dram = lambda n, shape, d=F32: nc.dram_tensor("scratch_" + n, shape, d).ap()
    slots = dram("slots", (P, NCH * 4))
    graph = dict(src=io["src"], dst=io["dst"], edge_weight=io["edge_weight"], slots=slots,
                 slot_rows=slots.rearrange("p (c f) -> (p c) f", f=4), offs=dram("offs", (P, 4), I32),
                 counts=dram("counts", (P, NBUCK * P), U16), wmat=dram("wmat", (KC, P, D)))
    x1 = dram("x1", (GC, P, TM))
    xs = dram("xs", (KC, P, N))
    with ExitStack() as ctx:
        x = ctx.enter_context(nc.sbuf_tensor("x", [P, KC, TM], F32))
        idx, pay = (nc.sbuf_tensor("idx", [EP, EK], I32), nc.sbuf_tensor("pay", [EP, EK, 4], F32))
        idx, pay = ctx.enter_context(idx), ctx.enter_context(pay)
        spill = ctx.enter_context(nc.sbuf_tensor("spill", [P, 1], I32))
        third = lambda n: lambda e, p: scatter(e, p, graph, idx, pay, *((0, 35), (35, 90), (90, EK))[n])

        @contextmanager
        def normed(layer):
            with (nc.sbuf_tensor(f"xh{layer}", [P, KC, TM], F32R) as xh,
                  nc.sbuf_tensor(f"xl{layer}", [P, KC, TM], F32R) as xl):
                yield xh, xl

        graph_sort(nc, known, graph, x, io["x"], idx, pay, spill)
        with normed(0) as (xh, xl):
            layer_norm(nc, known, "n0", x, xh, xl, third(0))
            dense(nc, known, "w1", xh, xl, io["w1"], GC, io["b1"], store=x1,
                  beside=third(1))
            attention(nc, known, "m0", xh, xl, x, io["qkv0"], io["bq0"], io["bkv0"], True, third(2))
            dense(nc, known, "o0", xh, xl, io["wo0"], KC, io["bo0"], out=x, base=io["x"])
        graph_home(nc, known, graph)
        graph_overflow(nc, known, graph, spill)
        graph_layer(nc, known, "gl", x, dict(x1=x1, counts=graph["counts"], gate_w=io["gate_w"],
                                             gate_b=io["gate_b"]))
        with normed(1) as (xh, xl):
            layer_norm(nc, known, "n1", x, xh, xl)
            with nc.sbuf_tensor("tw", [P, TC, 8], F32) as tw:
                router(nc, known, "ro", xh, xl, io["gate"], tw)
                gated_mlp(nc, known, "ex", x, xh, xl, io["experts"], 4, experts=(8, tw))
            layer_norm(nc, known, "n2", x, xh, xl)
            dense(nc, known, "gw", xh, xl, graph["wmat"], KC, io["gnn_bias"], out=x, spill=xs)
            attention(nc, known, "m1", xh, xl, x, io["qkv1"], io["bq1"], io["bkv1"], False)
            dense(nc, known, "o1", xh, xl, io["wo1"], KC, io["bo1"], out=x, base=xs)
            layer_norm(nc, known, "n3", x, xh, xl)
            gated_mlp(nc, known, "ff", x, xh, xl, io["ffn"], 3, dtype=I32, scale=1.0 / 127.0)
        with Phase(nc, known, "fin") as p:
            st = p.new("st", 16)
            block = p.block()

            @block.sync
            def _(e):
                for k in range(KC):
                    st.mark(e.dma_start(io["out"][k], x[:, k, 0:N]), f"y{k}")
                st.wait(e, f"y{KC - 1}")


def kernel(**a):
    import numpy as _np
    import concourse.bacc as _bacc
    from concourse.bass_utils import run_bass_kernel_spmd as _run

    a = {k: _np.asarray(v) for k, v in a.items()}

    def units(w):
        i, o = w.shape
        return w.reshape(i // P, P, o // P, P).transpose(2, 1, 0, 3).reshape(o // P, P, i)

    def downs(w):
        u = units(w)
        u = u.reshape(u.shape[0] // 2, 2, P, u.shape[2]).transpose(0, 2, 1, 3).reshape(u.shape[0] // 2, P, -1)
        return _np.concatenate([u, _np.zeros(u.shape[:2] + (D - u.shape[2],), u.dtype)], 2)

    def qkv(q, k, v):
        return _np.stack([units(k.T), units(v.T), units(q.T)], 1).reshape(3 * KC, P, D)

    def mlp(w1, w3, w2):
        up = _np.stack([units(w1), units(w3)], 1)
        return _np.concatenate([up.reshape(-1, P, D), downs(w2)], 0)

    col = lambda b: b.reshape(-1, P).T
    pair = lambda k, v: _np.stack([k.reshape(KC, P), v.reshape(KC, P)], 1).reshape(KC, 2 * P)
    g = lambda n: a[n]
    ins = dict(
        x=g("x").T.reshape(KC, P, N),
        src=g("src").reshape(EP, EK), dst=g("dst").reshape(EP, EK), edge_weight=g("edge_weight").reshape(EP, EK),
        w1=units(g("L0_gnn_W1")), b1=col(g("L0_gnn_b1")),
        gate_w=g("L0_gnn_gate_w").reshape(4, 2 * NH), gate_b=g("L0_gnn_gate_b").reshape(1, -1),
        qkv0=qkv(g("L0_mix_Wq"), g("L0_mix_Wk"), g("L0_mix_Wv")), bq0=col(g("L0_mix_bq")),
        bkv0=pair(g("L0_mix_bk"), g("L0_mix_bv")), wo0=units(g("L0_mix_Wo").T), bo0=col(g("L0_mix_bo")),
        gate=g("L0_ffn_gate").reshape(KC, P, 8).transpose(1, 0, 2).reshape(P, -1),
        experts=_np.concatenate([mlp(*w) for w in zip(g("L0_ffn_experts_w1"), g("L0_ffn_experts_w3"),
                                                      g("L0_ffn_experts_w2"))], 0),
        gnn_bias=col(g("L1_gnn_bias")),
        qkv1=qkv(g("L1_mix_q_w"), g("L1_mix_k_w"), g("L1_mix_v_w")), bq1=col(g("L1_mix_q_b")),
        bkv1=pair(g("L1_mix_k_b"), g("L1_mix_v_b")), wo1=units(g("L1_mix_o_w").T), bo1=col(g("L1_mix_o_b")),
        ffn=mlp(g("L1_ffn_w_gate").T, g("L1_ffn_w_up").T, g("L1_ffn_w_down").T),
    )
    ins = {n: _np.ascontiguousarray(v) for n, v in ins.items()}
    known = {}
    for _ in range(2):
        nc = _bacc.Bacc("TRN2", target_bir_lowering=False, num_devices=1)
        io = {n: nc.dram_tensor("in_" + n, v.shape, mybir.dt.from_np(v.dtype), kind="ExternalInput").ap()
              for n, v in ins.items()}
        io["out"] = nc.dram_tensor("out_y", (KC, P, N), F32, kind="ExternalOutput").ap()
        build(nc, io, known)
    r = _run(nc, [{"in_" + n: v for n, v in ins.items()}], core_ids=[0])
    y = r.results[0]["out_y"]
    return _np.ascontiguousarray(y.reshape(D, N).T)
```

```python
from contextlib import contextmanager, ExitStack

import numpy as np
import concourse.bass as bass
from concourse import mybir

F32, F32R, I32, U32, U16, BF16 = (mybir.dt.float32, mybir.dt.float32r, mybir.dt.int32, mybir.dt.uint32,
                                  mybir.dt.uint16, mybir.dt.bfloat16)
ALU = mybir.AluOpType
ACT = mybir.ActivationFunctionType
AX = mybir.AxisListType

P = 128
N = 1250
E = 20000
D = 1024
NH = 512
KC = D // P
GC = NH // P
NT = 3
TW = 418
TM = NT * TW
TC = 10
LAST = N - (TC - 1) * P
EPS = 1e-5
EP, EK = 125, 160
NBUCK = TC * TC
HOME = 3
NST = HOME * NBUCK
NOV = 160
NCH = NST + NOV
RANK = 1 << 15
assert E // P < NOV and EP * EK == E and E < RANK and RANK * NOV < 1 << 24


def rows_of(c):
    return P if c < TC - 1 else LAST


class Loops:

    def __init__(self):
        self.active, self.counts, self.steps = {}, {}, []

    @contextmanager
    def run(self, engine, name, count):
        self.counts[name] = count
        before = [s.count for s in self.steps]
        with engine.Fori(0, count) as i:
            self.active[name] = i
            yield i
        del self.active[name]
        for s, b in zip(self.steps, before):
            s.close(name, b, count)


class Steps:

    def __init__(self, nc, ctx, loops, name, known, each=1):
        self.sem = nc.alloc_semaphore(name)
        self.loops, self.each, self.name = loops, each, name
        self.known = known.get(name, ({}, {}))
        self.count, self.at, self.slope = 0, {}, {}
        if not loops.steps:
            loops.spare = nc.alloc_semaphore(name + "_spare")
        loops.steps.append(self)

    def mark(self, instruction, step):
        assert step not in self.at, step
        instruction.then_inc(self.sem, self.each)
        self.count += self.each
        self.at[step] = (self.count, tuple(self.loops.active))
        return instruction

    def alias(self, step, of):
        self.at[step] = self.at[of]

    def start(self, engine, by):
        engine.sem_inc(self.sem, by)
        self.count = by

    def close(self, loop, before, turns):
        if self.count > before:
            self.slope[loop] = self.count - before
            self.count = before + turns * (self.count - before)

    def wait(self, engine, step, back=0):
        at, slope = self.known
        if not at:
            return
        value, around = at[step]
        for n, loop in enumerate(around):
            shift = back.get(loop, 0) if isinstance(back, dict) else back if n == len(around) - 1 else 0
            i = self.loops.active.get(loop)
            if i is None:
                value += slope[loop] * (self.loops.counts[loop] - 1 - shift)
            else:
                value -= slope[loop] * shift
        assert value >= 0, (self.name, step, value)
        assert value or not any(l in self.loops.active for l in around), (self.name, step)
        for loop in around:
            i = self.loops.active.get(loop)
            if i is not None:
                value = i * slope[loop] + value
        engine.wait_ge(self.sem, value)
        if not isinstance(value, int):
            engine.sem_inc(self.loops.spare, 1)

    def learned(self):
        return self.at, self.slope



class Weights:

    def __init__(self, nc, ctx, tag, slots, width, new, dtype=F32, scale=None):
        t = lambda n, d: ctx.enter_context(nc.sbuf_tensor(f"{tag}_{n}", [P, slots, width], d))
        self.raw, self.hi, self.lo, self.scale = t("raw", dtype), t("hi", F32R), t("lo", F32R), scale
        self.loaded = [new(f"{tag}_ld{s}", 16) for s in range(slots)]
        self.his, self.los = new(f"{tag}_hi"), new(f"{tag}_lo")

    def load(self, e, slot, src, step):
        self.loaded[slot].mark(e.dma_start(self.raw[:, slot], src), step)

    def make_hi(self, e, slot, step, back=0):
        self.loaded[slot].wait(e, step, back)
        self.his.mark(e.activation(self.hi[:, slot], self.raw[:, slot], ACT.Copy, scale=self.scale or 1.0), step)

    def make_lo(self, e, slot, step, back=0):
        self.his.wait(e, step, back)
        hi = self.hi[:, slot].bitcast(F32)
        if self.scale is None:
            i = e.tensor_tensor(self.lo[:, slot], self.raw[:, slot], hi, ALU.subtract)
        else:
            i = e.scalar_tensor_tensor(self.lo[:, slot], self.raw[:, slot], self.scale, hi, ALU.mult, ALU.subtract)
        self.los.mark(i, step)

    def blocks(self, slot, first, count):
        cut = lambda w: [w[:, slot, (first + k) * P:(first + k + 1) * P] for k in range(count)]
        return cut(self.hi), cut(self.lo)


def product(e, out, w, x):
    (wh, wl), (xh, xl) = w, x
    terms = list(zip(wl, xh)) + list(zip(wh, xl)) + list(zip(wh, xh))
    for n, (a, b) in enumerate(terms):
        i = e.matmul(out, a, b, start=n == 0, stop=n == len(terms) - 1)
    return i


class Phase:

    def __init__(self, nc, known, tag):
        self.nc, self.known, self.tag = nc, known, tag
        self.ctx, self.loops, self.got = ExitStack(), Loops(), {}
        self.loops.counts = known.setdefault(tag + "_turns", {})

    def __enter__(self):
        return self

    def __exit__(self, *a):
        self.ctx.close()
        if a[0] is None:
            self.nc.clear_and_free_semaphores([self.loops.spare] + [s.sem for s in self.got.values()])
            self.nc.all_engine_barrier()
        self.known.update({n: s.learned() for n, s in self.got.items()})

    def new(self, n, each=1):
        n = f"{self.tag}_{n}"
        s = self.got[n] = Steps(self.nc, self.ctx, self.loops, n, self.known, each)
        return s

    def sb(self, n, shape, d=F32):
        return self.ctx.enter_context(self.nc.sbuf_tensor(f"{self.tag}_{n}", shape, d))

    def banks(self, count):
        return [self.ctx.enter_context(self.nc.psum_tensor(f"{self.tag}_bank{i}", [P, 512], F32))
                for i in range(count)]

    def block(self):
        return self.ctx.enter_context(self.nc.Block())


def tile(t):
    return slice(t * TW, (t + 1) * TW)


def parts(xh, xl, t, count=KC):
    return [xh[:, k, tile(t)] for k in range(count)], [xl[:, k, tile(t)] for k in range(count)]


def layer_norm(nc, known, tag, x, xh, xl):
    with Phase(nc, known, tag) as p:
        pl, dv, pe, ac = p.new("pool"), p.new("dve"), p.new("pe"), p.new("act")
        ones = p.sb("ones", [P, P])
        xc = p.sb("xc", [P, NT, KC, TW])
        sq = p.sb("sq", [P, 2, KC, TW])
        ve, rv, y = (p.sb(n, [P, NT, TW]) for n in ("ve", "rv", "y"))
        z = p.sb("z", [P, TW])
        HK = KC // 2
        ORDER = (("mean", 0), ("mean", 1), ("var", 0), ("mean", 2), ("var", 1), ("var", 2))
        bank = p.banks(6)
        block = p.block()

        dv_y, pl_n = p.new("dy"), p.new("pn")

        def norm(e, t, k, steps):
            steps.mark(e.tensor_tensor(xc[:, t, k:k + HK], xc[:, t, k:k + HK],
                                       y[:, t].unsqueeze(1).broadcast_to([P, HK, TW]), ALU.mult), f"normed{t}{k}")

        def low(e, t, steps):
            for k in range(0, KC, HK):
                ac.wait(e, f"hi{t}{k}")
                steps.mark(e.tensor_tensor(xl[:, k:k + HK, tile(t)], xc[:, t, k:k + HK],
                                           xh[:, k:k + HK, tile(t)].bitcast(F32), ALU.subtract), f"lo{t}{k}")

        @block.gpsimd
        def _(e):
            pl.mark(e.memset(ones[:], 1.0 / D), "ones")
            for t in range(NT - 1):
                dv_y.wait(e, f"y{t}")
                norm(e, t, HK, pl_n)
                low(e, t, pl)

        @block.tensor
        def _(e):
            pl.wait(e, "ones")
            for step, t in ORDER:
                if step == "mean":
                    for k in range(KC):
                        m = e.matmul(bank[t][:, 0:TW], ones[:], x[:, k, tile(t)], start=k == 0, stop=k == KC - 1)
                else:
                    ac.wait(e, f"sq{t}")
                    for k in range(KC):
                        m = e.matmul(bank[3 + t][:, 0:TW], ones[:], sq[:, t % 2, k], start=k == 0, stop=k == KC - 1)
                pe.mark(m, f"{step}{t}")

        @block.scalar
        def _(e):
            for step, t in ORDER:
                if step == "mean":
                    dv.wait(e, f"centred{t}")
                    if t == 2:
                        pe.wait(e, "var0")
                    ac.mark(e.activation(sq[:, t % 2], xc[:, t], ACT.Square), f"sq{t}")
                else:
                    dv.wait(e, f"rv{t}")
                    ac.mark(e.activation(y[:, t], rv[:, t], ACT.Sqrt), f"root{t}")
                    for k in range(0, KC, HK):
                        (dv if t == NT - 1 or k == 0 else pl_n).wait(e, f"normed{t}{k}")
                        ac.mark(e.activation(xh[:, k:k + HK, tile(t)], xc[:, t, k:k + HK], ACT.Copy), f"hi{t}{k}")

        @block.vector
        def _(e):
            pl.wait(e, "ones")
            for step, t in ORDER:
                pe.wait(e, f"{step}{t}")
                if step == "mean":
                    dv.mark(e.tensor_tensor(xc[:, t], x[:, :, tile(t)],
                                            bank[t][:, 0:TW].unsqueeze(1).broadcast_to([P, KC, TW]),
                                            ALU.subtract), f"centred{t}")
                    continue
                e.tensor_scalar(ve[:, t], bank[3 + t][:, 0:TW], EPS, None, ALU.add)
                e.drain()
                dv.mark(e.reciprocal(rv[:, t], ve[:, t]), f"rv{t}")
                ac.wait(e, f"root{t}")
                e.tensor_tensor(z[:], y[:, t], y[:, t], ALU.mult)
                e.drain()
                e.tensor_tensor(z[:], z[:], ve[:, t], ALU.mult)
                e.drain()
                e.tensor_scalar(z[:], z[:], -0.5, 1.5, ALU.mult, ALU.add)
                e.drain()
                if t < NT - 1:
                    dv_y.mark(e.tensor_tensor(y[:, t], y[:, t], z[:], ALU.mult), f"y{t}")
                else:
                    e.tensor_tensor(y[:, t], y[:, t], z[:], ALU.mult)
                e.drain()
                for k in range(0, KC, HK):
                    if t == NT - 1 or k == 0:
                        norm(e, t, k, dv)
            low(e, NT - 1, dv)


def dense(nc, known, tag, xh, xl, w_dram, units, bias_dram, out=None, store=None, base=None, spill=None,
          beside=None):
    with Phase(nc, known, tag) as p:
        w = Weights(nc, p.ctx, tag + "_w", 2, D, lambda n, each=1: p.new(n, each))
        ld, dv, pe, ac = p.new("ld", 16), p.new("dve"), p.new("pe"), p.new("act")
        bs, at = [p.new(f"base{b}", 16) for b in range(2)], p.new("at")
        sps = [p.new(f"spill{b}", 16) for b in range(2)]
        sts = [p.new(f"st{b}", 16) for b in range(2)]
        bias = p.sb("bias", [P, units])
        to_dram = store is not None
        res = p.sb("res", [P, 2, NT, TW]) if to_dram else None
        bank = p.banks(6)
        block = p.block()
        turns = units // 2

        if beside:
            @block.gpsimd
            def _(e):
                beside(e, p)

        if spill is not None:
            @block.gpsimd
            def _(e):
                with p.loops.run(e, "units", turns) as i:
                    for b in range(2):
                        dv.wait(e, f"ev{b}{NT - 1}")
                        o = out[:, bass.ds(i * 2 + b, 1), 0:N].rearrange("p a n -> p (a n)")
                        sps[b].mark(e.dma_start(spill[i * 2 + b], o), f"spill{b}")
                for b in range(2):
                    sps[b].wait(e, f"spill{b}")

        @block.sync
        def _(e):
            ld.mark(e.dma_start(bias[:], bias_dram, allow_slow_non_contiguous=True), "bias")
            if to_dram:
                for s in sts:
                    s.start(e, 1)
            w.load(e, 0, w_dram[0], "first")
            if base is not None:
                at.wait(e, f"al{NT - 1}")
            with p.loops.run(e, "units", turns) as i:
                if base is not None:
                    for b in range(2):
                        o = out[:, bass.ds(i * 2 + b, 1), 0:N].rearrange("p a n -> p (a n)")
                        bs[b].mark(e.dma_start(o, base[i * 2 + b]), f"base{b}")
                w.los.wait(e, "w1", back=1)
                w.load(e, 1, w_dram[i * 2 + 1], "w1")
                w.los.wait(e, "w0", back=1)
                w.load(e, 0, w_dram[(i * 2 + 2) % units], "w0")
                if to_dram:
                    for b in range(2):
                        for t in range(NT):
                            ac.wait(e, f"ev{b}{t}")
                        sts[b].mark(e.dma_start(store[i * 2 + b], res[:, b].rearrange("p t n -> p (t n)")), f"st{b}")
            if to_dram:
                sts[0].wait(e, "st0")
                sts[1].wait(e, "st1")

        @block.scalar
        def _(e):
            if base is not None:
                for t in range(NT):
                    ac.mark(e.activation(xh[:, :, tile(t)], out[:, :, tile(t)], ACT.Copy), f"ah{t}")
                    if t == 0:
                        w.make_hi(e, 0, "first")
            else:
                w.make_hi(e, 0, "first")
            if to_dram:
                ac.start(e, 6)
            ld.wait(e, "bias")
            with p.loops.run(e, "units", turns) as i:
                for b in range(2):
                    if b == 0:
                        pe.wait(e, "t12", back=1)
                        w.make_hi(e, 1, "w1")
                    else:
                        pe.wait(e, "t02")
                        w.make_hi(e, 0, "w0")
                    if to_dram:
                        sts[b].wait(e, f"st{b}", back=1)
                        for t in range(NT):
                            pe.wait(e, f"t{b}{t}")
                            ac.mark(e.activation(res[:, b, t], bank[3 * b + t][:, 0:TW], ACT.Identity,
                                                 bias=bias[:, bass.ds(i * 2 + b, 1)]), f"ev{b}{t}")

        @block.vector
        def _(e):
            if not to_dram:
                dv.start(e, 6)
            w.los.start(e, 1)
            if base is not None:
                for t in range(NT):
                    ac.wait(e, f"ah{t}")
                    at.mark(e.tensor_tensor(xl[:, :, tile(t)], out[:, :, tile(t)],
                                            xh[:, :, tile(t)].bitcast(F32), ALU.subtract), f"al{t}")
                    if t == 0:
                        w.make_lo(e, 0, "first")
            else:
                w.make_lo(e, 0, "first")
            ld.wait(e, "bias")
            with p.loops.run(e, "units", turns) as i:
                for b in range(2):
                    w.make_lo(e, 1 - b, f"w{1 - b}")
                    if base is not None:
                        bs[b].wait(e, f"base{b}")
                    if not to_dram:
                        for t in range(NT):
                            pe.wait(e, f"t{b}{t}")
                            o = out[:, i * 2 + b, tile(t)]
                            dv.mark(e.scalar_tensor_tensor(o, bank[3 * b + t][:, 0:TW],
                                                           bias[:, bass.ds(i * 2 + b, 1)], o, ALU.add, ALU.add),
                                    f"ev{b}{t}")

        @block.tensor
        def _(e):
            pe.start(e, 1)
            with p.loops.run(e, "units", turns):
                for b in range(2):
                    w.los.wait(e, f"w{b}", back=1 - b)
                    for t in range(NT):
                        if base is not None:
                            at.wait(e, f"al{t}")
                        (ac if to_dram else dv).wait(e, f"ev{b}{t}", back=1)
                        m = product(e, bank[3 * b + t][:, 0:TW], w.blocks(b, 0, KC), parts(xh, xl, t))
                        pe.mark(m, f"t{b}{t}")


def graph_sort(nc, known, dram, x, x_dram, idx, pay, spill):
    with Phase(nc, known, "gs") as p:
        sb, new, ctx = p.sb, p.new, p.ctx
        ld, pl, dv, pe = new("ld", 16), new("pool"), new("dve"), new("pe")
        fill, offs, xs = new("fill", 16), new("offs", 16), new("x", 16)
        src, dst, wgt = sb("src", [EP, EK], I32), sb("dst", [EP, EK], I32), sb("wgt", [EP, EK])
        hs, hd = sb("hs", [EP, EK], I32), sb("hd", [EP, EK], I32)
        fs, fd, fhs, fhd = sb("fs", [EP, EK]), sb("fd", [EP, EK]), sb("fhs", [EP, EK]), sb("fhd", [EP, EK])
        key = sb("key", [EP, EK])
        iob = sb("iob", [P, NBUCK])
        cid = sb("cid", [P, 2])
        hot = sb("hot", [EP, NBUCK, EK], BF16)
        run = sb("run", [EP, NBUCK, EK])
        cnt = sb("cnt", [EP, NBUCK])
        tri = sb("tri", [EP, P])
        ones = sb("ones", [EP, P])
        tot, toti = sb("tot", [P, NBUCK]), sb("toti", [P, NBUCK], I32)
        nch, incl = sb("nch", [P, NBUCK]), sb("incl", [P, NBUCK])
        base = sb("base", [EP, NBUCK])
        pos, posi = sb("pos", [EP, EK]), sb("posi", [EP, EK], I32)
        ranki, obi = sb("ranki", [EP, EK], I32), sb("obi", [EP, EK], I32)
        rank, ob, over = sb("rank", [EP, EK]), sb("ob", [EP, EK]), sb("over", [EP, EK])
        lo7, hi7, idf = sb("lo7", [EP, EK], I32), sb("hi7", [EP, EK], I32), sb("idf", [EP, EK])
        empty = sb("empty", [P, NCH * 4])
        cmp = sb("cmp", [P, NBUCK])
        bk = sb("bk", [P, 2])
        bki, sbi = sb("bki", [P, 2], I32), sb("sbi", [P, 2], I32)
        bkb, far = sb("bkb", [P, 2]), sb("far", [P, 2])
        sbf, offc, offw = sb("sbf", [P, 2]), sb("offc", [P, 2]), sb("offw", [P, 2])
        off = sb("off", [P, 2, 2], I32)
        pp = ctx.enter_context(nc.psum_tensor("gs_pp", [P, NBUCK], F32))
        pt = ctx.enter_context(nc.psum_tensor("gs_pt", [P, NBUCK], F32))
        SHARE = 68
        pl_p = new("padd")
        block = p.block()

        def place(e, first, last, between):
            r, n = run[:, first:last], last - first
            i = e.tensor_tensor(r, r, base[:, first:last].unsqueeze(2).broadcast_to([EP, n, EK]), ALU.add)
            if last == NBUCK:
                pl_p.mark(i, "added")
            between()
            i = e.tensor_tensor(r, r, hot[:, first:last], ALU.mult)
            if last == NBUCK:
                pl.mark(i, "placed")

        @block.sync
        def _(e):
            ld.mark(e.dma_start(src[:], dram["src"]), "src")
            ld.mark(e.dma_start(dst[:], dram["dst"]), "dst")
            ld.mark(e.dma_start(wgt[:], dram["edge_weight"]), "wgt")
            for k in range(KC):
                xs.mark(e.dma_start(x[:, k, 0:N], x_dram[k]), f"x{k}")
            pl.wait(e, "empty")
            fill.mark(e.dma_start(dram["slots"], empty[:]), "fill")
            dv.wait(e, "off")
            offs.mark(e.dma_start(dram["offs"], off[:]), "off")
            offs.wait(e, "off")
            fill.wait(e, "fill")
            xs.wait(e, f"x{KC - 1}")

        @block.gpsimd
        def _(e):
            e.iota(iob[:], [[1, NBUCK]], base=0, channel_multiplier=0, allow_small_or_imprecise_dtypes=True)
            e.iota(cid[:], [[P, 2]], base=0, channel_multiplier=1, allow_small_or_imprecise_dtypes=True)
            e.memset(ones[:], 1.0)
            e.memset(tri[:], 1.0)
            pl.mark(e.memset(empty[:], -1.0), "empty")
            pl.wait(e, "empty")
            pl.mark(e.affine_select(out=tri[:], in_=tri[:], compare_op=ALU.is_gt, fill=0.0, base=0,
                                    pattern=[[1, P]], channel_multiplier=-1), "tri")
            e.memset(x[:, :, N:TM], 0.0)
            dv.wait(e, "base")
            place(e, SHARE, NBUCK, lambda: pl_p.wait(e, "added"))

        @block.tensor
        def _(e):
            dv.wait(e, "cnt")
            pl.wait(e, "tri")
            e.matmul(pp[0:EP, :], tri[:, 0:EP], cnt[:], start=True, stop=True)
            pe.mark(e.matmul(pt[:], ones[:], cnt[:], start=True, stop=True), "sums")

        @block.vector
        def _(e):
            d = e.drain
            ld.wait(e, "wgt")
            e.tensor_scalar(hs[:], src[:], 7, None, ALU.arith_shift_right)
            e.tensor_scalar(hd[:], dst[:], 7, None, ALU.arith_shift_right)
            e.tensor_copy(fs[:], src[:])
            e.tensor_copy(fd[:], dst[:])
            d()
            e.tensor_copy(fhs[:], hs[:])
            e.tensor_copy(fhd[:], hd[:])
            d()
            e.scalar_tensor_tensor(key[:], fhs[:], float(TC), fhd[:], ALU.mult, ALU.add)
            e.scalar_tensor_tensor(pay[:, :, 0], fhs[:], -float(P), fs[:], ALU.mult, ALU.add)
            e.scalar_tensor_tensor(pay[:, :, 1], fhd[:], -float(P), fd[:], ALU.mult, ALU.add)
            e.tensor_copy(pay[:, :, 2], wgt[:])
            e.memset(pay[:, :, 3], 0.0)
            pl.wait(e, "tri")
            d()
            e.tensor_tensor(hot[:], key[:].unsqueeze(1).broadcast_to([EP, NBUCK, EK]),
                            iob[0:EP, :].unsqueeze(2).broadcast_to([EP, NBUCK, EK]), ALU.is_equal)
            d()
            flat = lambda t: t[:].rearrange("p b k -> p (b k)")
            e.tensor_tensor_scan(flat(run), flat(hot), flat(hot), 0.0, ALU.add, ALU.max)
            d()
            e.tensor_copy(cnt[:, 0:1], run[:, 0, EK - 1:EK])
            dv.mark(e.tensor_tensor(cnt[:, 1:NBUCK], run[:, 1:NBUCK, EK - 1], run[:, 0:NBUCK - 1, EK - 1],
                                    ALU.subtract), "cnt")
            pe.wait(e, "sums")
            e.tensor_scalar(tot[:], pt[:], float(HOME * P), 0.0, ALU.subtract, ALU.max)
            d()
            e.tensor_scalar(toti[:], tot[:], float(P - 1), None, ALU.add)
            d()
            e.tensor_scalar(toti[:], toti[:], 7, None, ALU.arith_shift_right)
            d()
            e.tensor_copy(nch[:], toti[:])
            d()
            e.tensor_tensor_scan(incl[:], nch[:], nch[:], 0.0, ALU.add, ALU.max)
            d()
            e.tensor_tensor(nch[:], incl[:], nch[:], ALU.subtract)
            e.tensor_copy(spill[:], incl[:, NBUCK - 1:NBUCK])
            d()
            e.scalar_tensor_tensor(base[:], nch[0:EP, :], float(RANK), pp[0:EP, :], ALU.mult, ALU.add)
            d()
            e.tensor_tensor(base[:, 1:NBUCK], base[:, 1:NBUCK], run[:, 0:NBUCK - 1, EK - 1], ALU.subtract)
            d()
            dv.mark(e.tensor_scalar(base[:], base[:], -1.0, None, ALU.add), "base")
            for t in range(2):
                e.tensor_scalar(cmp[:], incl[:], cid[:, t:t + 1], 0.0, ALU.is_le, ALU.add,
                                accum_out=bk[:, t:t + 1])
                d()
            d()
            place(e, 0, SHARE, d)
            e.tensor_copy(bki[:], bk[:])
            d()
            pl.wait(e, "placed")
            e.tensor_reduce(pos[:], run[:].rearrange("p b k -> p k b"), AX.X, ALU.add)
            d()
            e.tensor_copy(posi[:], pos[:])
            d()
            e.tensor_scalar(ranki[:], posi[:], RANK - 1, None, ALU.bitwise_and)
            e.tensor_scalar(obi[:], posi[:], 15, None, ALU.arith_shift_right)
            d()
            e.tensor_copy(rank[:], ranki[:])
            e.tensor_copy(ob[:], obi[:])
            d()
            e.tensor_scalar(over[:], rank[:], float(HOME * P), None, ALU.is_ge)
            e.scalar_tensor_tensor(pos[:], key[:], float(HOME * P), rank[:], ALU.mult, ALU.add)
            e.tensor_scalar(ob[:], ob[:], float(P), float(P * NST - HOME * P), ALU.mult, ALU.add)
            d()
            e.scalar_tensor_tensor(ob[:], key[:], -float(HOME * P), ob[:], ALU.mult, ALU.add)
            d()
            e.tensor_tensor(ob[:], ob[:], over[:], ALU.mult)
            d()
            e.tensor_tensor(posi[:], pos[:], ob[:], ALU.add)
            d()
            e.tensor_scalar(lo7[:], posi[:], P - 1, None, ALU.bitwise_and)
            e.tensor_scalar(hi7[:], posi[:], 7, None, ALU.arith_shift_right)
            d()
            e.tensor_copy(idf[:], lo7[:])
            e.tensor_copy(rank[:], hi7[:])
            d()
            e.scalar_tensor_tensor(idx[:], idf[:], float(NCH), rank[:], ALU.mult, ALU.add)
            e.tensor_scalar(bkb[:], bk[:], 103.0, None, ALU.mult)
            e.tensor_scalar(offc[:], bk[:], float(P), None, ALU.mult)
            d()
            e.tensor_copy(sbi[:], bkb[:])
            d()
            e.tensor_scalar(sbi[:], sbi[:], 10, None, ALU.arith_shift_right)
            d()
            e.tensor_copy(sbf[:], sbi[:])
            d()
            e.scalar_tensor_tensor(far[:], sbf[:], -float(TC), bk[:], ALU.mult, ALU.add)
            d()
            e.scalar_tensor_tensor(offw[:], sbf[:], float(KC), far[:], ALU.mult, ALU.add)
            d()
            e.tensor_scalar(far[:], far[:], float(KC), float(KC * KC), ALU.is_ge, ALU.mult)
            d()
            e.tensor_tensor(offw[:], offw[:], far[:], ALU.add)
            d()
            e.tensor_scalar(offw[:], offw[:], float(KC * KC), float(P), ALU.min, ALU.mult)
            d()
            e.tensor_copy(off[:, 0, :], offc[:])
            dv.mark(e.tensor_copy(off[:, 1, :], offw[:]), "off")


def scatter(e, p, dram, idx, pay, first, last):
    scat = p.new("scat", 16)
    for k in range(first, last):
        scat.mark(e.indirect_dma_start(dram["slot_rows"],
                                       bass.IndirectOffsetOnAxis(idx[:, k:k + 1].bitcast(U32), 0),
                                       pay[:, k, :], None), f"scatter{k}")
    scat.wait(e, f"scatter{last - 1}")


def graph_home(nc, known, dram, c16):
    HD = TC // 2
    HC = HD * HOME
    NW = (HD, KC - HD)
    with Phase(nc, known, "gh") as p:
        ld, st, pl, pe, ac = p.new("ld", 16), p.new("st", 16), p.new("pool"), p.new("pe"), p.new("act")
        pl_l, dv_0, dv_w, dv_e = p.new("low"), p.new("hs0"), p.new("wsplit"), p.new("dev")
        ac_c = p.new("ac")
        dv = p.new("dve")
        slots = p.sb("slots", [P, NST, 4])
        whi, wlo = p.sb("whi", [P, NST], F32R), p.sb("wlo", [P, NST])
        iot = p.sb("iot", [P, P])
        hs, hd = (p.sb(n, [P, 2, HC, P], F32R) for n in ("hs", "hd"))
        ws = p.sb("ws", [P, 2, HC, 2, P], F32R)
        wacc = p.sb("wacc", [P, TC, D])
        wide = lambda t, n=HC: t.unsqueeze(2).broadcast_to([P, n, P])
        pc = p.ctx.enter_context(nc.psum_tensor("gh_pc", [P, 8, P], F32))
        pw = [p.ctx.enter_context(nc.psum_tensor(f"gh_pw{h}", [P, 6, 2, P], F32)) for h in range(2)]
        block = p.block()

        def source(e, h):
            dv_0.wait(e, "source", back=1) if h == 0 else dv.wait(e, "hs1")

        @block.sync
        def _(e):
            ld.mark(e.dma_start(slots[:], dram["slots"].rearrange("p (c f) -> p c f", f=4)[:, 0:NST]), "slots")
            with p.loops.run(e, "rows", TC) as i:
                dv_e.wait(e, "w1")
                st.mark(e.dma_start(dram["wmat"][i], wacc[:, bass.ds(i, 1)].rearrange("p a b -> p (a b)")), "wmat")
            st.wait(e, "wmat")

        @block.gpsimd
        def _(e):
            pl.mark(e.iota(iot[:], [[1, P]], base=0, channel_multiplier=0,
                           allow_small_or_imprecise_dtypes=True), "iota")
            dv_w.wait(e, "wlo")
            with p.loops.run(e, "rows", TC) as i:
                for h in range(2):
                    pe.wait(e, f"w{h}", back=1)
                    source(e, h)
                    n = NW[h] * HOME
                    cut = bass.ds(i * (2 * HC) + h * HC, n)
                    pl_l.mark(e.tensor_tensor(ws[:, h, 0:n, 1], hs[:, h, 0:n].bitcast(F32), wide(wlo[:, cut], n),
                                              ALU.mult), f"wl{h}")

        @block.scalar
        def _(e):
            dv_w.wait(e, "wlo")
            with p.loops.run(e, "rows", TC) as i:
                for h in range(2):
                    pe.wait(e, f"w{h}", back=1)
                    source(e, h)
                    for u in range(NW[h] * HOME):
                        c = i * (2 * HC) + (h * HC + u)
                        a = e.activation(ws[:, h, u, 0], hs[:, h, u].bitcast(F32), ACT.Copy,
                                         scale=whi[:, bass.ds(c, 1)].bitcast(F32))
                    ac.mark(a, f"wh{h}")
                pe.wait(e, "w0")
                o = c16[:, bass.ds(i, 1), 0:HD * P].rearrange("p a b -> p (a b)")
                ac_c.mark(e.activation(o, pc[:, 0:HD].rearrange("p a b -> p (a b)"), ACT.Copy), "c0")

        @block.tensor
        def _(e):
            pe.start(e, 4)
            with p.loops.run(e, "rows", TC):
                for h in range(2):
                    dv_e.wait(e, f"w{h}", back=1)
                    dv_e.wait(e, "c1", back=1) if h == 0 else ac_c.wait(e, "c0")
                    dv_0.wait(e, "target", back=1) if h == 0 else dv.wait(e, "hd1")
                    for d in range(HD):
                        for n in range(HOME):
                            u = d * HOME + n
                            e.matmul(pc[:, d], hs[:, h, u], hd[:, h, u], start=n == 0, stop=n == HOME - 1)
                    ac.wait(e, f"wh{h}")
                    pl_l.wait(e, f"wl{h}")
                    for d in range(NW[h]):
                        for n in range(HOME):
                            u = d * HOME + n
                            m = e.matmul(pw[h][:, d].rearrange("p a b -> p (a b)"), hd[:, h, u],
                                         ws[:, h, u].rearrange("p a b -> p (a b)"),
                                         start=n == 0, stop=n == HOME - 1)
                    pe.mark(m, f"w{h}")

        @block.vector
        def _(e):
            ld.wait(e, "slots")
            e.tensor_copy(whi[:], slots[:, :, 2])
            e.drain()
            dv_w.mark(e.tensor_tensor(wlo[:], slots[:, :, 2], whi[:].bitcast(F32), ALU.subtract), "wlo")
            pl.wait(e, "iota")
            dv_e.start(e, 4)

            def hot(out, h, row, field):
                cut = bass.ds(row * (2 * HC) + h * HC, HC)
                return e.tensor_tensor(out[:, h], wide(slots[:, cut, field]),
                                       iot[:].unsqueeze(1).broadcast_to([P, HC, P]), ALU.is_equal)

            def evict(i, h):
                pe.wait(e, f"w{h}")
                if h == 1:
                    o = c16[:, bass.ds(i, 1), h * HD * P:(h + 1) * HD * P].rearrange("p a b -> p (a b)")
                    dv_e.mark(e.tensor_copy(o, pc[:, 0:HD].rearrange("p a b -> p (a b)")), f"c{h}")
                o = wacc[:, bass.ds(i, 1), h * HD * P:(h * HD + NW[h]) * P].rearrange("p a (b c) -> p (a b) c", c=P)
                dv_e.mark(e.tensor_reduce(o, pw[h][:, 0:NW[h]].rearrange("p d a b -> p d b a"), AX.X, ALU.add),
                          f"w{h}")

            dv_0.mark(hot(hs, 0, 0, 0), "first source")
            dv_0.mark(hot(hd, 0, 0, 1), "first target")
            with p.loops.run(e, "rows", TC) as i:
                pe.wait(e, "w1", back=1)
                dv.mark(hot(hs, 1, i, 0), "hs1")
                dv.mark(hot(hd, 1, i, 1), "hd1")
                evict(i, 0)
                dv_0.mark(hot(hs, 0, (i + 1) % TC, 0), "source")
                dv_0.mark(hot(hd, 0, (i + 1) % TC, 1), "target")
                evict(i, 1)


def graph_overflow(nc, known, dram, c16, spill):
    UN = 8
    BODY = 2 * UN
    with Phase(nc, known, "gb") as p:
        sb, new, ctx, loops = p.sb, p.new, p.ctx, p.loops
        ld, pl, dv, pe, act, st = new("ld", 16), new("pool"), new("dve"), new("pe"), new("act"), new("st", 16)
        slots = sb("slots", [P, NOV, 4])
        whi, wlo = sb("whi", [P, NOV], F32R), sb("wlo", [P, NOV])
        offc, offw = sb("offc", [1, 2 * P], I32), sb("offw", [1, 2 * P], I32)
        iot = sb("iot", [P, P])
        hs = sb("hs", [P, 2, UN, P], F32R)
        hd = sb("hd", [P, 2, UN, P], F32R)
        wh = sb("wh", [P, 2, UN, P], F32R)
        wl = sb("wl", [P, 2, UN, P], F32R)
        cacc = sb("cacc", [P, (NBUCK + 1) * P])
        wacc = sb("wacc", [P, (KC * KC + 1) * P])
        flat = c16[:].rearrange("p a b -> p (a b)")
        pc = [ctx.enter_context(nc.psum_tensor(f"gb_pc{i}", [P, 4, P], F32)) for i in range(4)]
        pw = [ctx.enter_context(nc.psum_tensor(f"gb_pw{i}", [P, 4, P], F32)) for i in range(4)]
        block = p.block()

        def some(e):
            return e.If(e.value_load(spill[0:1, 0:1], min_val=0, max_val=NOV) > 0)

        @block.sync
        def _(e):
            with some(e):
                ld.mark(e.dma_start(slots[:], dram["slots"].rearrange("p (c f) -> p c f", f=4)[:, NST:]), "slots")
                ld.mark(e.dma_start(wacc[:, 0:KC * KC * P].rearrange("p (m n) -> p m n", m=KC),
                                    dram["wmat"][0:KC].rearrange("m p n -> p m n")), "wmat")
                o = dram["offs"].rearrange("p (a t) -> a t p", a=2)
                ld.mark(e.dma_start(offc[:], o[0:1], allow_slow_non_contiguous=True), "offc")
                ld.mark(e.dma_start(offw[:], o[1:2], allow_slow_non_contiguous=True), "offw")
                dv.wait(e, "c16")
                st.mark(e.dma_start(dram["wmat"][0:KC].rearrange("m p n -> p m n"),
                                    wacc[:, 0:KC * KC * P].rearrange("p (m n) -> p m n", m=KC)), "wmat")
                st.wait(e, "wmat")

        @block.gpsimd
        def _(e):
            with some(e):
                pl.mark(e.iota(iot[:], [[1, P]], base=0, channel_multiplier=0,
                               allow_small_or_imprecise_dtypes=True), "iota")
                e.memset(cacc[:, NBUCK * P:], 0.0)
                pl.mark(e.memset(wacc[:, KC * KC * P:], 0.0), "zero")

        @block.scalar
        def _(e):
            with some(e):
                dv.wait(e, "wlo")
                with loops.run(e, "chunks", NOV // BODY) as i:
                    for h in range(2):
                        pe.wait(e, f"w{h}", back=1)
                        dv.wait(e, f"hs{h}")
                        for u in range(UN):
                            c = i * BODY + (h * UN + u)
                            e.activation(wh[:, h, u], hs[:, h, u].bitcast(F32), ACT.Copy,
                                         scale=whi[:, bass.ds(c, 1)].bitcast(F32))
                            a = e.activation(wl[:, h, u], hs[:, h, u].bitcast(F32), ACT.Copy,
                                             scale=wlo[:, bass.ds(c, 1)])
                        act.mark(a, f"wh{h}")

        @block.tensor
        def _(e):
            with some(e):
                pe.start(e, 2)
                with loops.run(e, "chunks", NOV // BODY):
                    for h in range(2):
                        dv.wait(e, f"add{h}", back=1)
                        dv.wait(e, f"hd{h}")
                        for u in range(UN):
                            e.matmul(pc[2 * h + u // 4][:, u % 4], hs[:, h, u], hd[:, h, u], start=True, stop=True)
                        act.wait(e, f"wh{h}")
                        for u in range(UN):
                            o = pw[2 * h + u // 4][:, u % 4]
                            e.matmul(o, hd[:, h, u], wh[:, h, u], start=True, stop=False)
                            m = e.matmul(o, hd[:, h, u], wl[:, h, u], start=False, stop=True)
                        pe.mark(m, f"w{h}")

        @block.vector
        def _(e):
            with some(e):
                dv.start(e, 8)
                ld.wait(e, "offw")
                e.tensor_copy(whi[:], slots[:, :, 2])
                e.drain()
                dv.mark(e.tensor_tensor(wlo[:], slots[:, :, 2], whi[:].bitcast(F32), ALU.subtract), "wlo")
                pl.wait(e, "iota")
                pl.wait(e, "zero")
                e.tensor_copy(cacc[:, 0:NBUCK * P], flat)

                def hot(i, h):
                    for field, out, step in ((0, hs, "hs"), (1, hd, "hd")):
                        t = slots[:, bass.ds(i * BODY + h * UN, UN), field]
                        dv.mark(e.tensor_tensor(out[:, h], t.unsqueeze(2).broadcast_to([P, UN, P]),
                                                iot[:].unsqueeze(1).broadcast_to([P, UN, P]), ALU.is_equal),
                                f"{step}{h}")

                with loops.run(e, "chunks", NOV // BODY) as i:
                    for h in range(2):
                        pe.wait(e, f"w{h}", back=1)
                        hot(i, h)
                    for h in range(2):
                        pe.wait(e, f"w{h}")
                        for u in range(UN):
                            c = i * BODY + (h * UN + u)
                            oc = e.value_load(offc[0:1, bass.ds(c, 1)], min_val=0, max_val=NBUCK * P)
                            ow = e.value_load(offw[0:1, bass.ds(c, 1)], min_val=0, max_val=KC * KC * P)
                            a, b = cacc[:, bass.ds(oc, P)], wacc[:, bass.ds(ow, P)]
                            e.tensor_tensor(a, a, pc[2 * h + u // 4][:, u % 4], ALU.add)
                            last = e.tensor_tensor(b, b, pw[2 * h + u // 4][:, u % 4], ALU.add)
                            if u < UN - 1:
                                e.drain()
                        dv.mark(last, f"add{h}")
                        e.drain()
                dv.mark(e.tensor_copy(flat, cacc[:, 0:NBUCK * P]), "c16")


def attention(nc, known, tag, xh, xl, at, w_dram, bq_dram, bkv_dram, softly, beside=None):
    PAIRS, W2 = KC, 2 * P
    KW = W2 + 2
    Q, K, V = 0, 1, 2
    with Phase(nc, known, tag) as p:
        w = Weights(nc, p.ctx, tag + "_w", 3, D, lambda n, each=1: p.new(n, each))
        ld, pl = p.new("ld", 16), p.new("pool")
        dv_kv, dv_q, dv_m, dv_at = p.new("dkv"), p.new("dq"), p.new("dm"), p.new("dat")
        ac_kv, ac_q, ac_m = p.new("akv"), p.new("aq"), p.new("am")
        pe_kv, pe_q, pe_m, pe_at = p.new("pkv"), p.new("pq"), p.new("pm"), p.new("pat")
        bq = p.sb("bq", [P, KC])
        bkv = p.sb("bkv", [P, W2])
        bld = p.new("bld", 16)
        mask = p.sb("mask", [P, P])
        kvf = p.sb("kvf", [P, 4, W2])
        neg = p.sb("neg", [P, 4, P])
        kvh, kvl = p.sb("kvh", [P, TC, KW], F32R), p.sb("kvl", [P, TC, KW], F32R)
        qf = p.sb("qf", [P, NT, TW])
        qn = p.sb("qn", [P, NT, TW])
        qh, ql = p.sb("qh", [P, TM], F32R), p.sb("ql", [P, TM], F32R)
        ks = p.sb("ks", [P, 1])
        mf = p.sb("mf", [P, W2])
        mh, ml = p.sb("mh", [P, W2], F32R), p.sb("ml", [P, W2], F32R)
        bank = p.banks(8)
        NUM, DEN = (7, 0, 2), (5, 1, 6)
        KVB, QB = 0, 3
        MW = W2 if softly else P
        block = p.block()

        @block.sync
        def _(e):
            ld.mark(e.dma_start(bq[:], bq_dram, allow_slow_non_contiguous=True), "bq")
            bld.mark(e.dma_start(bkv[:], bkv_dram[0:1].broadcast_to([P, W2])), "first")
            for n, s in ((2, Q), (0, K), (1, V)):
                w.load(e, s, w_dram[n], f"first{s}")
            with p.loops.run(e, "pairs", PAIRS) as j:
                for n, s in ((2, Q), (0, K), (1, V)):
                    w.los.wait(e, f"w{s}", back=1)
                    w.load(e, s, w_dram[(j * 3 + (3 + n)) % (3 * PAIRS)], f"w{s}")
                    if s == V:
                        dv_kv.wait(e, f"kv{TC - 1}")
                        bld.mark(e.dma_start(bkv[:], bkv_dram[bass.ds((j + 1) % PAIRS, 1)].broadcast_to([P, W2])),
                                 "next")
            bld.wait(e, "next")

        @block.gpsimd
        def _(e):
            for a in range(2):
                for b in range(2):
                    i = e.memset(mask[64 * a:64 * a + 64, 64 * b:64 * b + 64], 1.0 if a == b else 0.0)
                pl.mark(i, f"mask{a}")
                pl.wait(e, f"mask{a}")
            e.memset(kvh[:, :, W2:KW].bitcast(F32), 1.0)
            pl.mark(e.memset(kvl[:, :, W2:KW].bitcast(F32), 0.0), "consts")
            if beside:
                beside(e, p)

        @block.tensor
        def _(e):
            pe_m.start(e, 1)
            pe_at.start(e, 1)
            pl.wait(e, "consts")
            with p.loops.run(e, "pairs", PAIRS):
                w.los.wait(e, f"w{Q}", back=1)
                for t in range(NT):
                    if QB + t == DEN[0]:
                        dv_at.wait(e, "at0", back=1)
                    m = product(e, bank[QB + t][:, 0:TW], w.blocks(Q, 0, KC), parts(xh, xl, t))
                    pe_q.mark(m, f"q{t}")
                w.los.wait(e, f"w{V}", back=1)
                dv_at.wait(e, "at2", back=1)
                for c in range(TC):
                    r = rows_of(c)
                    if c < 3:
                        dv_kv.wait(e, f"kv{TC - 3 + c}", back=1)
                    else:
                        dv_kv.wait(e, f"kv{c - 3}")
                    tok = slice(c * P, c * P + r)
                    n = 0
                    for a, b in ((xh, w.lo), (xl, w.hi), (xh, w.hi)):
                        for k in range(KC):
                            m = e.matmul(bank[KVB + c % 3][0:r, 0:W2], a[:, k, tok],
                                         b[:, K:V + 1, k * P:(k + 1) * P], start=n == 0, stop=n == 3 * KC - 1)
                            n += 1
                    pe_kv.mark(m, f"kv{c}")
                for c in range(TC):
                    dv_kv.wait(e, f"lo{c}")
                    r = rows_of(c)
                    for n, (a, b) in enumerate(((kvl, kvh), (kvh, kvl), (kvh, kvh))):
                        m = e.matmul(bank[6][:, 0:KW], a[0:r, c, 0:P], b[0:r, c],
                                     start=c == 0 and n == 0, stop=c == TC - 1 and n == 2)
                pe_m.mark(m, "m")
                dv_q.wait(e, "lo2")
                dv_m.wait(e, "lo")
                for t in range(NT):
                    for cut, b in ((slice(0, P), NUM[t]), (slice(P, W2), DEN[t]))[:2 if softly else 1]:
                        e.matmul(bank[b][:, 0:TW], ml[:, cut], qh[:, tile(t)], start=True, stop=False)
                        e.matmul(bank[b][:, 0:TW], mh[:, cut], ql[:, tile(t)], start=False, stop=False)
                        m = e.matmul(bank[b][:, 0:TW], mh[:, cut], qh[:, tile(t)], start=False, stop=True)
                    pe_at.mark(m, f"at{t}")

        @block.scalar
        def _(e):
            ac_q.start(e, 16)
            for s in (Q, K, V):
                w.make_hi(e, s, f"first{s}")
            ld.wait(e, "bq")
            with p.loops.run(e, "pairs", PAIRS) as j:
                for t in range(NT):
                    pe_q.wait(e, f"q{t}")
                    ac_q.mark(e.activation(qf[:, t], bank[QB + t][:, 0:TW], ACT.Identity if softly else ACT.Relu,
                                           bias=bq[:, bass.ds(j, 1)]), f"q{t}")
                if softly:
                    for t in range(NT):
                        dv_q.wait(e, f"neg{t}")
                        ac_q.mark(e.activation(qn[:, t], qn[:, t], ACT.Exp), f"exp{t}")
                else:
                    e.drain()
                pe_at.wait(e, "at2", back=1)
                for t in range(NT):
                    if softly:
                        dv_q.wait(e, f"map{t}")
                    ac_q.mark(e.activation(qh[:, tile(t)], qf[:, t], ACT.Copy), f"hi{t}")
                w.make_hi(e, Q, f"w{Q}")
                for s in range(TC + 1):
                    if s < TC and softly:
                        dv_kv.wait(e, f"kv{s}")
                        r = rows_of(s)
                        ac_kv.mark(e.activation(neg[0:r, s % 4], neg[0:r, s % 4], ACT.Exp), f"exp{s}")
                    if s >= 1:
                        c = s - 1
                        r = rows_of(c)
                        dv_kv.wait(e, f"map{c}")
                        if c == 0:
                            pe_m.wait(e, "m", back=1)
                        ac_kv.mark(e.activation(kvh[0:r, c, 0:W2], kvf[0:r, c % 4], ACT.Copy), f"hi{c}")
                pe_kv.wait(e, f"kv{TC - 1}")
                w.make_hi(e, K, f"w{K}")
                w.make_hi(e, V, f"w{V}")
                dv_m.wait(e, "m")
                ac_m.mark(e.activation(mh[:, 0:MW], mf[:, 0:MW], ACT.Copy), "hi")

        @block.vector
        def _(e):
            dv_kv.start(e, 64)
            dv_at.start(e, 3)
            pl.wait(e, "consts")
            for s in (Q, K, V):
                w.make_lo(e, s, f"first{s}")
            with p.loops.run(e, "pairs", PAIRS) as j:
                if softly:
                    for t in range(NT):
                        ac_q.wait(e, f"q{t}")
                        dv_q.mark(e.tensor_scalar(qn[:, t], qf[:, t], 0.0, None, ALU.min), f"neg{t}")
                    for t in range(NT):
                        ac_q.wait(e, f"exp{t}")
                        dv_q.mark(e.scalar_tensor_tensor(qf[:, t], qf[:, t], 0.0, qn[:, t], ALU.max, ALU.add),
                                  f"map{t}")
                for t in range(NT):
                    ac_q.wait(e, f"hi{t}")
                    dv_q.mark(e.tensor_tensor(ql[:, tile(t)], qf[:, t], qh[:, tile(t)].bitcast(F32),
                                              ALU.subtract), f"lo{t}")
                w.make_lo(e, Q, f"w{Q}")
                bld.wait(e, "next", back=1)
                for s in range(TC + 2):
                    if s < TC:
                        r = rows_of(s)
                        pe_kv.wait(e, f"kv{s}")
                        f = kvf[0:r, s % 4]
                        i = e.tensor_tensor(f, bank[KVB + s % 3][0:r, 0:W2], bkv[0:r], ALU.add)
                        e.drain()
                        if softly:
                            i = e.tensor_scalar(neg[0:r, s % 4], f[:, 0:P], 0.0, None, ALU.min)
                            dv_kv.mark(i, f"kv{s}")
                        else:
                            dv_kv.mark(e.tensor_scalar(f[:, 0:P], f[:, 0:P], 0.0, None, ALU.max), f"kv{s}")
                    if 1 <= s <= TC:
                        c = s - 1
                        r = rows_of(c)
                        f = kvf[0:r, c % 4]
                        if softly:
                            ac_kv.wait(e, f"exp{c}")
                            dv_kv.mark(e.scalar_tensor_tensor(f[:, 0:P], f[:, 0:P], 0.0, neg[0:r, c % 4],
                                                              ALU.max, ALU.add), f"map{c}")
                        else:
                            dv_kv.alias(f"map{c}", f"kv{c}")
                    if s >= 2:
                        c = s - 2
                        r = rows_of(c)
                        ac_kv.wait(e, f"hi{c}")
                        dv_kv.mark(e.tensor_tensor(kvl[0:r, c, 0:W2], kvf[0:r, c % 4],
                                                   kvh[0:r, c, 0:W2].bitcast(F32), ALU.subtract), f"lo{c}")
                pe_m.wait(e, "m")
                if softly:
                    e.tensor_copy(ks[:], bank[6][:, W2:W2 + 1])
                    e.drain()
                    e.tensor_scalar(mf[:, P:W2], mask[:], ks[:, 0:1], None, ALU.mult)
                dv_m.mark(e.tensor_tensor(mf[:, 0:P], bank[6][:, P:W2], mask[:], ALU.mult), "m")
                ac_m.wait(e, "hi")
                dv_m.mark(e.tensor_tensor(ml[:, 0:MW], mf[:, 0:MW], mh[:, 0:MW].bitcast(F32), ALU.subtract), "lo")
                w.make_lo(e, K, f"w{K}")
                w.make_lo(e, V, f"w{V}")
                for t in range(NT):
                    pe_at.wait(e, f"at{t}")
                    o = at[:, bass.ds(j, 1), tile(t)].rearrange("p a b -> p (a b)")
                    if softly:
                        e.tensor_scalar(qn[:, t], bank[DEN[t]][:, 0:TW], 1e-6, None, ALU.add)
                        e.drain()
                        e.reciprocal(qn[:, t], qn[:, t])
                        e.drain()
                        i = e.tensor_tensor(o, bank[NUM[t]][:, 0:TW], qn[:, t], ALU.mult)
                    else:
                        i = e.tensor_copy(o, bank[NUM[t]][:, 0:TW])
                    dv_at.mark(i, f"at{t}")
                e.drain()


def graph_layer(nc, known, tag, x, cnt, dram):
    HOPS, HALF = 4, TC // 2
    HWID = (HALF * P, N - HALF * P)
    with Phase(nc, known, tag) as p:
        ld, pl = p.new("ld", 16), p.new("pool")
        x1s = p.new("x1", 16)
        pe_t, dv_t, ac_t = p.new("pt"), p.new("dt"), p.new("at")
        pe_s, dv_s, ac_s = p.new("ps"), p.new("ds"), p.new("as")
        pe_g, dv_g, dv_o, ac_g = p.new("pg"), p.new("dg"), p.new("do"), p.new("ag")
        dv_f, ac_f = p.new("df"), p.new("af")
        dv_a, ac_a, pe_a = p.new("da"), p.new("aa"), p.new("pa")
        x1 = p.sb("x1", [P, GC, TM])
        g = p.sb("g", [P, TC, NH])
        gf = p.sb("gf", [P, 4, NH])
        gh, gl = p.sb("gh", [P, TC, NH], F32R), p.sb("gl", [P, TC, NH], F32R)
        gw = p.sb("gw", [P, 2, NH])
        dump = p.sb("dump", [P, HALF, NH], BF16)
        gld = p.new("gld", 16)
        gb = p.sb("gb", [P, HOPS])
        ident, ones = p.sb("ident", [P, P]), p.sb("ones", [P, P])
        deg, rdeg, dis, z = (p.sb(n, [P, TC]) for n in ("deg", "rdeg", "dis", "z"))
        ga, gs, gsb = p.sb("ga", [P, TC]), p.sb("gs", [P, TC]), p.sb("gsb", [P, TC])
        diag = p.sb("diag", [P, TC, P])
        ab = p.sb("ab", [P, TM])
        th = p.sb("th", [P, 2, HALF * P])
        af = p.sb("af", [P, 4, HALF * P])
        ah, al = p.sb("ah", [P, 2, HALF * P], F32R), p.sb("al", [P, 2, HALF * P], F32R)
        bank = p.banks(8)
        block = p.block()
        BANKS = ((0, 1, 2, 3, 4), (5, 6, 7, 0, 1))
        AB, ABW = ((2, 3), (5, 6)), HALF * P // 2
        cols = lambda h: slice(h * HALF * P, h * HALF * P + HWID[h])

        @block.sync
        def _(e):
            x1s.mark(e.dma_start(x1[:], dram["x1"].rearrange("m p n -> p m n")), "x1")
            ld.mark(e.dma_start(gb[:], dram["gate_b"].broadcast_to([P, HOPS])), "gb")
            gwf = gw[:].rearrange("p b c -> p (b c)")
            gld.mark(e.dma_start(gwf, dram["gate_w"][0:1].broadcast_to([P, 2 * NH])), "first")
            with p.loops.run(e, "hops", HOPS) as k:
                dv_g.wait(e, "diag1")
                gld.mark(e.dma_start(gwf, dram["gate_w"][bass.ds((k + 1) % HOPS, 1)].broadcast_to([P, 2 * NH])),
                         "next")
            gld.wait(e, "next")

        @block.gpsimd
        def _(e):
            e.memset(ones[:], 1.0)
            e.memset(ga[:], 0.0)
            e.memset(gs[:], 0.0)
            e.memset(g[:, TC - 1], 0.0)
            e.memset(ab[:, N:TM], 0.0)
            pl.mark(e.memset(ident[:], 1.0), "one")
            pl.wait(e, "one")
            pl.mark(e.affine_select(out=ident[:], in_=ident[:], compare_op=ALU.is_equal, fill=0.0, base=0,
                                    pattern=[[1, P]], channel_multiplier=-1), "ident")
            x1s.wait(e, "x1")
            e.tensor_tensor(x[:, 0:GC], x[:, 0:GC], x1[:], ALU.add)

        GROUPS = [(m, c, min(c + 4, TC)) for m in range(GC) for c in (0, 4, 8)]
        width = lambda a, b: sum(rows_of(c) for c in range(a, b))

        @block.tensor
        def _(e):
            pe_a.start(e, 2)
            pl.wait(e, "ident")
            x1s.wait(e, "x1")
            for c in range(TC):
                r = rows_of(c)
                if c >= 4:
                    ac_t.wait(e, f"g{c - 4}")
                for m in range(GC):
                    i = e.transpose(bank[c % 4][0:r, m * P:(m + 1) * P], x1[:, m, c * P:c * P + r], ident[:])
                pe_t.mark(i, f"t{c}")
            dv_s.wait(e, "sum")
            for t in range(NT):
                m = e.matmul(bank[4 + t][:, 0:TW], ones[:], ab[:, tile(t)], start=True, stop=True)
            pe_s.mark(m, "row")
            dv_s.wait(e, "row")
            for c in range(TC):
                r = rows_of(c)
                m = e.matmul(bank[7][0:r, c:c + 1], ab[0:1, c * P:c * P + r], ones[0:1, 0:1], start=True, stop=True)
            pe_s.mark(m, "deg")

            def spread_row(h, name):
                dv_g.wait(e, f"diag{name}")
                for n, b in enumerate(AB[h]):
                    at = h * HALF * P + n * ABW
                    m = e.matmul(bank[b][:, 0:ABW], ones[:], diag[:].rearrange("p a b -> p (a b)")[:, at:at + ABW],
                                 start=True, stop=True)
                pe_g.mark(m, f"ab{name}")

            spread_row(0, "first")
            with p.loops.run(e, "hops", HOPS):
                for h in range(2):
                    for c in range(TC):
                        r = rows_of(c)
                        if c == 0:
                            dv_o.wait(e, f"shared{h}")
                            dv_o.wait(e, "rest1", back=1) if h == 0 else dv_o.wait(e, "rest0")
                            ac_g.wait(e, "ab0", back=1) if h == 0 else ac_g.wait(e, "ab1")
                        if c == TC - 3:
                            dv_o.wait(e, f"rest{h}")
                            spread_row(1 - h, str(1 - h))
                        dv_a.wait(e, f"al{h}{c}")
                        for d in range(HALF):
                            q = rows_of(h * HALF + d)
                            cut = slice(d * P, d * P + q)
                            o = bank[BANKS[h][d]][0:q, :]
                            e.matmul(o, al[0:r, c % 2, cut], gh[0:r, c], start=c == 0, stop=False)
                            e.matmul(o, ah[0:r, c % 2, cut], gl[0:r, c], start=False, stop=False)
                            m = e.matmul(o, ah[0:r, c % 2, cut], gh[0:r, c], start=False, stop=c == TC - 1)
                        pe_a.mark(m, f"a{h}{c}")
            dv_o.wait(e, "last")
            ac_g.wait(e, "ab0")
            for n, (m, a, b) in enumerate(GROUPS):
                if n >= 8:
                    dv_t.wait(e, f"x{n - 8}")
                for c in range(a, b):
                    r, at = rows_of(c), (c - a) * P
                    i = e.transpose(bank[n % 8][:, at:at + r], g[0:r, c, m * P:(m + 1) * P], ident[0:r, 0:r])
                pe_t.mark(i, f"b{n}")

        @block.scalar
        def _(e):
            pl.wait(e, "one")
            for c in range(TC):
                pe_t.wait(e, f"t{c}")
                r = rows_of(c)
                ac_t.mark(e.activation(g[0:r, c], bank[c % 4][0:r, :], ACT.Copy), f"g{c}")
            dv_s.wait(e, "rdeg")
            ac_s.mark(e.activation(dis[:], rdeg[:], ACT.Sqrt), "root")

            def copy_row(h, name):
                pe_g.wait(e, f"ab{name}")
                for n, b in enumerate(AB[h]):
                    at = h * HALF * P + n * ABW
                    w = min(ABW, TM - at)
                    i = e.activation(ab[:, at:at + w], bank[b][:, 0:w], ACT.Copy)
                ac_g.mark(i, f"ab{name}")
                e.drain()

            copy_row(0, "first")
            with p.loops.run(e, "hops", HOPS):
                for h in range(2):
                    for s in range(TC + 1):
                        if s < TC:
                            r, b = rows_of(s), s % 2
                            if s >= 2:
                                dv_a.wait(e, f"af{h}{s - 2}")
                            if h == 0 and s == 0:
                                dv_g.wait(e, "gs0", back=1)
                            if h == 0 and s == HALF:
                                dv_g.wait(e, "gs1")
                            ac_a.mark(e.activation(th[0:r, b, 0:HWID[h]], ab[0:r, cols(h)], ACT.Tanh,
                                                   bias=gsb[0:r, s:s + 1]), f"th{h}{s}")
                            if h == 0:
                                dv_f.wait(e, f"gf{s}")
                                ac_f.mark(e.activation(gh[0:r, s], gf[0:r, s % 4], ACT.Copy), f"gh{s}")
                            if s == TC - 1:
                                copy_row(1 - h, str(1 - h))
                        if s >= 1:
                            c = s - 1
                            r, b = rows_of(c), c % 2
                            dv_a.wait(e, f"af{h}{c}")
                            if c >= 2:
                                pe_a.wait(e, f"a{h}{c - 2}")
                            elif h == 1:
                                pe_a.wait(e, f"a0{TC - 2 + c}")
                            else:
                                pe_a.wait(e, f"a1{TC - 2 + c}", back=1)
                            ac_a.mark(e.activation(ah[0:r, b, 0:HWID[h]], af[0:r, (c + 2 * h) % 4, 0:HWID[h]], ACT.Copy),
                                      f"ah{h}{c}")
        @block.vector
        def _(e):
            dv_o.start(e, 1)
            pl.wait(e, "ident")
            dv_s.mark(e.tensor_reduce(ab[:, 0:N], cnt[:, :, 0:N].rearrange("p c n -> p n c"), AX.X, ALU.add), "sum")
            ac_t.wait(e, f"g{TC - 1}")
            ld.wait(e, "gb")
            e.drain()

            def dots(out, w, first, last):
                for c in range(first, last):
                    r = rows_of(c)
                    e.tensor_tensor_reduce(dump[0:r, c % HALF], g[0:r, c], gw[0:r, w],
                                           1.0, 0.0, ALU.mult, ALU.add, out[0:r, c:c + 1])

            def spread(first, last):
                n = last - first
                return e.tensor_tensor(diag[:, first:last], ident[:].unsqueeze(1).broadcast_to([P, n, P]),
                                       ga[:, first:last].unsqueeze(2).broadcast_to([P, n, P]), ALU.mult)

            def bias(h, k, step):
                cut = slice(h * HALF, (h + 1) * HALF)
                dv_g.mark(e.tensor_scalar(gsb[:, cut], gs[:, cut], gb[:, k], None, ALU.add), step)

            def update(h, ds):
                for d in ds:
                    c = h * HALF + d
                    q = rows_of(c)
                    i = e.scalar_tensor_tensor(g[0:q, c], bank[BANKS[h][d]][0:q, :], dis[0:q, c:c + 1],
                                               g[0:q, c], ALU.mult, ALU.add)
                return i

            shared = [[d for d in range(HALF) if BANKS[h][d] in BANKS[1 - h]] for h in range(2)]
            rest = [[d for d in range(HALF) if d not in shared[h]] for h in range(2)]

            def aside(s, h, o, k):
                first = o * HALF
                if s == 1:
                    dv_o.mark(update(o, rest[o]), f"rest{h}")
                    e.drain()
                    dots(gs, 1, first, first + 2)
                elif s == 2:
                    dots(gs, 1, first + 2, first + HALF)
                    e.drain()
                    if o == 1:
                        bias(o, k, "gs1")
                elif 4 <= s <= 6:
                    dots(ga, 0, first + 2 * (s - 4), min(first + 2 * (s - 3), first + HALF))
                    if o == 0 and s == 6:
                        bias(o, k, "gs0")
                elif s == 7:
                    e.drain()
                    dv_g.mark(spread(first, first + HALF), f"diag{o}")

            gld.wait(e, "first")
            dots(gs, 1, 0, HALF)
            e.drain()
            bias(0, slice(0, 1), "gsfirst")
            dots(ga, 0, 0, HALF)
            e.drain()
            dv_g.mark(spread(0, HALF), "diagfirst")
            pe_s.wait(e, "row")
            for t in range(NT):
                i = e.tensor_copy(ab[0:1, tile(t)], bank[4 + t][0:1, 0:TW])
            dv_s.mark(i, "row")
            e.memset(deg[:], 1.0)
            pe_s.wait(e, "deg")
            e.drain()
            e.tensor_scalar(deg[:, 0:TC - 1], bank[7][:, 0:TC - 1], 1.0, None, ALU.max)
            e.tensor_scalar(deg[0:LAST, TC - 1:TC], bank[7][0:LAST, TC - 1:TC], 1.0, None, ALU.max)
            e.drain()
            dv_s.mark(e.reciprocal(rdeg[:], deg[:]), "rdeg")
            ac_s.wait(e, "root")
            e.tensor_tensor(z[:], dis[:], dis[:], ALU.mult)
            e.drain()
            e.tensor_tensor(z[:], z[:], deg[:], ALU.mult)
            e.drain()
            e.tensor_scalar(z[:], z[:], -0.5, 1.5, ALU.mult, ALU.add)
            e.drain()
            e.tensor_tensor(dis[:], dis[:], z[:], ALU.mult)
            for b in BANKS[1]:
                e.memset(bank[b][:], 0.0)
            e.drain()

            with p.loops.run(e, "hops", HOPS) as k:
                for h in range(2):
                    for s in range(TC + 1):
                        if s < TC:
                            r, b = rows_of(s), s % 2
                            if h == 0:
                                dv_f.mark(e.tensor_scalar(gf[0:r, s % 4], g[0:r, s], dis[0:r, s:s + 1], None,
                                                          ALU.mult), f"gf{s}")
                            ac_a.wait(e, f"th{h}{s}")
                            dv_a.mark(e.tensor_tensor(af[0:r, (s + 2 * h) % 4, 0:HWID[h]], th[0:r, b, 0:HWID[h]],
                                                      cnt[0:r, s, cols(h)], ALU.mult), f"af{h}{s}")
                        if s >= 1:
                            c = s - 1
                            r, b = rows_of(c), c % 2
                            if h == 0:
                                ac_f.wait(e, f"gh{c}")
                                e.tensor_tensor(gl[0:r, c], gf[0:r, c % 4], gh[0:r, c].bitcast(F32), ALU.subtract)
                            ac_a.wait(e, f"ah{h}{c}")
                            dv_a.mark(e.tensor_tensor(al[0:r, b, 0:HWID[h]], af[0:r, (c + 2 * h) % 4, 0:HWID[h]],
                                                      ah[0:r, b, 0:HWID[h]].bitcast(F32), ALU.subtract),
                                      f"al{h}{c}")
                        if s == 1:
                            pe_a.wait(e, f"a1{TC - 1}", back=1) if h == 0 else pe_a.wait(e, f"a0{TC - 1}")
                            dv_o.mark(update(1 - h, shared[1 - h]), f"shared{h}")
                            if h == 1:
                                gld.wait(e, "next")
                        aside(s, h, 1 - h, bass.ds(k, 1) if h == 0 else bass.ds((k + 1) % HOPS, 1))
            pe_a.wait(e, f"a1{TC - 1}")
            dv_o.mark(update(1, range(HALF)), "last")
            for n, (m, a, b) in enumerate(GROUPS):
                pe_t.wait(e, f"b{n}")
                w = width(a, b)
                o = x[:, GC + m, a * P:a * P + w]
                dv_t.mark(e.tensor_tensor(o, o, bank[n % 8][:, 0:w], ALU.add), f"x{n}")


def router(nc, known, tag, xh, xl, gate_dram, tw):
    EX = 8
    with Phase(nc, known, tag) as p:
        ld, pl, dv, pe, ac = p.new("ld", 16), p.new("pool"), p.new("dve"), p.new("pe"), p.new("act")
        gr = p.sb("gr", [P, KC, EX])
        gh, gl = p.sb("gh", [P, KC, EX], F32R), p.sb("gl", [P, KC, EX], F32R)
        lg, top = p.sb("lg", [P, TC, EX]), p.sb("top", [P, TC, EX])
        at = p.sb("at", [P, TC, EX], U32)
        af = p.sb("af", [P, TC, EX])
        io = p.sb("io", [P, EX])
        df, ex, w1, w2 = (p.sb(n, [P, TC]) for n in ("df", "ex", "w1", "w2"))
        hot = p.sb("hot", [P, TC, EX])
        row = p.sb("row", [EX, TM])
        ident = p.sb("ident", [EX, EX])
        bank = p.banks(4)
        block = p.block()

        @block.sync
        def _(e):
            ld.mark(e.dma_start(gr[:].rearrange("p a b -> p (a b)"), gate_dram), "gate")

        @block.gpsimd
        def _(e):
            e.memset(lg[:], 0.0)
            pl.mark(e.memset(ident[:], 1.0), "one")
            pl.wait(e, "one")
            e.affine_select(out=ident[:], in_=ident[:], compare_op=ALU.is_equal, fill=0.0, base=0,
                            pattern=[[1, EX]], channel_multiplier=-1)
            pl.mark(e.iota(io[:], [[1, EX]], base=0, channel_multiplier=0, allow_small_or_imprecise_dtypes=True),
                    "iota")

        @block.scalar
        def _(e):
            dv.wait(e, "df")
            ac.mark(e.activation(ex[:], df[:], ACT.Exp), "exp")

        @block.tensor
        def _(e):
            w = lambda g: [g[:, k] for k in range(KC)]
            dv.wait(e, "gate")
            for t in range(NT):
                m = product(e, bank[t][0:EX, 0:TW], (w(gh), w(gl)), parts(xh, xl, t))
                pe.mark(m, f"row{t}")
            pl.wait(e, "iota")
            for c in range(TC):
                if c in (0, 3, 6):
                    dv.wait(e, f"row{c // 3}")
                r = rows_of(c)
                m = e.transpose(bank[3][0:r, c * EX:(c + 1) * EX], row[:, c * P:c * P + r], ident[:])
            pe.mark(m, "logits")

        @block.vector
        def _(e):
            ld.wait(e, "gate")
            e.tensor_copy(gh[:], gr[:])
            e.drain()
            dv.mark(e.tensor_tensor(gl[:], gr[:], gh[:].bitcast(F32), ALU.subtract), "gate")
            pl.wait(e, "iota")
            for t in range(NT):
                pe.wait(e, f"row{t}")
                dv.mark(e.tensor_copy(row[:, tile(t)], bank[t][0:EX, 0:TW]), f"row{t}")
            pe.wait(e, "logits")
            b = bank[3][:, 0:TC * EX].rearrange("p (c x) -> p c x", x=EX)
            e.tensor_copy(lg[:, 0:TC - 1], b[:, 0:TC - 1])
            e.tensor_copy(lg[0:LAST, TC - 1], b[0:LAST, TC - 1])
            e.drain()
            for c in range(TC):
                e.max(top[:, c], lg[:, c])
            e.drain()
            for c in range(TC):
                e.max_index(at[:, c], top[:, c], lg[:, c])
            dv.mark(e.tensor_tensor(df[:], top[:, :, 1], top[:, :, 0], ALU.subtract), "df")
            e.drain()
            e.tensor_copy(af[:], at[:])
            ac.wait(e, "exp")
            e.tensor_scalar(w2[:], ex[:], 1.0, None, ALU.add)
            e.drain()
            e.reciprocal(w1[:], w2[:])
            e.drain()
            e.tensor_tensor(w2[:], w1[:], ex[:], ALU.mult)
            wide = lambda t: t.unsqueeze(2).broadcast_to([P, TC, EX])
            iow = io[:].unsqueeze(1).broadcast_to([P, TC, EX])
            e.tensor_tensor(hot[:], wide(af[:, :, 0]), iow, ALU.is_equal)
            e.drain()
            e.tensor_tensor(tw[:], hot[:], wide(w1[:]), ALU.mult)
            e.drain()
            e.tensor_tensor(hot[:], wide(af[:, :, 1]), iow, ALU.is_equal)
            e.drain()
            e.tensor_tensor(hot[:], hot[:], wide(w2[:]), ALU.mult)
            e.drain()
            e.tensor_tensor(tw[:], tw[:], hot[:], ALU.add)


def gated_mlp(nc, known, tag, x, xh, xl, w_dram, hc, experts=None, dtype=F32, scale=None, store=None):
    count, tw = experts or (1, None)
    with Phase(nc, known, tag) as p:
        w = Weights(nc, p.ctx, tag + "_w", 2, D, lambda n, each=1: p.new(n, each), dtype, scale)
        pl, pe, pe_wb, dv, dv_d, ac, ac_wb = (p.new(n) for n in ("pool", "pe", "pwb", "dve", "dd", "act", "awb"))
        sts = [[p.new(f"st{b}{r}", 16) for r in range(2)] for b in range(2)]
        hh, hl = p.sb("hh", [P, hc, TM], F32R), p.sb("hl", [P, hc, TM], F32R)
        sg, hf = p.sb("sg", [P, NT, TW]), p.sb("hf", [P, NT, TW])
        if tw is not None:
            wb = p.sb("wb", [P, TM])
            ident, ones = p.sb("ident", [P, P]), p.sb("ones", [P, P])
            diag = p.sb("diag", [P, TC, P])
        bank = p.banks(8)
        block = p.block()
        downs = KC // 4
        per = 2 * hc + 2 * downs
        total = count * per
        flat = lambda ap: ap.rearrange("p a b -> p (a b)")

        @block.sync
        def _(e):
            w.load(e, 0, w_dram[0], "first")
            with p.loops.run(e, "experts", count) as x_:
                for kind, at, turns in (("u", 0, hc), ("d", 2 * hc, downs)):
                    with p.loops.run(e, kind, turns) as i:
                        w.los.wait(e, kind + "1", back=1)
                        w.load(e, 1, w_dram[x_ * per + i * 2 + (at + 1)], kind + "1")
                        w.los.wait(e, kind + "0", back=1)
                        w.load(e, 0, w_dram[(x_ * per + i * 2 + (at + 2)) % total], kind + "0")

        @block.gpsimd
        def _(e):
            if store is not None:
                with p.loops.run(e, "experts", count), p.loops.run(e, "d", downs) as i:
                    for b in range(2):
                        for r in range(2):
                            dv.wait(e, f"x{b}{r}{NT - 1}")
                            c = i * 4 + (2 * b + r)
                            sts[b][r].mark(e.dma_start(store[c], flat(x[:, bass.ds(c, 1), 0:N])), f"y{b}{r}")
                for b in range(2):
                    for r in range(2):
                        sts[b][r].wait(e, f"y{b}{r}")
            if tw is not None:
                e.memset(ones[:], 1.0)
                pl.mark(e.memset(ident[:], 1.0), "one")
                pl.wait(e, "one")
                pl.mark(e.affine_select(out=ident[:], in_=ident[:], compare_op=ALU.is_equal, fill=0.0, base=0,
                                        pattern=[[1, P]], channel_multiplier=-1), "ident")

        @block.tensor
        def _(e):
            def spread(name):
                dv_d.wait(e, "diag" + name)
                for t in range(NT):
                    if t == 2:
                        ac_wb.wait(e, f"wb0{name}")
                    pe_wb.mark(e.matmul(bank[6 + t % 2][:, 0:TW], ones[:], flat(diag[:])[:, tile(t)],
                                        start=True, stop=True), f"wb{t}{name}")

            pe.start(e, 1)
            if tw is not None:
                spread("first")
            with p.loops.run(e, "experts", count):
                with p.loops.run(e, "u", hc):
                    w.los.wait(e, "u0", back=1)
                    for t in range(NT):
                        ac.wait(e, f"sg{t}", back=1)
                        dv.wait(e, f"x10{t}", back={"experts": 1})
                        m = product(e, bank[t][:, 0:TW], w.blocks(0, 0, KC), parts(xh, xl, t))
                        pe.mark(m, f"g{t}")
                    w.los.wait(e, "u1")
                    for t in range(NT):
                        dv.wait(e, f"h{t}", back=1)
                        dv.wait(e, f"x11{t}", back={"experts": 1})
                        m = product(e, bank[3 + t][:, 0:TW], w.blocks(1, 0, KC), parts(xh, xl, t))
                        pe.mark(m, f"u{t}")
                with p.loops.run(e, "d", downs):
                    for b in range(2):
                        w.los.wait(e, f"d{b}", back=1 - b)
                        for r in range(2):
                            for t in range(NT):
                                if b == 0 and r == 0:
                                    dv.wait(e, f"lo{t}")
                                dv.wait(e, f"x{1 - b}{r}{t}", back=1 - b)
                                m = product(e, bank[3 * r + t][:, 0:TW], w.blocks(b, r * hc, hc),
                                            parts(hh, hl, t, hc))
                                pe.mark(m, f"d{b}{r}{t}")
                if tw is not None:
                    spread("")

        @block.scalar
        def _(e):
            def spread(name):
                for t in range(NT):
                    pe_wb.wait(e, f"wb{t}{name}")
                    ac_wb.mark(e.activation(wb[:, tile(t)], bank[6 + t % 2][:, 0:TW], ACT.Copy), f"wb{t}{name}")

            ac.start(e, 6)
            w.make_hi(e, 0, "first")
            if tw is not None:
                spread("first")
            with p.loops.run(e, "experts", count):
                with p.loops.run(e, "u", hc) as i:
                    pe.wait(e, "u2", back=1)
                    w.make_hi(e, 1, "u1")
                    for t in range(NT):
                        pe.wait(e, f"g{t}")
                        dv.wait(e, f"h{t}", back=1)
                        ac.mark(e.activation(sg[:, t], bank[t][:, 0:TW], ACT.Silu), f"sg{t}")
                    w.make_hi(e, 0, "u0")
                    for t in range(NT):
                        dv.wait(e, f"h{t}")
                        ac.mark(e.activation(flat(hh[:, bass.ds(i, 1), tile(t)]), hf[:, t], ACT.Copy), f"hh{t}")
                with p.loops.run(e, "d", downs):
                    pe.wait(e, "d112", back=1)
                    w.make_hi(e, 1, "d1")
                    pe.wait(e, "d012")
                    w.make_hi(e, 0, "d0")
                if tw is not None:
                    spread("")

        @block.vector
        def _(e):
            def spread(expert, name):
                col = tw[:, :, expert].broadcast_to([P, TC, P])
                dv_d.mark(e.tensor_tensor(diag[:], ident[:].unsqueeze(1).broadcast_to([P, TC, P]), col,
                                          ALU.mult), "diag" + name)

            dv.start(e, 12)
            w.los.start(e, 1)
            if tw is not None:
                pl.wait(e, "ident")
                spread(slice(0, 1), "first")
            w.make_lo(e, 0, "first")
            with p.loops.run(e, "experts", count) as x_:
                if tw is not None:
                    ac_wb.wait(e, "wb2", back=1)
                with p.loops.run(e, "u", hc) as i:
                    w.make_lo(e, 1, "u1")
                    if tw is not None:
                        for t in range(NT):
                            ac.wait(e, f"sg{t}")
                            e.tensor_tensor(sg[:, t], sg[:, t], wb[:, tile(t)], ALU.mult)
                    w.make_lo(e, 0, "u0")
                    e.drain()
                    for t in range(NT + 1):
                        if t < NT:
                            pe.wait(e, f"u{t}")
                            ac.wait(e, f"sg{t}")
                            dv.mark(e.tensor_tensor(hf[:, t], sg[:, t], bank[3 + t][:, 0:TW], ALU.mult), f"h{t}")
                        if t:
                            ac.wait(e, f"hh{t - 1}")
                            dv.mark(e.tensor_tensor(flat(hl[:, bass.ds(i, 1), tile(t - 1)]), hf[:, t - 1],
                                                    flat(hh[:, bass.ds(i, 1), tile(t - 1)]).bitcast(F32),
                                                    ALU.subtract), f"lo{t - 1}")
                if tw is not None:
                    spread(bass.ds((x_ + 1) % count, 1), "")
                with p.loops.run(e, "d", downs) as i:
                    for b in range(2):
                        w.make_lo(e, 1 - b, f"d{1 - b}")
                        for r in range(2):
                            for t in range(NT):
                                pe.wait(e, f"d{b}{r}{t}")
                                o = flat(x[:, bass.ds(i * 4 + (2 * b + r), 1), tile(t)])
                                dv.mark(e.tensor_tensor(o, o, bank[3 * r + t][:, 0:TW], ALU.add), f"x{b}{r}{t}")


def build(nc, io, known):
    dram = lambda n, shape, d=F32: nc.dram_tensor("scratch_" + n, shape, d).ap()
    slots = dram("slots", (P, NCH * 4))
    graph = dict(src=io["src"], dst=io["dst"], edge_weight=io["edge_weight"], slots=slots,
                 slot_rows=slots.rearrange("p (c f) -> (p c) f", f=4), offs=dram("offs", (P, 4), I32),
                 wmat=dram("wmat", (TC, P, D)))
    x1 = dram("x1", (GC, P, TM))
    xs = dram("xs", (KC, P, N))
    with ExitStack() as ctx:
        x = ctx.enter_context(nc.sbuf_tensor("x", [P, KC, TM], F32))
        idx, pay = (nc.sbuf_tensor("idx", [EP, EK], I32), nc.sbuf_tensor("pay", [EP, EK, 4], F32))
        idx, pay = ctx.enter_context(idx), ctx.enter_context(pay)
        spill = ctx.enter_context(nc.sbuf_tensor("spill", [P, 1], I32))
        part = lambda first, last: lambda e, p: scatter(e, p, graph, idx, pay, first, last)

        @contextmanager
        def normed(layer):
            with (nc.sbuf_tensor(f"xh{layer}", [P, KC, TM], F32R) as xh,
                  nc.sbuf_tensor(f"xl{layer}", [P, KC, TM], F32R) as xl):
                yield xh, xl

        graph_sort(nc, known, graph, x, io["x"], idx, pay, spill)
        with normed(0) as (xh, xl):
            layer_norm(nc, known, "n0", x, xh, xl)
            dense(nc, known, "w1", xh, xl, io["w1"], GC, io["b1"], store=x1,
                  beside=part(0, EK // 3))
            attention(nc, known, "m0", xh, xl, x, io["qkv0"], io["bq0"], io["bkv0"], True, part(EK // 3, EK))
            dense(nc, known, "o0", xh, xl, io["wo0"], KC, io["bo0"], out=x, base=io["x"])
        with nc.sbuf_tensor("counts", [P, TC, TC * P], U16) as cnt:
            graph_home(nc, known, graph, cnt)
            graph_overflow(nc, known, graph, cnt, spill)
            graph_layer(nc, known, "gl", x, cnt, dict(x1=x1, gate_w=io["gate_w"], gate_b=io["gate_b"]))
        with normed(1) as (xh, xl):
            layer_norm(nc, known, "n1", x, xh, xl)
            with nc.sbuf_tensor("tw", [P, TC, 8], F32) as tw:
                router(nc, known, "ro", xh, xl, io["gate"], tw)
                gated_mlp(nc, known, "ex", x, xh, xl, io["experts"], 4, experts=(8, tw))
            layer_norm(nc, known, "n2", x, xh, xl)
            dense(nc, known, "gw", xh, xl, graph["wmat"], KC, io["gnn_bias"], out=x, spill=xs)
            attention(nc, known, "m1", xh, xl, x, io["qkv1"], io["bq1"], io["bkv1"], False)
            dense(nc, known, "o1", xh, xl, io["wo1"], KC, io["bo1"], out=x, base=xs)
            layer_norm(nc, known, "n3", x, xh, xl)
            gated_mlp(nc, known, "ff", x, xh, xl, io["ffn"], 3, dtype=I32, scale=1.0 / 127.0,
                      store=io["out"])


def kernel(**a):
    import numpy as _np
    import concourse.bacc as _bacc
    from concourse.bass_utils import run_bass_kernel_spmd as _run

    a = {k: _np.asarray(v) for k, v in a.items()}

    def units(w):
        i, o = w.shape
        return w.reshape(i // P, P, o // P, P).transpose(2, 1, 0, 3).reshape(o // P, P, i)

    def downs(w):
        u = units(w)
        u = u.reshape(u.shape[0] // 2, 2, P, u.shape[2]).transpose(0, 2, 1, 3).reshape(u.shape[0] // 2, P, -1)
        return _np.concatenate([u, _np.zeros(u.shape[:2] + (D - u.shape[2],), u.dtype)], 2)

    def qkv(q, k, v):
        return _np.stack([units(k.T), units(v.T), units(q.T)], 1).reshape(3 * KC, P, D)

    def mlp(w1, w3, w2):
        up = _np.stack([units(w1), units(w3)], 1)
        return _np.concatenate([up.reshape(-1, P, D), downs(w2)], 0)

    col = lambda b: b.reshape(-1, P).T
    pair = lambda k, v: _np.stack([k.reshape(KC, P), v.reshape(KC, P)], 1).reshape(KC, 2 * P)
    g = lambda n: a[n]
    ins = dict(
        x=g("x").T.reshape(KC, P, N),
        src=g("src").reshape(EP, EK), dst=g("dst").reshape(EP, EK), edge_weight=g("edge_weight").reshape(EP, EK),
        w1=units(g("L0_gnn_W1")), b1=col(g("L0_gnn_b1")),
        gate_w=g("L0_gnn_gate_w").reshape(4, 2 * NH), gate_b=g("L0_gnn_gate_b").reshape(1, -1),
        qkv0=qkv(g("L0_mix_Wq"), g("L0_mix_Wk"), g("L0_mix_Wv")), bq0=col(g("L0_mix_bq")),
        bkv0=pair(g("L0_mix_bk"), g("L0_mix_bv")), wo0=units(g("L0_mix_Wo").T), bo0=col(g("L0_mix_bo")),
        gate=g("L0_ffn_gate").reshape(KC, P, 8).transpose(1, 0, 2).reshape(P, -1),
        experts=_np.concatenate([mlp(*w) for w in zip(g("L0_ffn_experts_w1"), g("L0_ffn_experts_w3"),
                                                      g("L0_ffn_experts_w2"))], 0),
        gnn_bias=col(g("L1_gnn_bias")),
        qkv1=qkv(g("L1_mix_q_w"), g("L1_mix_k_w"), g("L1_mix_v_w")), bq1=col(g("L1_mix_q_b")),
        bkv1=pair(g("L1_mix_k_b"), g("L1_mix_v_b")), wo1=units(g("L1_mix_o_w").T), bo1=col(g("L1_mix_o_b")),
        ffn=mlp(g("L1_ffn_w_gate").T, g("L1_ffn_w_up").T, g("L1_ffn_w_down").T),
    )
    ins = {n: _np.ascontiguousarray(v) for n, v in ins.items()}
    known = {}
    for _ in range(2):
        nc = _bacc.Bacc("TRN2", target_bir_lowering=False, num_devices=1)
        io = {n: nc.dram_tensor("in_" + n, v.shape, mybir.dt.from_np(v.dtype), kind="ExternalInput").ap()
              for n, v in ins.items()}
        io["out"] = nc.dram_tensor("out_y", (KC, P, N), F32, kind="ExternalOutput").ap()
        build(nc, io, known)
    r = _run(nc, [{"in_" + n: v for n, v in ins.items()}], core_ids=[0])
    y = r.results[0]["out_y"]
    return _np.ascontiguousarray(y.reshape(D, N).T)
```
